# Optimizing a Trainium2 kernel written in Bass

```python
import numpy as np
import jax
import jax.numpy as jnp

def _softmax(x, axis=-1):
    return jax.nn.softmax(x, axis=axis)

def _gelu(x):
    return jax.nn.gelu(x, approximate=True)

def _silu(x):
    return jax.nn.silu(x)

def _sigmoid(x):
    return jax.nn.sigmoid(x)

def _layernorm(x, axis=-1, eps=1e-05):
    m = jnp.mean(x, axis=axis, keepdims=True)
    v = jnp.var(x, axis=axis, keepdims=True)
    return (x - m) / jnp.sqrt(v + eps)

def _scatter_add(tgt, idx, src, axis=0):
    return tgt.at[idx].add(src)

def _segment_sum(src, seg, n):
    return jax.ops.segment_sum(src, seg, n)
kernel_name = 'mk_adaln_ffn_d1_seqx_r4_d0c53b'

def setup_inputs(seed: int=0):
    np.random.seed(seed)
    _w = jnp.asarray

    def _rec_inputs():
        import jax
        import jax.numpy as jnp
        _rk = jax.random.key(seed)
        x = -0.0003929 + 0.9999 * jax.random.normal(jax.random.fold_in(_rk, 1), (4, 512, 512), jnp.float32)
        _lenS = 512 - jax.random.randint(jax.random.fold_in(_rk, 7), (4,), 0, max(1, 512 // 4) + 1, jnp.int32)
        _lenS2 = 512 - jax.random.randint(jax.random.fold_in(_rk, 8), (4,), 0, max(1, 512 // 4) + 1, jnp.int32)
        cond_2048 = 0.00782532 + 1.00527 * jax.random.normal(jax.random.fold_in(_rk, 11), (4, 512), jnp.float32)
        return (x, cond_2048)
    x, cond_2048 = _rec_inputs()

    def _L0_cond_setup():
        import jax, jax.numpy as jnp
        import numpy as np
        HEADS = 16
        EPS = 1e-06

        def _rms_norm(x, g):
            xf = x.astype(jnp.float32)
            y = xf * jax.lax.rsqrt(jnp.mean(xf * xf, axis=-1, keepdims=True) + EPS)
            return y.astype(x.dtype) * g
        key = jax.random.key(seed)
        ks = jax.random.split(key, 6)
        b, n, dim, emb_dim = (4, 512, 512, 512)
        d_head = dim // HEADS
        return {'x': jax.random.normal(ks[0], (b, n, dim), jnp.float32), 'emb': jax.random.normal(ks[1], (b, 1, emb_dim), jnp.float32), 'W_emb': jax.random.normal(ks[2], (emb_dim, 2 * dim), jnp.float32) * emb_dim ** (-0.5), 'b_emb': jnp.zeros((2 * dim,), jnp.float32), 'g_norm': jnp.ones((dim,), jnp.float32), 'W_qkv': jax.random.normal(ks[3], (dim, 3 * dim), jnp.float32) * dim ** (-0.5), 'g_q': jnp.ones((d_head,), jnp.float32), 'g_k': jnp.ones((d_head,), jnp.float32), 'W_out': jax.random.normal(ks[4], (dim, dim), jnp.float32) * dim ** (-0.5)}
    _L0_cond_all = _L0_cond_setup()
    _L0_cond_in = {k: v for k, v in _L0_cond_all.items() if k in ('W_emb', 'b_emb', 'g_norm', 'W_qkv', 'g_q', 'g_k', 'W_out')}
    del _L0_cond_all

    def _L0_ffn_setup():
        import jax, jax.numpy as jnp
        import numpy as np
        TOP_K = 2
        key = jax.random.key(seed)
        ks = jax.random.split(key, 8)
        B, S, H, I, E = (1, 256, 512, 352, 8)
        s = 0.02
        return {'hidden_states': jax.random.normal(ks[0], (B, S, H), jnp.float32), 'gate_weight': jax.random.normal(ks[1], (E, H), jnp.float32) * s, 'expert_gate_w': jax.random.normal(ks[2], (E, I, H), jnp.float32) * s, 'expert_up_w': jax.random.normal(ks[3], (E, I, H), jnp.float32) * s, 'expert_down_w': jax.random.normal(ks[4], (E, H, I), jnp.float32) * s, 'shared_gate_w': jax.random.normal(ks[5], (I, H), jnp.float32) * s, 'shared_up_w': jax.random.normal(ks[6], (I, H), jnp.float32) * s, 'shared_down_w': jax.random.normal(ks[7], (H, I), jnp.float32) * s}
    _L0_ffn_all = _L0_ffn_setup()
    _L0_ffn_in = {k: v for k, v in _L0_ffn_all.items() if k in ('gate_weight', 'expert_gate_w', 'expert_up_w', 'expert_down_w', 'shared_gate_w', 'shared_up_w', 'shared_down_w')}
    del _L0_ffn_all
    return {'x': x, 'cond_2048': cond_2048, 'L0_cond_W_emb': _L0_cond_in['W_emb'], 'L0_cond_b_emb': _L0_cond_in['b_emb'], 'L0_cond_g_norm': _L0_cond_in['g_norm'], 'L0_cond_W_qkv': _L0_cond_in['W_qkv'], 'L0_cond_g_q': _L0_cond_in['g_q'], 'L0_cond_g_k': _L0_cond_in['g_k'], 'L0_cond_W_out': _L0_cond_in['W_out'], 'L0_ffn_gate_weight': _L0_ffn_in['gate_weight'], 'L0_ffn_expert_gate_w': _L0_ffn_in['expert_gate_w'], 'L0_ffn_expert_up_w': _L0_ffn_in['expert_up_w'], 'L0_ffn_expert_down_w': _L0_ffn_in['expert_down_w'], 'L0_ffn_shared_gate_w': _L0_ffn_in['shared_gate_w'], 'L0_ffn_shared_up_w': _L0_ffn_in['shared_up_w'], 'L0_ffn_shared_down_w': _L0_ffn_in['shared_down_w']}

def reference(x, cond_2048, L0_cond_W_emb, L0_cond_b_emb, L0_cond_g_norm, L0_cond_W_qkv, L0_cond_g_q, L0_cond_g_k, L0_cond_W_out, L0_ffn_gate_weight, L0_ffn_expert_gate_w, L0_ffn_expert_up_w, L0_ffn_expert_down_w, L0_ffn_shared_gate_w, L0_ffn_shared_up_w, L0_ffn_shared_down_w):
    import jax
    import jax.numpy as jnp

    def _L0_cond_ref(x, emb, W_emb, b_emb, g_norm, W_qkv, g_q, g_k, W_out):
        import jax, jax.numpy as jnp
        import numpy as np
        HEADS = 16
        EPS = 1e-06

        def _rms_norm(x, g):
            xf = x.astype(jnp.float32)
            y = xf * jax.lax.rsqrt(jnp.mean(xf * xf, axis=-1, keepdims=True) + EPS)
            return y.astype(x.dtype) * g
        b, n, dim = x.shape
        h = HEADS
        d = dim // h
        scale_shift = emb @ W_emb + b_emb
        scale, shift = jnp.split(scale_shift, 2, axis=-1)
        xn = _rms_norm(x, g_norm) * (1.0 + scale) + shift
        qkv = xn @ W_qkv
        qkv = qkv.reshape(b, n, 3, h, d)
        q, k, v = jnp.moveaxis(qkv, 2, 0)
        q = jnp.swapaxes(q, 1, 2)
        k = jnp.swapaxes(k, 1, 2)
        v = jnp.swapaxes(v, 1, 2)
        q = _rms_norm(q, g_q)
        k = _rms_norm(k, g_k)
        logits = jnp.einsum('bhqd,bhkd->bhqk', q, k) * d ** (-0.5)
        attn = jax.nn.softmax(logits, axis=-1)
        o = jnp.einsum('bhqk,bhkd->bhqd', attn, v)
        o = jnp.swapaxes(o, 1, 2).reshape(b, n, dim)
        return o + o @ W_out

    def _L0_ffn_ref(hidden_states, gate_weight, expert_gate_w, expert_up_w, expert_down_w, shared_gate_w, shared_up_w, shared_down_w):
        import jax, jax.numpy as jnp
        import numpy as np
        TOP_K = 2
        B, S, H = hidden_states.shape
        E = gate_weight.shape[0]
        x = hidden_states.reshape(-1, H)
        T = x.shape[0]
        logits = x @ gate_weight.T
        topk_logits, topk_idx = jax.lax.top_k(logits, TOP_K)
        topk_w = jax.nn.softmax(topk_logits, axis=-1)
        comb = jnp.zeros((T, E), x.dtype).at[jnp.arange(T)[:, None], topk_idx].add(topk_w)
        g = jnp.einsum('th,eih->tei', x, expert_gate_w)
        u = jnp.einsum('th,eih->tei', x, expert_up_w)
        h = jax.nn.silu(g) * u
        y = jnp.einsum('tei,ehi->teh', h, expert_down_w)
        out = jnp.einsum('teh,te->th', y, comb)
        sh = jax.nn.silu(x @ shared_gate_w.T) * (x @ shared_up_w.T) @ shared_down_w.T
        out = out + sh
        return out.reshape(B, S, H)
    x = x + _L0_ffn_ref(_L0_cond_ref(x, cond_2048[:, None, :], L0_cond_W_emb, L0_cond_b_emb, L0_cond_g_norm, L0_cond_W_qkv, L0_cond_g_q, L0_cond_g_k, L0_cond_W_out), L0_ffn_gate_weight, L0_ffn_expert_gate_w, L0_ffn_expert_up_w, L0_ffn_expert_down_w, L0_ffn_shared_gate_w, L0_ffn_shared_up_w, L0_ffn_shared_down_w)
    return x

_drawn_inputs = setup_inputs


def setup_inputs(seed=0):
    import zlib

    import numpy as np

    out = dict(_drawn_inputs(seed))
    spreads = {'L0_cond_b_emb': (0.0, 0.482),
     'L0_cond_g_norm': (1.0, 0.6),
     'L0_cond_g_q': (1.0, 0.6),
     'L0_cond_g_k': (1.0, 0.6)}
    factors = {}
    for name, (base, spread) in spreads.items():
        noise = np.random.default_rng([zlib.crc32(name.encode()), seed]).standard_normal(out[name].shape)
        drawn = base * np.exp(spread * noise) if base else spread * noise
        out[name] = jnp.asarray(drawn.astype(out[name].dtype))
    for name, factor in factors.items():
        out[name] = (out[name] * factor).astype(out[name].dtype)
    return out
```

```python
from contextlib import ExitStack

import concourse.bass as bass
from concourse import mybir

ALU = mybir.AluOpType
ACT = mybir.ActivationFunctionType
AX = mybir.AxisListType
F32 = mybir.dt.float32
F32R = mybir.dt.float32r

P = 128
B = 4
S = 512
D = 512
HEADS = 16
DH = D // HEADS
KT = D // P
TT = S // P
HG = P // DH
NG = HEADS // HG
SR = 3 * DH
EPS = 1e-6
CREDIT = 16
M_STEP = (5, 5, 6, 0)
M_FIRST = (0, 5, 10, 16)


def attention_block(nc, x, cond_t, w_emb, b_emb, g_norm, w_qkv, g_q, g_k, w_out, h_rows, out):
    with ExitStack() as ctx:
        def sb(name, shape, dt=F32):
            return ctx.enter_context(nc.sbuf_tensor(name, shape, dt))

        def sem(name):
            return ctx.enter_context(nc.semaphore(name))

        ps = ctx.enter_context(nc.psum_tensor("ps", [P, 8, S], F32))

        wqkv = sb("wqkv", [P, 2, KT, 3 * D], F32R)
        wout = sb("wout", [P, 2, KT, D], F32R)
        xn = sb("xn", [P, 2, KT, S], F32R)
        xtmp = sb("xtmp", [P, 2, S])
        qk = sb("qk", [P, TT, 2 * D])
        v = sb("v", [P, TT, D])
        q_st = sb("q_st", [P, 3, HG, S], F32R)
        k_st = sb("k_st", [P, 3, HG, S], F32R)
        p_sb = sb("p_sb", [P, 2, HG, S])
        o_t = sb("o_t", [P, NG, S])
        o_hl = sb("o_hl", [P, 2, NG, S], F32R)
        ident = sb("ident", [P, P])
        ones = sb("ones", [P, DH])
        ab = sb("ab", [P, 2, KT, B])
        condt = sb("condt", [P, KT, B])
        bemb = sb("bemb", [P, 2 * KT])
        gn = sb("gn", [P, KT])
        gqk = sb("gqk", [P, 2, DH])
        grow = sb("grow", [P, DH])
        ssx = sb("ssx", [P, TT])
        rx = sb("rx", [P, TT])
        ss = sb("ss", [P, 2, 2 * HEADS])
        rr = sb("rr", [P, 2, 2 * HEADS])
        mhalf = sb("mhalf", [P, 2 * HEADS])
        mx = sb("mx", [P, 2, HG * TT])
        nm = sb("nm", [HG * TT, 2, P], F32R)
        x_nat = p_sb[:, 1, :, :]
        sq = p_sb[:, 0, 0:2, :]
        parts = xn[:].rearrange("p a k n -> p (a k n)")[:, 0:2 * 2 * 2 * TT * SR].rearrange(
            "p (w r h t c) -> p w r h t c", w=2, r=2, h=2, t=TT)
        w_raw = [p_sb[:, 0, 0:3, :], p_sb[:, 1, 0:3, :]]

        rows_out = sem("rows_out")
        const_in = sem("const_in")
        wemb_in = sem("wemb_in")
        wraw_in = [sem("wraw_in0"), sem("wraw_in1")]
        ident0 = sem("ident0")
        pool_const = sem("pool_const")
        pool_settled = sem("pool_settled")
        w_hi = sem("w_hi")
        diag_ready = sem("diag_ready")
        w_lo = sem("w_lo")
        emb_mm = sem("emb_mm")
        pre = sem("pre")
        ab_ready = sem("ab_ready")
        ones_ready = sem("ones_ready")
        grow_ready = sem("grow_ready")
        x_in = sem("x_in")
        ssx_ready = sem("ssx_ready")
        vx_ready = sem("vx_ready")
        rx_ready = sem("rx_ready")
        xs_ready = sem("xs_ready")
        xt_ready = sem("xt_ready")
        xtmp_ready = sem("xtmp_ready")
        xh_ready = sem("xh_ready")
        xl_ready = sem("xl_ready")
        qkv_ready = sem("qkv_ready")
        sq_ready = sem("sq_ready")
        v_ready = sem("v_ready")
        ss_ready = sem("ss_ready")
        vv_ready = sem("vv_ready")
        rr_ready = sem("rr_ready")
        qk_ready = sem("qk_ready")
        t_ready = sem("t_ready")
        part_hi = sem("part_hi")
        part_lo = sem("part_lo")
        qg_ready = sem("qg_ready")
        stack_ready = sem("stack_ready")
        m_ready = sem("m_ready")
        max_ready = sem("max_ready")
        maxt_ready = sem("maxt_ready")
        nmhi_ready = sem("nmhi_ready")
        nm_ready = sem("nm_ready")
        nm_in = sem("nm_in")
        st_ready = sem("st_ready")
        exp_ready = sem("exp_ready")
        pv_ready = sem("pv_ready")
        rsum_ready = sem("rsum_ready")
        norm_ready = sem("norm_ready")
        oh_ready = sem("oh_ready")
        ol_ready = sem("ol_ready")
        w_ready = sem("w_ready")
        h_ready = sem("h_ready")
        h_out = [sem("h_out0"), sem("h_out1")]

        x_tiles = x.rearrange("(b t p) h -> b p t h", b=B, p=P)
        h_tiles = h_rows[0:B * S].rearrange("(b t p) h -> b t p h", b=B, p=P)

        block = ctx.enter_context(nc.Block())
        w_emb_sb = qk[:, :, :]

        def part(n, r, c):
            return parts[:, n % 2, r, :, :, c * DH:(c + 1) * DH].rearrange("p h t d -> p t h d")

        def heads_of(n, r):
            return qk[:, :, r * D + 2 * n * DH:r * D + 2 * (n + 1) * DH].rearrange("p t (h d) -> p t h d", d=DH)

        @block.sync
        def _(sp):
            sp.dma_start(out[0:B * S], x).then_inc(rows_out, 16)
            sp.dma_start(out[B * S:B * S + P], x[0:P]).then_inc(rows_out, 16)
            sp.dma_start(h_rows[B * S:B * S + P], x[0:P]).then_inc(rows_out, 16)
            sp.dma_start(condt[:], cond_t).then_inc(const_in, 16)
            sp.dma_start(bemb[:], b_emb).then_inc(const_in, 16)
            sp.dma_start(gn[:], g_norm).then_inc(const_in, 16)
            sp.dma_start(gqk[:, 0], g_q.broadcast_to([P, DH])).then_inc(const_in, 16)
            sp.dma_start(gqk[:, 1], g_k.broadcast_to([P, DH])).then_inc(const_in, 16)
            sp.dma_start(w_emb_sb, w_emb).then_inc(wemb_in, 16)
            for n in range(KT + 2):
                if n >= 2:
                    sp.wait_ge(w_lo, n - 1)
                if n < KT:
                    sp.dma_start(w_raw[n % 2], w_qkv[:, n]).then_inc(wraw_in[n % 2], 16)
                else:
                    k = 2 * (n - KT)
                    sp.dma_start(w_raw[n % 2][:, 0:2], w_out[:, k:k + 2]).then_inc(wraw_in[n % 2], 16)
            sp.wait_ge(w_lo, KT + 2)
            for credit in (nm_in, h_out[0], h_out[1]):
                sp.sem_inc(credit, CREDIT)
            with sp.Fori(0, B) as b:
                sp.wait_ge(pv_ready, b * (NG * TT) + 1)
                sp.dma_start(x_nat, x_tiles[b]).then_inc(x_in, 16)
                for g in range(NG):
                    sp.wait_ge(nm_ready, b * NG + g + 1)
                    for part in range(2):
                        row = SR + part
                        sp.dma_start(
                            q_st[row:row + 1, g % 3].rearrange("o h (t q) -> o (h t) q", q=P).bitcast(F32),
                            nm[:, part, :].bitcast(F32)).then_inc(nm_in, 16)
                for m in range(KT):
                    sp.wait_ge(h_ready, b * KT + m + 2)
                    sp.dma_start(h_tiles[b, m], xtmp[:, m % 2]).then_inc(h_out[m % 2], 16)
            for slot in range(2):
                sp.wait_ge(h_out[slot], CREDIT + 16 * B * KT // 2)
            sp.wait_ge(rows_out, 48)

        @block.gpsimd
        def _(pool):
            nc.gpsimd.memset(ident[:], 0.0).then_inc(ident0, 1)
            pool.wait_ge(ident0, 1)
            nc.gpsimd.affine_select(out=ident[:], in_=ident[:], compare_op=ALU.not_equal, fill=1.0, base=0,
                                    pattern=[[-1, P]], channel_multiplier=1).then_inc(pool_const, 1)
            nc.gpsimd.memset(ones[:], 1.0).then_inc(pool_const, 1)
            nc.gpsimd.memset(mhalf[:], -0.5).then_inc(pool_const, 1)
            pool.wait_ge(pool_const, 3)

            def settled():
                pool.sem_inc(pool_settled, 1)

            with pool.Fori(0, B) as b:
                pool.wait_ge(vx_ready, b + 1)
                nc.gpsimd.tensor_tensor(rx[:], ssx[:], mhalf[:, 0:TT], ALU.pow).then_inc(rx_ready, 1)
                for j in range(KT):
                    pool.wait_ge(xtmp_ready, b * KT + j + 1)
                    settled()
                    nc.gpsimd.tensor_copy(xn[:, 0, j], xtmp[:, j % 2]).then_inc(xh_ready, 1)
                for t in range(TT):
                    pool.wait_ge(vv_ready, b * TT + t + 1)
                    nc.gpsimd.tensor_tensor(rr[:, t % 2], ss[:, t % 2], mhalf[:], ALU.pow).then_inc(rr_ready, 1)

                def part_high(n):
                    if n == 0:
                        pool.wait_ge(qg_ready, (b + 1) * TT)
                    if n >= 2:
                        pool.wait_ge(t_ready, b * HEADS + 2 * (n - 1))
                    settled()
                    for r, c in ((0, 0), (1, 0), (0, 2), (1, 1)):
                        nc.gpsimd.tensor_copy(part(n, r, c), heads_of(n, r)).then_inc(part_hi, 1)

                def high_o(g):
                    pool.wait_ge(norm_ready, b * NG + g + 1)
                    settled()
                    nc.gpsimd.tensor_copy(o_hl[:, 0, g], o_t[:, g]).then_inc(oh_ready, 1)

                part_high(0)
                for vg in range(-2, NG):
                    for s in range(TT):
                        n = (HG * (vg + 2) + s) // 2 + 1
                        if s % 2 == 0 and n < HEADS // 2:
                            part_high(n)
                        if vg >= 1 and s == 1:
                            high_o(vg - 1)
                high_o(NG - 1)

        @block.scalar
        def _(act):
            for n in range(KT + 2):
                act.wait_ge(wraw_in[n % 2], 16 * (n // 2 + 1))
                if n < KT:
                    out, raw = wqkv[:, 0, n], w_raw[n % 2]
                else:
                    k = 2 * (n - KT)
                    act.wait_ge(diag_ready, k + 2)
                    out, raw = wout[:, 0, k:k + 2], w_raw[n % 2][:, 0:2]
                    out = out.rearrange("p k n -> p (k n)")
                    raw = raw.rearrange("p k n -> p (k n)")
                if n < KT:
                    raw = raw.rearrange("p k n -> p (k n)")
                nc.scalar.copy(out, raw).then_inc(w_hi, 1)
            act.wait_ge(ab_ready, 2)
            with act.Fori(0, B) as b:
                act.wait_ge(x_in, b * 16 + 16)
                for t in range(TT):
                    ins = nc.scalar.activation(p_sb[:, 0, t], x_nat[:, t], ACT.Square, accum_out=ssx[:, t:t + 1])
                ins.then_inc(ssx_ready, 1)
                for slot in range(2):
                    act.wait_ge(h_out[slot], b * (8 * KT) + CREDIT)
                for j in range(KT):
                    act.wait_ge(xt_ready, b * KT + j + 1)
                    if j >= 2:
                        act.wait_ge(xl_ready, b * KT + j - 1)
                    nc.scalar.activation(xtmp[:, j % 2], ps[:, j % 2], ACT.Identity,
                                         bias=ab[:, 1, j, bass.ds(b, 1)],
                                         scale=ab[:, 0, j, bass.ds(b, 1)]).then_inc(xtmp_ready, 1)
                for t in range(TT):
                    bank = 2 if t % 2 == 0 else 5
                    act.wait_ge(qkv_ready, b * TT + t + 1)
                    if t >= 1:
                        act.wait_ge(ss_ready, b * TT + t)
                    nc.scalar.activation(sq, ps[:, bank:bank + 2], ACT.Square).then_inc(sq_ready, 1)
                    nc.scalar.copy(v[:, t], ps[:, bank + 2]).then_inc(v_ready, 1)

                def stack(g, h):
                    act.wait_ge(t_ready, b * HEADS + HG * g + h + 1)
                    for r in range(2):
                        nc.scalar.copy((q_st, k_st)[r][0:SR, g % 3, h], ps[0:SR, r]).then_inc(stack_ready, 1)

                def exps(g, kt, pair):
                    n = (TT * g + kt) * 2 + pair
                    act.wait_ge(st_ready, b * (NG * TT * 2) + n + 1)
                    if TT * g + kt >= 2:
                        act.wait_ge(pv_ready, b * (NG * TT) + TT * g + kt)
                    nc.scalar.activation(p_sb[:, kt % 2, 2 * pair:2 * pair + 2], ps[:, 4:6],
                                         ACT.Exp).then_inc(exp_ready, 1)

                for vg in range(-2, NG):
                    for s in range(TT):
                        if vg + 2 < NG:
                            stack(vg + 2, s)
                        if vg >= 0:
                            exps(vg, s, 0)
                            exps(vg, s, 1)

        @block.tensor
        def _(pe):
            pe.wait_ge(const_in, 16 * 5)
            pe.wait_ge(wemb_in, 16)
            for m in range(2 * KT):
                for k in range(KT):
                    ins = pe.matmul(ps[:, 0, m * B:(m + 1) * B], w_emb_sb[:, k, m * P:(m + 1) * P],
                                    condt[:, k], start=(k == 0), stop=(k == KT - 1))
            ins.then_inc(emb_mm, 1)
            pe.wait_ge(pool_const, 3)
            pe.wait_ge(ab_ready, 2)
            pe.wait_ge(ones_ready, 1)
            pe.sem_inc(pv_ready, 1)
            with pe.Fori(0, B) as b:
                pe.wait_ge(xs_ready, b + 1)
                for j in range(KT):
                    if j >= 2:
                        pe.wait_ge(xtmp_ready, b * KT + j - 1)
                    for t in range(TT):
                        ins = pe.transpose(ps[:, j % 2, t * P:(t + 1) * P], x_nat[:, t, j * P:(j + 1) * P], ident[:])
                    ins.then_inc(xt_ready, 1)
                pe.wait_ge(w_lo, KT + 2)
                pe.wait_ge(h_ready, b * KT + 1)
                for t in range(TT):
                    bank = 2 if t % 2 == 0 else 5
                    if t >= 2:
                        pe.wait_ge(qk_ready, b * TT + t - 1)
                        pe.wait_ge(v_ready, b * TT + t - 1)
                    for j in range(KT):
                        if t == 0:
                            pe.wait_ge(xl_ready, b * KT + j + 1)
                        for xpart, wpart in ((0, 0), (0, 1), (1, 0)):
                            for c in range(3):
                                ins = pe.matmul(ps[:, bank + c], xn[:, xpart, j, t * P:(t + 1) * P],
                                                wqkv[:, wpart, j, c * D:(c + 1) * D],
                                                start=(j == 0 and xpart + wpart == 0),
                                                stop=(j == KT - 1 and xpart == 1))
                    ins.then_inc(qkv_ready, 1)
                pe.wait_ge(qk_ready, (b + 1) * TT)
                pe.wait_ge(v_ready, (b + 1) * TT)

                def transposes(g, h):
                    n = HG * g + h
                    pe.wait_ge(part_lo, b * HEADS + 2 * (n // 2) + 2)
                    if n >= 1:
                        pe.wait_ge(stack_ready, b * (2 * HEADS) + 2 * n)
                    if h == 0 and g >= 2:
                        pe.wait_ge(nm_ready, b * NG + g - 1)
                    for r in range(2):
                        for t in range(TT):
                            ins = pe.transpose(ps[0:SR, r, t * P:(t + 1) * P],
                                               parts[:, n // 2 % 2, r, n % 2, t].bitcast(F32), ident[:])
                    ins.then_inc(t_ready, 1)

                def max_scores(g, i):
                    h, t = divmod(i, TT)
                    n = HG * TT * g + i
                    pe.wait_ge(stack_ready, b * (2 * HEADS) + 2 * (HG * g + h) + 2)
                    if n >= 2:
                        pe.wait_ge(max_ready, b * (HEADS * TT) + n - 1)
                    pe.matmul(ps[:, 2 + i % 2], q_st[0:SR, g % 3, h, t * P:(t + 1) * P],
                              k_st[0:SR, g % 3, h], start=True, stop=True).then_inc(m_ready, 1)

                def max_rows(g):
                    pe.wait_ge(max_ready, b * (HEADS * TT) + HG * TT * (g + 1))
                    if g + 2 < NG:
                        n = HG * (g + 1) + HG
                        pe.wait_ge(stack_ready, b * (2 * HEADS) + 2 * n)
                    pe.transpose(ps[0:HG * TT, 0, 0:P], mx[:, g % 2], ident[:]).then_inc(maxt_ready, 1)

                def scores(g, kt, pair):
                    n = (TT * g + kt) * 2 + pair
                    if kt == 0 and pair == 0:
                        pe.wait_ge(nm_in, b * (NG * 32) + 32 * (g + 1) + CREDIT)
                    if n >= 1:
                        pe.wait_ge(exp_ready, b * (NG * TT * 2) + n)
                    for i in range(2):
                        h = 2 * pair + i
                        ins = pe.matmul(ps[:, 4 + i], k_st[0:SR + 2, g % 3, h, kt * P:(kt + 1) * P],
                                        q_st[0:SR + 2, g % 3, h], start=True, stop=True)
                    ins.then_inc(st_ready, 1)

                def products(g, kt):
                    pe.wait_ge(exp_ready, b * (NG * TT * 2) + (TT * g + kt) * 2 + 2)
                    if kt == 0 and g >= 1:
                        pe.wait_ge(norm_ready, b * NG + g)
                    for what in range(2):
                        for h in range(HG):
                            col = (HG * g + h) * DH
                            w = v[:, kt, col:col + DH] if what == 0 else ones[:]
                            ins = pe.matmul(ps[h * DH:(h + 1) * DH, 6 + what], w, p_sb[:, kt % 2, h],
                                            start=(kt == 0), stop=(kt == TT - 1))
                    ins.then_inc(pv_ready, 1)

                for vg in range(-2, NG):
                    for s in range(TT):
                        if vg + 2 < NG:
                            transposes(vg + 2, s)
                        if vg >= 0:
                            scores(vg, s, 0)
                        if -1 <= vg < NG - 1:
                            for i in range(M_FIRST[s], M_FIRST[s] + min(2, M_STEP[s])):
                                max_scores(vg + 1, i)
                        if vg >= 0 and (vg, s) != (0, 0):
                            products(*divmod(TT * vg + s - 1, TT))
                        if vg >= 0:
                            scores(vg, s, 1)
                        if -1 <= vg < NG - 1:
                            for i in range(M_FIRST[s] + 2, M_FIRST[s] + M_STEP[s]):
                                max_scores(vg + 1, i)
                    if -1 <= vg < NG - 1:
                        max_rows(vg + 1)
                products(NG - 1, TT - 1)

                for m in range(TT):
                    if m >= 2:
                        pe.wait_ge(h_ready, b * KT + m)
                    for k in range(KT):
                        if m == 0:
                            pe.wait_ge(ol_ready, b * NG + k + 1)
                        for wpart, opart in ((0, 0), (0, 1), (1, 0)):
                            ins = pe.matmul(ps[:, 2 + m % 2], o_hl[:, opart, k, m * P:(m + 1) * P],
                                            wout[:, wpart, k], start=(k == 0 and wpart + opart == 0),
                                            stop=(k == KT - 1 and wpart == 1))
                    ins.then_inc(w_ready, 1)

        @block.vector
        def _(dve):
            nc.vector.memset(k_st[SR:SR + DH].bitcast(F32), 1.0).then_inc(ones_ready, 1)
            dve.wait_ge(const_in, 16 * 5)
            nc.vector.scalar_tensor_tensor(out=grow[:], in0=gqk[:, 0], scalar=float(DH) ** -0.5,
                                           in1=gqk[:, 1], op0=ALU.mult, op1=ALU.mult).then_inc(grow_ready, 1)
            dve.wait_ge(pool_const, 3)
            dve.wait_ge(emb_mm, 1)
            sv = ps[:, 0, 0:2 * KT * B].rearrange("p (m b) -> p m b", b=B)
            bb = bemb[:].rearrange("p (m o) -> p m o", o=1).broadcast_to([P, 2 * KT, B])
            dve.wait_ge(grow_ready, 1)
            nc.vector.tensor_tensor(ab[:].rearrange("p a k b -> p (a k) b"), sv, bb, ALU.add).then_inc(ab_ready, 1)
            dve.wait_ge(ab_ready, 1)
            nc.vector.scalar_tensor_tensor(out=ab[:, 0], in0=ab[:, 0], scalar=1.0,
                                           in1=gn[:].rearrange("p (k o) -> p k o", o=1).broadcast_to([P, KT, B]),
                                           op0=ALU.add, op1=ALU.mult).then_inc(ab_ready, 1)
            for n in range(KT + 2):
                if n >= KT:
                    dve.wait_ge(wraw_in[n % 2], 16 * (n // 2 + 1))
                    for i in range(2):
                        diag = w_raw[n % 2][:, i, (2 * (n - KT) + i) * P:(2 * (n - KT) + i + 1) * P]
                        nc.vector.tensor_tensor(diag, diag, ident[:], ALU.add).then_inc(diag_ready, 1)
                dve.wait_ge(w_hi, n + 1)
                if n < KT:
                    hi, lo, raw = wqkv[:, 0, n], wqkv[:, 1, n], w_raw[n % 2]
                    raw = raw.rearrange("p k n -> p (k n)")
                else:
                    k = 2 * (n - KT)
                    hi, lo, raw = wout[:, 0, k:k + 2], wout[:, 1, k:k + 2], w_raw[n % 2][:, 0:2]
                nc.vector.tensor_tensor(lo, raw, hi.bitcast(F32), ALU.subtract).then_inc(w_lo, 1)
            dve.sem_inc(h_ready, 1)
            with dve.Fori(0, B) as b:
                dve.wait_ge(ssx_ready, b + 1)
                nc.vector.tensor_scalar(ssx[:], ssx[:], 1.0 / D, EPS, ALU.mult, ALU.add).then_inc(vx_ready, 1)
                dve.wait_ge(rx_ready, b + 1)
                for t in range(TT):
                    ins = nc.vector.tensor_scalar(x_nat[:, t], x_nat[:, t], rx[:, t:t + 1], None, ALU.mult)
                ins.then_inc(xs_ready, 1)
                for j in range(KT):
                    dve.wait_ge(xh_ready, b * KT + j + 1)
                    nc.vector.tensor_tensor(xn[:, 1, j], xtmp[:, j % 2], xn[:, 0, j].bitcast(F32),
                                            ALU.subtract).then_inc(xl_ready, 1)
                for t in range(TT):
                    bank = 2 if t % 2 == 0 else 5
                    dve.wait_ge(sq_ready, b * TT + t + 1)
                    nc.vector.tensor_reduce(ss[:, t % 2], sq.rearrange("p r (h d) -> p (r h) d", d=DH),
                                            AX.X, ALU.add).then_inc(ss_ready, 1)
                    dve.wait_ge(ss_ready, b * TT + t + 1)
                    nc.vector.tensor_scalar(ss[:, t % 2], ss[:, t % 2], 1.0 / DH, EPS, ALU.mult,
                                            ALU.add).then_inc(vv_ready, 1)
                    dve.wait_ge(rr_ready, b * TT + t + 1)
                    nc.vector.tensor_tensor(
                        qk[:, t].rearrange("p (h d) -> p h d", d=DH),
                        ps[:, bank:bank + 2].rearrange("p r (h d) -> p (r h) d", d=DH),
                        rr[:, t % 2].rearrange("p (h o) -> p h o", o=1).broadcast_to([P, 2 * HEADS, DH]),
                        ALU.mult).then_inc(qk_ready, 1)
                    dve.wait_ge(qk_ready, b * TT + t + 1)
                    q_heads = qk[:, t, 0:D].rearrange("p (h d) -> p h d", d=DH)
                    nc.vector.tensor_tensor(
                        q_heads, q_heads,
                        grow[:].rearrange("p (o d) -> p o d", o=1).broadcast_to([P, HEADS, DH]),
                        ALU.mult).then_inc(qg_ready, 1)

                def part_low(n):
                    dve.wait_ge(part_hi, b * (2 * HEADS) + 4 * (n + 1))
                    for r, c in ((0, 1), (1, 2)):
                        nc.vector.tensor_tensor(part(n, r, c), heads_of(n, r), part(n, r, 0).bitcast(F32),
                                                ALU.subtract).then_inc(part_lo, 1)

                def maximum(g, i):
                    dve.wait_ge(m_ready, b * (HEADS * TT) + HG * TT * g + i + 1)
                    nc.vector.tensor_reduce(mx[:, g % 2, i:i + 1], ps[:, 2 + i % 2], AX.X,
                                            ALU.max).then_inc(max_ready, 1)

                def minus_max(g):
                    dve.wait_ge(maxt_ready, b * NG + g + 1)
                    dve.wait_ge(nm_in, b * (NG * 32) + 32 * g + CREDIT)
                    rows = ps[0:HG * TT, 0, 0:P]
                    nc.vector.tensor_scalar(nm[:, 0], rows, -1.0, None, ALU.mult).then_inc(nmhi_ready, 1)
                    dve.wait_ge(nmhi_ready, b * NG + g + 1)
                    nc.vector.scalar_tensor_tensor(out=nm[:, 1], in0=rows, scalar=-1.0,
                                                   in1=nm[:, 0].bitcast(F32), op0=ALU.mult,
                                                   op1=ALU.subtract).then_inc(nm_ready, 1)

                def normalise(g):
                    dve.wait_ge(pv_ready, b * (NG * TT) + TT * (g + 1) + 1)
                    nc.vector.reciprocal(o_t[:, g], ps[:, 7]).then_inc(rsum_ready, 1)
                    dve.wait_ge(rsum_ready, b * NG + g + 1)
                    nc.vector.tensor_tensor(o_t[:, g], ps[:, 6], o_t[:, g], ALU.mult).then_inc(norm_ready, 1)

                def low_o(g):
                    dve.wait_ge(oh_ready, b * NG + g + 1)
                    nc.vector.tensor_tensor(o_hl[:, 1, g], o_t[:, g], o_hl[:, 0, g].bitcast(F32),
                                            ALU.subtract).then_inc(ol_ready, 1)

                part_low(0)
                for vg in range(-2, NG):
                    for s in range(TT):
                        if -1 <= vg < NG - 1:
                            for i in range(M_FIRST[s], M_FIRST[s] + min(2, M_STEP[s])):
                                maximum(vg + 1, i)
                        if vg >= 1 and s == 0:
                            normalise(vg - 1)
                        n = (HG * (vg + 2) + s) // 2 + 1
                        if s % 2 == 0 and n < HEADS // 2:
                            part_low(n)
                        if vg >= 1 and s == 1:
                            low_o(vg - 1)
                        if -1 <= vg < NG - 1:
                            for i in range(M_FIRST[s] + 2, M_FIRST[s] + M_STEP[s]):
                                maximum(vg + 1, i)
                    if -1 <= vg < NG - 1:
                        minus_max(vg + 1)
                normalise(NG - 1)
                low_o(NG - 1)
                for m in range(TT):
                    dve.wait_ge(w_ready, b * KT + m + 1)
                    if m >= 2:
                        dve.wait_ge(h_out[m % 2], b * (8 * KT) + 16 * (m // 2) + CREDIT)
                    nc.vector.tensor_copy(xtmp[:, m % 2], ps[:, 2 + m % 2]).then_inc(h_ready, 1)


E_N = 8
I_W = 352
IC = -(-I_W // P)
I_REST = I_W - (IC - 1) * P
TOP = 2
TOK_TILES = B * S // P
SLOT_TILES = (B * S * TOP + E_N * (P - 1)) // P + 1
TILES = TOK_TILES + SLOT_TILES
SHARED = E_N


def ffn_block(nc, h_rows, gate_t, w_gu, w_down, out):
    assert TILES % 2 == 0
    with ExitStack() as ctx:
        def sb(name, shape, dt=F32):
            return ctx.enter_context(nc.sbuf_tensor(name, shape, dt))

        def sem(name):
            return ctx.enter_context(nc.semaphore(name))

        I32 = mybir.dt.int32
        U32 = mybir.dt.uint32
        ps = ctx.enter_context(nc.psum_tensor("ps2", [P, 8, 512], F32))

        wgu = sb("wgu", [P, E_N + 1, KT, 2 * I_W])
        wdn = sb("wdn", [P, E_N + 1, IC, D])
        gate = sb("gate", [P, KT, E_N])
        rows = sb("rows", [P, 2, D])
        rows_t = sb("rows_t", [P, 2, KT, P])
        act_g = sb("act_g", [P, 2, I_W])
        hid = sb("hid", [P, 2, I_W])
        hid_t = sb("hid_t", [P, 2, IC, P])
        y = sb("y", [P, 2, D])
        idx_g = sb("idx_g", [P, 2], U32)
        idx_s = sb("idx_s", [P, 2], U32)
        tab_tok = sb("tab_tok", [P, TILES], I32)
        tab_w = sb("tab_w", [P, TILES])
        tab_e = sb("tab_e", [1, TILES], I32)

        ident = sb("ident2", [P, P])
        ones = sb("ones2", [P, P])
        before = sb("before", [P, P])
        lane = sb("lane", [P, P])
        own = sb("own", [P, 1])
        token = sb("token", [P, TOK_TILES])
        logits = sb("logits", [P, TOK_TILES, E_N])
        top = sb("top", [P, TOK_TILES, 8])
        top_i = sb("top_i", [P, TOK_TILES, 8], U32)
        pick = sb("pick", [P, TOP, TOK_TILES])
        hot = sb("hot", [P, TOP, TOK_TILES, E_N])
        both = sb("both", [P, TOK_TILES, E_N])
        wts = sb("wts", [P, TOP, TOK_TILES])
        ex = sb("ex", [P, 2, TOK_TILES])
        tot = sb("tot", [P, E_N, TOK_TILES])
        run = sb("run", [P, E_N, TOK_TILES])
        carry = sb("carry", [P, E_N, TOK_TILES])
        cnt_i = sb("cnt_i", [P, E_N], I32)
        cnt = sb("cnt", [P, E_N])
        ends = sb("ends", [P, E_N])
        base = sb("base", [P, E_N])
        pos = sb("pos", [P, TOK_TILES, E_N])
        sel = sb("sel", [P, TOP, TOK_TILES, E_N])
        slot = sb("slot", [P, TOP * TOK_TILES])
        slot_i = sb("slot_i", [P, 3, TOP * TOK_TILES], I32)
        slot_p = sb("slot_p", [P, TOP * TOK_TILES])
        slot_j = sb("slot_j", [P, TOP * TOK_TILES])
        hot_p = sb("hot_p", [P, 2, P])
        hot_j = sb("hot_j", [P, 2, 2, SLOT_TILES])
        late = sb("late", [1, SLOT_TILES, E_N])
        tile_e = sb("tile_e", [1, SLOT_TILES])
        empty = sb("empty", [P, SLOT_TILES])
        tok_f = sb("tok_f", [P, SLOT_TILES])

        names = ("gate_in shared_in experts_in pool_ready ident_ready logit_rows_in0 logit_rows_in1 "
                 "logit_t logit_evac logit_mm logit_out r exp_done count_mm hot_done tab_mm "
                 "idx_ready rows_in0 rows_in1 rows_t_mm rows_t_out gate_mm up_mm silu_done hid_done "
                 "hid_t_mm hid_t_out down_mm y_ready y_out pool_settled").split()
        s = {n: sem(n + "_f") for n in names}
        rows_in = (s["rows_in0"], s["rows_in1"])
        block = ctx.enter_context(nc.Block())
        C = 2

        def at(n):
            return n + (C + 1)

        @block.sync
        def _(sp):
            sp.dma_start(gate[:], gate_t).then_inc(s["gate_in"], 16)
            for t in range(TOK_TILES):
                if t >= 2:
                    sp.wait_ge(s["logit_t"], t - 1)
                sp.dma_start(rows[:, t % 2], h_rows[t * P:(t + 1) * P]).then_inc(s[f"logit_rows_in{t % 2}"], 16)
                if t == 1:
                    sp.dma_start(wgu[:, SHARED], w_gu[SHARED]).then_inc(s["shared_in"], 16)
                    sp.dma_start(wdn[:, SHARED], w_down[SHARED]).then_inc(s["shared_in"], 16)
            for e in range(E_N):
                sp.dma_start(wgu[:, e], w_gu[e]).then_inc(s["experts_in"], 16)
                sp.dma_start(wdn[:, e], w_down[e]).then_inc(s["experts_in"], 16)

        @block.gpsimd
        def _(pool):
            nc.gpsimd.memset(ident[:], 0.0).then_inc(s["pool_ready"], 1)
            nc.gpsimd.memset(ones[:], 1.0).then_inc(s["pool_ready"], 1)
            pool.wait_ge(s["pool_ready"], 2)
            nc.gpsimd.affine_select(out=ident[:], in_=ident[:], compare_op=ALU.not_equal, fill=1.0, base=0,
                                    pattern=[[-1, P]], channel_multiplier=1).then_inc(s["ident_ready"], 1)
            nc.gpsimd.affine_select(out=before[:], in_=ones[:], compare_op=ALU.is_gt, fill=0.0, base=0,
                                    pattern=[[1, P]], channel_multiplier=-1).then_inc(s["pool_ready"], 1)
            nc.gpsimd.iota(lane[:], pattern=[[1, P]], base=0, channel_multiplier=0,
                           allow_small_or_imprecise_dtypes=True).then_inc(s["pool_ready"], 1)
            nc.gpsimd.iota(own[:], pattern=[[1, 1]], base=B * S + 1, channel_multiplier=1,
                           allow_small_or_imprecise_dtypes=True).then_inc(s["pool_ready"], 1)
            nc.gpsimd.iota(token[:], pattern=[[P, TOK_TILES]], base=1, channel_multiplier=1,
                           allow_small_or_imprecise_dtypes=True).then_inc(s["pool_ready"], 1)
            nc.gpsimd.iota(tab_tok[:, 0:TOK_TILES], pattern=[[P, TOK_TILES]], base=0,
                           channel_multiplier=1).then_inc(s["pool_ready"], 1)

            def gather(n, par):
                pool.wait_ge(s["idx_ready"], n + 1)
                pool.sem_inc(s["pool_settled"], 1)
                pool.indirect_dma_start(out=rows[:, par], out_offset=None, in_=h_rows,
                                        in_offset=bass.IndirectOffsetOnAxis(ap=idx_g[:, par:par + 1], axis=0),
                                        ).then_inc(rows_in[par], 16)

            def scatter(n, par):
                pool.wait_ge(s["y_ready"], at(n))
                if not isinstance(n, int) or n > 0:
                    pool.wait_ge(s["y_out"], 16 * n)
                pool.sem_inc(s["pool_settled"], 1)
                pool.indirect_dma_start(out=out, in_=y[:, par], in_offset=None,
                                        out_offset=bass.IndirectOffsetOnAxis(ap=idx_s[:, par:par + 1], axis=0),
                                        compute_op=ALU.add).then_inc(s["y_out"], 16)

            gather(0, 0)
            gather(1, 1)
            gather(2, 0)
            for m in (1, 2):
                gather(m + 2, m % 2)
                scatter(m - 1, 1 - m % 2)
            with pool.Fori(0, (TILES - 6) // 2) as i:
                for u in range(2):
                    m = i * 2 + (3 + u)
                    gather(m + 2, (1 + u) % 2)
                    scatter(m - 1, u % 2)
            gather(TILES - 1, 1)
            for n in range(TILES - 4, TILES):
                scatter(n, n % 2)
            pool.wait_ge(s["y_out"], 16 * TILES)

        @block.scalar
        def _(act):
            for t in range(TOK_TILES):
                act.wait_ge(s["logit_t"], t + 1)
                if t >= 2:
                    act.wait_ge(s["logit_mm"], t - 1)
                nc.scalar.copy(rows_t[:, t % 2].rearrange("p k n -> p (k n)"), ps[:, t % 2]).then_inc(s["logit_evac"], 1)
            act.wait_ge(s["r"], R_DIFF)
            nc.scalar.activation(ex[:, 0], ex[:, 1], ACT.Exp).then_inc(s["exp_done"], 1)
            for c in ("rows_t_out", "silu_done", "hid_t_out"):
                act.sem_inc(s[c], C)

            def rows_out(n, par):
                act.wait_ge(s["rows_t_mm"], n + 1)
                act.wait_ge(s["up_mm"], at(n - 2))
                nc.scalar.copy(rows_t[:, par].rearrange("p k n -> p (k n)"), ps[:, 0]).then_inc(s["rows_t_out"], 1)

            def silu(n, par):
                act.wait_ge(s["gate_mm"], n + 1)
                act.wait_ge(s["hid_done"], at(n - 2))
                nc.scalar.activation(act_g[:, par], ps[:, 2 + 2 * par, 0:I_W], ACT.Silu).then_inc(s["silu_done"], 1)

            def hid_out(n, par):
                act.wait_ge(s["hid_t_mm"], at(n))
                act.wait_ge(s["down_mm"], at(n - 2))
                nc.scalar.copy(hid_t[:, par, 0:IC - 1].rearrange("p k n -> p (k n)"),
                               ps[:, 1, 0:(IC - 1) * P])
                nc.scalar.copy(hid_t[0:I_REST, par, IC - 1], ps[0:I_REST, 1, (IC - 1) * P:IC * P]
                               ).then_inc(s["hid_t_out"], 1)

            rows_out(0, 0)
            silu(0, 0)
            rows_out(1, 1)
            with act.Fori(0, (TILES - 2) // 2) as i:
                for u in range(2):
                    n = i * 2 + (1 + u)
                    silu(n, (1 + u) % 2)
                    hid_out(n - 1, u % 2)
                    rows_out(n + 1, u % 2)
            silu(TILES - 1, 1)
            hid_out(TILES - 2, 0)
            hid_out(TILES - 1, 1)

        @block.tensor
        def _(pe):
            pe.wait_ge(s["ident_ready"], 1)
            pe.wait_ge(s["gate_in"], 16)

            def logit(t):
                pe.wait_ge(s["logit_evac"], t + 1)
                for k in range(KT):
                    ins = pe.matmul(ps[:, 2, t * E_N:(t + 1) * E_N], rows_t[:, t % 2, k], gate[:, k],
                                    start=(k == 0), stop=(k == KT - 1))
                ins.then_inc(s["logit_mm"], 1)

            for t in range(TOK_TILES):
                pe.wait_ge(s[f"logit_rows_in{t % 2}"], 16 * (t // 2 + 1))
                if t >= 2:
                    pe.wait_ge(s["logit_evac"], t - 1)
                for k in range(KT):
                    ins = pe.transpose(ps[:, t % 2, k * P:(k + 1) * P], rows[:, t % 2, k * P:(k + 1) * P], ident[:])
                ins.then_inc(s["logit_t"], 1)
                if t >= 1:
                    logit(t - 1)
            logit(TOK_TILES - 1)

            pe.wait_ge(s["pool_ready"], 7)
            pe.wait_ge(s["r"], R_HOT)
            flat = both[:].rearrange("p t e -> p (t e)")
            pe.matmul(ps[:, 3, 0:P], before[:], flat, start=True, stop=True)
            pe.matmul(ps[:, 3, P:2 * P], ones[:], flat, start=True, stop=True).then_inc(s["count_mm"], 1)
            for n in range(TOP * TOK_TILES):
                pe.wait_ge(s["hot_done"], 3 * (n + 1))
                pe.matmul(ps[:, 4, 0:2 * SLOT_TILES], hot_p[:, n % 2], hot_j[:, n % 2].rearrange("p a j -> p (a j)"),
                          start=(n == 0), stop=(n == TOP * TOK_TILES - 1)).then_inc(s["tab_mm"], 1)
            for c in ("up_mm", "hid_t_mm", "down_mm"):
                pe.sem_inc(s[c], C)

            def rows_turn(n, par):
                pe.wait_ge(rows_in[par], (n // 2 + 1) * 16 if isinstance(n, int) else n[1])
                n = n if isinstance(n, int) else n[0]
                pe.wait_ge(s["rows_t_out"], at(n - 1))
                for k in range(KT):
                    ins = pe.transpose(ps[:, 0, k * P:(k + 1) * P], rows[:, par, k * P:(k + 1) * P], ident[:])
                ins.then_inc(s["rows_t_mm"], 1)

            def gate_up(n, par, e, up):
                if up:
                    pe.wait_ge(s["hid_done"], at(n - 2))
                else:
                    pe.wait_ge(s["rows_t_out"], at(n))
                    pe.wait_ge(s["silu_done"], at(n - 2))
                for k in range(KT):
                    w = wgu[:, bass.ds(e, 1), k, up * I_W:(up + 1) * I_W].rearrange("p o n -> p (o n)")
                    ins = pe.matmul(ps[:, 2 + 2 * par + up, 0:I_W], rows_t[:, par, k], w,
                                    start=(k == 0), stop=(k == KT - 1))
                ins.then_inc(s["up_mm" if up else "gate_mm"], 1)

            def hid_turn(n, par):
                pe.wait_ge(s["hid_done"], at(n))
                pe.wait_ge(s["hid_t_out"], at(n - 1))
                for c in range(IC):
                    w = P if c < IC - 1 else I_REST
                    ins = pe.transpose(ps[0:w, 1, c * P:(c + 1) * P], hid[:, par, c * P:c * P + w], ident[:])
                ins.then_inc(s["hid_t_mm"], 1)

            def down(n, par, e):
                pe.wait_ge(s["hid_t_out"], at(n))
                pe.wait_ge(s["y_ready"], at(n - 2))
                for c in range(IC):
                    w = P if c < IC - 1 else I_REST
                    wd = wdn[0:w, bass.ds(e, 1), c].rearrange("p o n -> p (o n)")
                    ins = pe.matmul(ps[:, 6 + par], hid_t[0:w, par, c], wd, start=(c == 0), stop=(c == IC - 1))
                ins.then_inc(s["down_mm"], 1)

            def expert(n):
                return pe.value_load(tab_e[0:1, bass.ds(n, 1)], min_val=0, max_val=E_N)

            pe.wait_ge(s["shared_in"], 32)
            rows_turn(0, 0)
            gate_up(0, 0, SHARED, 0)
            rows_turn(1, 1)
            gate_up(0, 0, SHARED, 1)

            def body(i, first, u, e, e_last):
                n = i * 2 + (first + u)
                par = (first + u) % 2
                gate_up(n, par, e, 0)
                hid_turn(n - 1, 1 - par)
                rows_turn((n + 1, i * 16 + 16 * ((first + u + 1) // 2 + 1)), 1 - par)
                gate_up(n, par, e, 1)
                down(n - 1, 1 - par, e_last)

            with pe.Fori(0, (TOK_TILES - 2) // 2) as i:
                for u in range(2):
                    body(i, 1, u, SHARED, SHARED)
            pe.wait_ge(s["experts_in"], 32 * E_N)
            with pe.Fori(0, SLOT_TILES // 2) as i:
                for u in range(2):
                    n = i * 2 + (TOK_TILES - 1 + u)
                    body(i, TOK_TILES - 1, u, expert(n), expert(n - 1))
            n = TILES - 1
            e = expert(n)
            e_last = expert(n - 1)
            gate_up(n, 1, e, 0)
            hid_turn(n - 1, 0)
            gate_up(n, 1, e, 1)
            down(n - 1, 0, e_last)
            hid_turn(n, 1)
            down(n, 1, e)

        @block.vector
        def _(dve):
            done = [0]

            def step(ins):
                done[0] += 1
                ins.then_inc(s["r"], 1)
                dve.wait_ge(s["r"], done[0])

            V = nc.vector
            dve.wait_ge(s["pool_ready"], 7)
            step(V.memset(tab_e[:], SHARED))
            step(V.memset(tab_w[:], 1.0))
            step(V.memset(run[:], 1.0))
            step(V.memset(run[:, :, 0:1], 0.0))
            dve.wait_ge(s["logit_mm"], TOK_TILES)
            step(V.tensor_copy(logits[:].rearrange("p t e -> p (t e)"), ps[:, 2, 0:TOK_TILES * E_N]))
            for t in range(TOK_TILES):
                ins = V.max(top[:, t], logits[:, t])
            step(ins)
            for t in range(TOK_TILES):
                ins = V.max_index(top_i[:, t], top[:, t], logits[:, t])
            step(ins)
            step(V.tensor_tensor(ex[:, 1], top[:, :, 1], top[:, :, 0], ALU.subtract))
            assert done[0] == R_DIFF
            for c in range(TOP):
                step(V.tensor_copy(pick[:, c], top_i[:, :, c]))
                step(V.tensor_tensor(
                    hot[:, c],
                    pick[:, c].rearrange("p (t o) -> p t o", o=1).broadcast_to([P, TOK_TILES, E_N]),
                    lane[:, 0:E_N].rearrange("p (o e) -> p o e", o=1).broadcast_to([P, TOK_TILES, E_N]),
                    ALU.is_equal))
            step(V.tensor_tensor(both[:], hot[:, 0], hot[:, 1], ALU.add))
            assert done[0] == R_HOT
            dve.wait_ge(s["exp_done"], 1)
            step(V.tensor_scalar(ex[:, 1], ex[:, 0], 1.0, None, ALU.add))
            step(V.reciprocal(wts[:, 0], ex[:, 1]))
            step(V.tensor_tensor(wts[:, 1], ex[:, 0], wts[:, 0], ALU.mult))
            dve.wait_ge(s["count_mm"], 1)
            step(V.tensor_copy(tot[:], ps[:, 3, P:2 * P].rearrange("p (t e) -> p e t", e=E_N)))
            step(V.tensor_tensor_scan(carry[:].rearrange("p e t -> p (e t)"), run[:].rearrange("p e t -> p (e t)"),
                                      tot[:].rearrange("p e t -> p (e t)"), 0.0, ALU.mult, ALU.add))
            step(V.tensor_scalar(cnt_i[:], carry[:, :, TOK_TILES - 1], float(P - 1), None, ALU.add))
            step(V.tensor_scalar(cnt_i[:], cnt_i[:], 7, None, ALU.arith_shift_right))
            step(V.tensor_copy(cnt[:], cnt_i[:]))
            step(V.tensor_tensor_scan(ends[:], ones[:, 0:E_N], cnt[:], 0.0, ALU.mult, ALU.add))
            step(V.tensor_tensor(base[:], ends[:], cnt[:], ALU.subtract))
            step(V.tensor_tensor(carry[:], carry[:], tot[:], ALU.subtract))
            step(V.scalar_tensor_tensor(
                out=pos[:], in0=base[:].rearrange("p (o e) -> p o e", o=1).broadcast_to([P, TOK_TILES, E_N]),
                scalar=float(P), in1=carry[:].rearrange("p e t -> p t e"), op0=ALU.mult, op1=ALU.add))
            step(V.tensor_tensor(pos[:].rearrange("p t e -> p (t e)"), pos[:].rearrange("p t e -> p (t e)"),
                                 ps[:, 3, 0:P], ALU.add))
            for c in range(TOP):
                step(V.tensor_tensor(sel[:, c], hot[:, c], pos[:], ALU.mult))
            step(V.tensor_reduce(slot[:], sel[:].rearrange("p c t e -> p (c t) e"), AX.X, ALU.add))
            step(V.tensor_copy(slot_i[:, 0], slot[:]))
            step(V.tensor_scalar(slot_i[:, 1], slot_i[:, 0], P - 1, None, ALU.bitwise_and))
            step(V.tensor_scalar(slot_i[:, 2], slot_i[:, 0], 7, None, ALU.arith_shift_right))
            step(V.tensor_copy(slot_p[:], slot_i[:, 1]))
            step(V.tensor_copy(slot_j[:], slot_i[:, 2]))
            step(V.tensor_tensor(
                late[:], lane[0:1, 0:SLOT_TILES].rearrange("p (j o) -> p j o", o=1).broadcast_to([1, SLOT_TILES, E_N]),
                ends[0:1].rearrange("p (o e) -> p o e", o=1).broadcast_to([1, SLOT_TILES, E_N]), ALU.is_ge))
            step(V.tensor_reduce(tile_e[:], late[:], AX.X, ALU.add))
            step(V.tensor_scalar(tab_e[:, TOK_TILES:], tile_e[:], float(E_N - 1), None, ALU.min))
            for c in range(TOP):
                for t in range(TOK_TILES):
                    n = c * TOK_TILES + t
                    if n >= 2:
                        dve.wait_ge(s["tab_mm"], n - 1)
                    V.tensor_scalar(hot_p[:, n % 2], lane[:], slot_p[:, n:n + 1], None,
                                    ALU.is_equal).then_inc(s["hot_done"], 1)
                    V.tensor_scalar(hot_j[:, n % 2, 0], lane[:, 0:SLOT_TILES], slot_j[:, n:n + 1],
                                    token[:, t:t + 1], ALU.is_equal, ALU.mult).then_inc(s["hot_done"], 1)
                    V.tensor_scalar(hot_j[:, n % 2, 1], lane[:, 0:SLOT_TILES], slot_j[:, n:n + 1],
                                    wts[:, c, t:t + 1], ALU.is_equal, ALU.mult).then_inc(s["hot_done"], 1)
            dve.wait_ge(s["tab_mm"], TOP * TOK_TILES)
            step(V.tensor_copy(tok_f[:], ps[:, 4, 0:SLOT_TILES]))
            step(V.tensor_copy(tab_w[:, TOK_TILES:], ps[:, 4, SLOT_TILES:2 * SLOT_TILES]))
            step(V.tensor_scalar(empty[:], tok_f[:], 0.0, None, ALU.is_equal))
            step(V.scalar_tensor_tensor(out=tok_f[:], in0=empty[:], scalar=own[:], in1=tok_f[:],
                                        op0=ALU.mult, op1=ALU.add))
            step(V.tensor_scalar(tab_tok[:, TOK_TILES:], tok_f[:], -1.0, None, ALU.add))

            for c in ("hid_done", "y_ready"):
                dve.sem_inc(s[c], C)

            def index(n, par):
                V.tensor_copy(idx_g[:, par:par + 1], tab_tok[:, bass.ds(n, 1)]).then_inc(s["idx_ready"], 1)

            def multiply(n, par):
                dve.wait_ge(s["up_mm"], at(n))
                dve.wait_ge(s["silu_done"], at(n))
                dve.wait_ge(s["hid_t_mm"], at(n - 2))
                V.tensor_tensor(hid[:, par], act_g[:, par], ps[:, 3 + 2 * par, 0:I_W], ALU.mult).then_inc(s["hid_done"], 1)

            def weigh(n, par):
                dve.wait_ge(s["down_mm"], at(n))
                if not isinstance(n, int) or n > 1:
                    dve.wait_ge(s["y_out"], 16 * (n - 1))
                V.tensor_copy(idx_s[:, par:par + 1], tab_tok[:, bass.ds(n, 1)])
                V.tensor_scalar(y[:, par], ps[:, 6 + par], tab_w[:, bass.ds(n, 1)], None, ALU.mult).then_inc(s["y_ready"], 1)

            index(0, 0)
            index(1, 1)
            multiply(0, 0)
            index(2, 0)
            for n in (1, 2):
                multiply(n, n % 2)
                index(n + 2, n % 2)
                weigh(n - 1, 1 - n % 2)
            with dve.Fori(0, (TILES - 6) // 2) as i:
                for u in range(2):
                    n = i * 2 + (3 + u)
                    multiply(n, (1 + u) % 2)
                    index(n + 2, (1 + u) % 2)
                    weigh(n - 1, u % 2)
            multiply(TILES - 3, 1)
            index(TILES - 1, 1)
            weigh(TILES - 4, 0)
            multiply(TILES - 2, 0)
            weigh(TILES - 3, 1)
            multiply(TILES - 1, 1)
            weigh(TILES - 2, 0)
            weigh(TILES - 1, 1)


R_DIFF = 8
R_HOT = 13


def kernel(**inputs):
    import numpy as np
    import concourse.bacc as bacc
    from concourse.bass_utils import run_bass_kernel_spmd as run

    nc = bacc.Bacc("TRN2", target_bir_lowering=False, num_devices=1)
    i = {k: np.asarray(a) for k, a in inputs.items()}

    def tiles(a):
        return np.ascontiguousarray(a.reshape(-1, P, a.shape[-1]).transpose(1, 0, 2))

    def all_experts(name):
        return np.concatenate([i[f"L0_ffn_expert_{name}_w"], i[f"L0_ffn_shared_{name}_w"][None]])

    gu = np.concatenate([all_experts("gate"), all_experts("up")], axis=1)
    gu = gu.reshape(E_N + 1, 2 * I_W, KT, P).transpose(0, 3, 2, 1)
    dn = np.pad(all_experts("down"), ((0, 0), (0, 0), (0, IC * P - I_W)))
    dn = dn.reshape(E_N + 1, D, IC, P).transpose(0, 3, 2, 1)
    arrays = {
        "x": np.ascontiguousarray(i["x"].reshape(B * S, D)),
        "cond_t": tiles(np.ascontiguousarray(i["cond_2048"].T)),
        "w_emb": tiles(i["L0_cond_W_emb"]),
        "b_emb": np.ascontiguousarray(i["L0_cond_b_emb"].reshape(2 * KT, P).T),
        "g_norm": np.ascontiguousarray(i["L0_cond_g_norm"].reshape(KT, P).T),
        "w_qkv": np.ascontiguousarray(tiles(i["L0_cond_W_qkv"]).reshape(P, KT, 3, D)),
        "g_q": i["L0_cond_g_q"].reshape(1, DH),
        "g_k": i["L0_cond_g_k"].reshape(1, DH),
        "w_out": tiles(i["L0_cond_W_out"]),
        "gate_t": tiles(np.ascontiguousarray(i["L0_ffn_gate_weight"].T)),
        "w_gu": np.ascontiguousarray(gu),
        "w_down": np.ascontiguousarray(dn),
    }
    ap = {k: nc.dram_tensor(k, a.shape, F32, kind="ExternalInput").ap() for k, a in arrays.items()}
    h_rows = nc.dram_tensor("h_rows", (B * S + P, D), F32, kind="Internal").ap()
    out = nc.dram_tensor("out", (B * S + P, D), F32, kind="ExternalOutput").ap()
    attention_block(nc, *(ap[k] for k in ("x", "cond_t", "w_emb", "b_emb", "g_norm", "w_qkv", "g_q", "g_k",
                                          "w_out")), h_rows, out)
    ffn_block(nc, h_rows, ap["gate_t"], ap["w_gu"], ap["w_down"], out)
    got = run(nc, [arrays], core_ids=[0]).results[0]["out"]
    return np.ascontiguousarray(got[0:B * S]).reshape(B, S, D)
```

```python
from contextlib import ExitStack

import concourse.bass as bass
from concourse import mybir

ALU = mybir.AluOpType
ACT = mybir.ActivationFunctionType
AX = mybir.AxisListType
F32 = mybir.dt.float32
F32R = mybir.dt.float32r

P = 128
B = 4
S = 512
D = 512
HEADS = 16
DH = D // HEADS
KT = D // P
TT = S // P
HG = P // DH
NG = HEADS // HG
SR = 3 * DH
EPS = 1e-6
LN_EXP = 6
CREDIT = 16
M_FIRST = (0, 2, 8, 16, 16)
SLOTS = {
    (0, 1): (("x", 0), ("x", 1)), (0, 2): (("x", 2), ("x", 3)),
    (0, 3): (("q", 0), ("k", 0)), (1, 2): (("q", 1), ("k", 1)),
    (1, 3): (("q", 2), ("k", 2)), (2, 1): (("q", 3), ("k", 3)),
    (2, 3): (("v", 0), ("v", 1)), (3, 2): (("v", 2), ("v", 3)),
}


def attention_block(nc, x, cond_t, w_emb, b_emb, g_norm, w_qkv, g_q, g_k, h_rows, o_parts, out):
    with ExitStack() as ctx:
        def sb(name, shape, dt=F32):
            return ctx.enter_context(nc.sbuf_tensor(name, shape, dt))

        def sem(name):
            return ctx.enter_context(nc.semaphore(name))

        ps = ctx.enter_context(nc.psum_tensor("ps", [P, 8, S], F32))

        wqkv = sb("wqkv", [P, 2, KT, 3 * D], F32R)
        xn = sb("xn", [P, 2, KT, S], F32R)
        x_nat = sb("x_nat", [P, 2, D])
        xtmp = sb("xtmp", [P, 2, KT, P])
        sq = sb("sq", [P, 2, D])
        qk = sb("qk", [P, 2, TT, 2 * D])
        v = sb("v", [P, TT, D])
        v_next = sb("v_next", [P, TT, D])
        parts = sb("parts", [P, 2, 2, 2, TT, SR], F32R)
        q_st = sb("q_st", [P, 2, HG, S], F32R)
        k_st = sb("k_st", [P, 2, HG, S], F32R)
        p_sb = sb("p_sb", [P, 2, HG, S])
        o_t = sb("o_t", [P, 2, S])
        o_n = sb("o_n", [P, S])
        ident = sb("ident", [P, P])
        ones = sb("ones", [P, DH])
        ab = sb("ab", [P, 2, KT, B])
        condt = sb("condt", [P, KT, B])
        bemb = sb("bemb", [P, 2 * KT])
        gn = sb("gn", [P, KT])
        gqk = sb("gqk", [P, 2, DH])
        grow = sb("grow", [P, DH])
        sx = sb("sx", [P, 2, 4])
        sh = sb("sh", [P, 2, 4, HEADS])
        mx = sb("mx", [P, 2, HG * TT])
        nm = sb("nm", [HG * TT, 2, P], F32R)
        w_raw = [p_sb[:, 0, 0:3, :], p_sb[:, 1, 0:3, :]]
        w_emb_sb = qk[:, 1]

        rows_out = sem("rows_out")
        const_in = sem("const_in")
        wemb_in = sem("wemb_in")
        wraw_in = [sem("wraw_in0"), sem("wraw_in1")]
        ident0 = sem("ident0")
        pool_const = sem("pool_const")
        pool_settled = sem("pool_settled")
        act_settled = sem("act_settled")
        w_hi = sem("w_hi")
        w_lo = sem("w_lo")
        emb_mm = sem("emb_mm")
        ab_ready = sem("ab_ready")
        ones_ready = sem("ones_ready")
        grow_ready = sem("grow_ready")
        x_in = [sem("x_in0"), sem("x_in1")]
        ssx_ready = sem("ssx_ready")
        vx_ready = sem("vx_ready")
        gx_ready = sem("gx_ready")
        nx_ready = sem("nx_ready")
        xs_ready = sem("xs_ready")
        xt_ready = sem("xt_ready")
        xtmp_ready = sem("xtmp_ready")
        xh_ready = sem("xh_ready")
        xl_ready = sem("xl_ready")
        chunk_ready = sem("chunk_ready")
        sq_ready = sem("sq_ready")
        ss_ready = sem("ss_ready")
        vv_ready = sem("vv_ready")
        gr_ready = sem("gr_ready")
        nr_ready = sem("nr_ready")
        qk_ready = sem("qk_ready")
        qg_ready = sem("qg_ready")
        v_ready = sem("v_ready")
        v_moved = sem("v_moved")
        part_hi = sem("part_hi")
        part_lo = sem("part_lo")
        t_ready = sem("t_ready")
        stack_ready = sem("stack_ready")
        m_ready = sem("m_ready")
        max_ready = sem("max_ready")
        maxt_ready = sem("maxt_ready")
        nmhi_ready = sem("nmhi_ready")
        nm_ready = sem("nm_ready")
        nm_in = sem("nm_in")
        st_ready = sem("st_ready")
        exp_ready = sem("exp_ready")
        pv_ready = sem("pv_ready")
        guess_ready = sem("guess_ready")
        newton_ready = sem("newton_ready")
        norm_ready = sem("norm_ready")
        o_out = [sem("o_out0"), sem("o_out1")]

        PAIRS = HEADS // 2

        def pairs_ahead(g, s, last):
            n = 2 * (g + 2) + s - 2
            return [n] if s >= 2 and (n < PAIRS or not last) else []

        x_tiles = x.rearrange("(b t p) h -> b t p h", b=B, p=P)
        block = ctx.enter_context(nc.Block())

        def wait(eng, s, value):
            if not isinstance(value, int) or value > 0:
                eng.wait_ge(s, value)

        def part(n, r, c):
            return parts[:, n % 2, r, :, :, c * DH:(c + 1) * DH].rearrange("p h t d -> p t h d")

        def heads_of(b, n, r):
            half = (b + n // (HEADS // 2)) % 2
            n = n % (HEADS // 2)
            cols = slice(r * D + 2 * n * DH, r * D + 2 * (n + 1) * DH)
            if isinstance(half, int):
                a = qk[:, half, :, cols]
            else:
                a = qk[:, bass.ds(half, 1), :, cols].rearrange("p o t n -> p (o t) n")
            return a.rearrange("p t (h d) -> p t h d", d=DH)


        TURN = [(g, s) for g in range(NG) for s in range(TT)][1:] + [(NG, 0)]
        AHEAD = [(-1, s) for s in range(TT)] + [(0, 0)]

        @block.sync
        def _(sp):
            sp.dma_start(condt[:], cond_t).then_inc(const_in, 16)
            sp.dma_start(bemb[:], b_emb).then_inc(const_in, 16)
            sp.dma_start(gn[:], g_norm).then_inc(const_in, 16)
            sp.dma_start(gqk[:, 0], g_q.broadcast_to([P, DH])).then_inc(const_in, 16)
            sp.dma_start(gqk[:, 1], g_k.broadcast_to([P, DH])).then_inc(const_in, 16)
            sp.dma_start(x_nat[:, 0], x_tiles[0, 0]).then_inc(x_in[0], 16)
            sp.dma_start(x_nat[:, 1], x_tiles[0, 1]).then_inc(x_in[1], 16)
            sp.dma_start(w_emb_sb, w_emb).then_inc(wemb_in, 16)
            sp.dma_start(w_raw[0], w_qkv[:, 0]).then_inc(wraw_in[0], 16)
            sp.dma_start(w_raw[1], w_qkv[:, 1]).then_inc(wraw_in[1], 16)
            for credit in o_out:
                sp.sem_inc(credit, CREDIT)

            def load_x(b, t):
                wait(sp, xt_ready, b * TT + t - 1)
                sp.dma_start(x_nat[:, t % 2], x_tiles[b, t]).then_inc(x_in[t % 2], 16)

            def max_rows(b, g):
                sp.wait_ge(nm_ready, b * NG + g + 1)
                for which in range(2):
                    row = SR + which
                    sp.dma_start(
                        q_st[row:row + 1, g % 2].rearrange("o h (t q) -> o (h t) q", q=P).bitcast(F32),
                        nm[:, which, :].bitcast(F32)).then_inc(nm_in, 16)

            def store_o(b, g):
                sp.wait_ge(norm_ready, b * NG + g + 2)
                sp.dma_start(o_parts[b, g], o_t[:, g % 2]).then_inc(o_out[g % 2], 16)

            for t in range(2, TT):
                load_x(0, t)
                sp.wait_ge(w_lo, t - 1)
                sp.dma_start(w_raw[t % 2], w_qkv[:, t]).then_inc(wraw_in[t % 2], 16)
            sp.dma_start(out[0:B * S], x).then_inc(rows_out, 16)
            sp.dma_start(out[B * S:B * S + P], x[0:P]).then_inc(rows_out, 16)
            sp.dma_start(h_rows[B * S:B * S + P], x[0:P]).then_inc(rows_out, 16)
            max_rows(0, 0)

            def turn(b, last):
                if not last:
                    for t in range(TT):
                        load_x(b + 1, t)
                for g in range(NG):
                    if g + 1 < NG or not last:
                        max_rows(b, g + 1)
                    store_o(b, g)

            with sp.Fori(0, B - 1) as b:
                turn(b, False)
            turn(B - 1, True)
            for slot in range(2):
                sp.wait_ge(o_out[slot], CREDIT + 16 * B * NG // 2)
            sp.wait_ge(rows_out, 48)

        @block.gpsimd
        def _(pool):
            nc.gpsimd.memset(ident[:], 0.0).then_inc(ident0, 1)
            pool.wait_ge(ident0, 1)
            nc.gpsimd.affine_select(out=ident[:], in_=ident[:], compare_op=ALU.not_equal, fill=1.0, base=0,
                                    pattern=[[-1, P]], channel_multiplier=1).then_inc(pool_const, 1)
            nc.gpsimd.memset(ones[:], 1.0).then_inc(pool_const, 1)

            def part_high(b, n):
                if n % PAIRS == 0:
                    pool.wait_ge(qg_ready, b * TT + TT * (1 + n // PAIRS))
                    pool.wait_ge(qk_ready, b * (2 * TT) + 2 * TT * (1 + n // PAIRS))
                wait(pool, t_ready, b * HEADS + 2 * (n - 1))
                pool.sem_inc(pool_settled, 1)
                for r, c in ((0, 0), (1, 0), (0, 2), (1, 1)):
                    nc.gpsimd.tensor_copy(part(n, r, c), heads_of(b, n, r)).then_inc(part_hi, 1)

            for n in range(2):
                part_high(0, n)
            for g, s in AHEAD:
                for n in pairs_ahead(g, s, False):
                    part_high(0, n)

            def turn(b, last):
                for g, s in TURN:
                    for n in pairs_ahead(g, s, last):
                        part_high(b, n)

            with pool.Fori(0, B - 1) as b:
                turn(b, False)
            turn(B - 1, True)

        @block.scalar
        def _(act):
            def column(a, b):
                return a[:, b:b + 1] if isinstance(b, int) else a[:, bass.ds(b, 1)]

            def tile_guess(b, t):
                i = t % 2
                act.wait_ge(x_in[i], b * (8 * TT) + 16 * (t // 2 + 1))
                wait(act, ssx_ready, b * TT + t - 1)
                if t < 2:
                    wait(act, ss_ready, b * (2 * TT))
                wait(act, xs_ready, b * TT + t - 1)
                nc.scalar.activation(sq[:, i], x_nat[:, i], ACT.Square,
                                     accum_out=sx[:, i, 0:1]).then_inc(ssx_ready, 1)
                act.wait_ge(vx_ready, b * TT + t + 1)
                nc.scalar.activation(sx[:, i, 2:3], sx[:, i, 1:2], ACT.Ln).then_inc(gx_ready, 1)
                act.wait_ge(gx_ready, b * (2 * TT) + 2 * t + 1)
                nc.scalar.activation(sx[:, i, 2:3], sx[:, i, 2:3], ACT.Exp, scale=-0.5).then_inc(gx_ready, 1)

            def tile_out(b, t):
                act.wait_ge(xt_ready, b * TT + t + 1)
                wait(act, xl_ready, b * TT + t - 1)
                act.sem_inc(act_settled, 1)
                for j in range(KT):
                    ins = nc.scalar.activation(xtmp[:, t % 2, j], ps[:, t % 2, j * P:(j + 1) * P], ACT.Identity,
                                               bias=column(ab[:, 1, j], b), scale=column(ab[:, 0, j], b))
                ins.then_inc(xtmp_ready, 1)

            def chunk_out(b, kind, t):
                if kind == "v":
                    act.wait_ge(chunk_ready, b * (3 * TT) + 2 * TT + t + 1)
                    wait(act, v_moved, b + 0)
                    nc.scalar.copy(v_next[:, t], ps[:, t % 2]).then_inc(v_ready, 1)
                    return
                r = "qk".index(kind)
                n = 2 * t + r
                act.wait_ge(chunk_ready, b * (3 * TT) + n + 1)
                if n < 2:
                    act.wait_ge(ssx_ready, b * TT + TT)
                else:
                    act.wait_ge(ss_ready, b * (2 * TT) + n - 1)
                nc.scalar.activation(sq[:, r], ps[:, r], ACT.Square).then_inc(sq_ready, 1)
                act.wait_ge(vv_ready, b * (2 * TT) + n + 1)
                nc.scalar.activation(sh[:, r, 2], sh[:, r, 1], ACT.Ln).then_inc(gr_ready, 1)
                act.wait_ge(gr_ready, b * (4 * TT) + 2 * n + 1)
                nc.scalar.activation(sh[:, r, 2], sh[:, r, 2], ACT.Exp, scale=-0.5).then_inc(gr_ready, 1)

            def stack(b, n):
                act.wait_ge(t_ready, b * HEADS + n + 1)
                for r in range(2):
                    nc.scalar.copy((q_st, k_st)[r][0:SR, n // HG % 2, n % HG], ps[0:SR, r]).then_inc(stack_ready, 1)

            def exps(b, g, kt, pair):
                act.wait_ge(st_ready, b * (NG * TT * 2) + (TT * g + kt) * 2 + pair + 1)
                act.wait_ge(pv_ready, b * (NG * TT) + TT * g + kt + 1)
                nc.scalar.activation(p_sb[:, kt % 2, 2 * pair:2 * pair + 2], ps[:, 4:6],
                                     ACT.Exp).then_inc(exp_ready, 1)

            def sums_guess(b, g):
                act.wait_ge(pv_ready, b * (NG * TT) + TT * (g + 1) + 2)
                act.wait_ge(o_out[g % 2], b * (8 * NG) + 16 * (g // 2) + CREDIT)
                nc.scalar.activation(o_t[:, g % 2], ps[:, 7], ACT.Ln).then_inc(guess_ready, 1)
                act.wait_ge(guess_ready, b * (2 * NG) + 2 * g + 1)
                nc.scalar.activation(o_t[:, g % 2], o_t[:, g % 2], ACT.Exp, scale=-1.0).then_inc(guess_ready, 1)

            def weight_high(n):
                act.wait_ge(wraw_in[n % 2], 16 * (n // 2 + 1))
                nc.scalar.copy(wqkv[:, 0, n], w_raw[n % 2].rearrange("p k n -> p (k n)")).then_inc(w_hi, 1)

            def step(b, g, s, last):
                stacks = s < 2 and (not last or g + 1 < NG)
                if stacks:
                    stack(b, HG * (g + 1) + 2 * s)
                if g >= 0:
                    exps(b, g, s, 0)
                if stacks:
                    stack(b, HG * (g + 1) + 2 * s + 1)
                slots = () if last else SLOTS.get((g, s), ())
                for kind, t in slots:
                    if kind == "x":
                        tile_guess(b + 1, t)
                for kind, t in slots:
                    if kind == "x":
                        tile_out(b + 1, t)
                    else:
                        chunk_out(b + 1, kind, t)
                if g >= 0:
                    exps(b, g, s, 1)
                if s == 0 and g >= 1:
                    sums_guess(b, g - 1)

            nc.scalar.add_instruction(mybir.InstLoadActFuncSet(
                name=nc.get_next_instruction_name(), act_func_set_id=LN_EXP, engine=mybir.EngineType.Activation))
            act.wait_ge(ab_ready, 2)
            for t in range(TT):
                tile_guess(0, t)
                tile_out(0, t)
                weight_high(t)
            for t in range(TT):
                chunk_out(0, "q", t)
                chunk_out(0, "k", t)
            for t in range(TT):
                chunk_out(0, "v", t)
            for g, s in AHEAD:
                step(0, g, s, False)

            def turn(b, last):
                for g, s in TURN:
                    if not last or g < NG:
                        step(b, g, s, last)
                if last:
                    sums_guess(b, NG - 1)

            with act.Fori(0, B - 1) as b:
                turn(b, False)
            turn(B - 1, True)

        @block.tensor
        def _(pe):
            pe.wait_ge(const_in, 16 * 5)
            pe.wait_ge(wemb_in, 16)
            for m in range(2 * KT):
                for k in range(KT):
                    ins = pe.matmul(ps[:, 0, m * B:(m + 1) * B], w_emb_sb[:, k, m * P:(m + 1) * P],
                                    condt[:, k], start=(k == 0), stop=(k == KT - 1))
            ins.then_inc(emb_mm, 1)
            pe.wait_ge(pool_const, 2)
            pe.wait_ge(ab_ready, 2)
            pe.wait_ge(ones_ready, 1)
            pe.sem_inc(pv_ready, 2)

            def slot_left(b, kind, t):
                if kind == "x":
                    pe.wait_ge(xtmp_ready, b * TT + t + 1)
                elif kind == "v":
                    pe.wait_ge(v_ready, b * TT + t + 1)
                else:
                    pe.wait_ge(qk_ready, b * (2 * TT) + 2 * t + "qk".index(kind) + 1)

            def stacked(b, g, i):
                pe.wait_ge(stack_ready, b * (2 * HEADS) + 2 * (HG * g + i) + 2)

            def banks_left(b, g, s, last):
                slots = () if last else SLOTS.get((g, s), ())
                for kind, t in slots:
                    slot_left(b + 1, kind, t)
                if s < 2 and not slots:
                    stacked(b, g + 1, 2 * s + 1)
                if s == 3 and not slots:
                    banks_left(b, g, 2, last)
                if s == 2:
                    if not slots:
                        banks_left(b, g, 1, last)
                    pe.wait_ge(nm_ready, b * NG + g + 2)

            def slot(b, kind, t):
                bank = t % 2 if kind in "xv" else "qk".index(kind)
                if kind == "x":
                    pe.wait_ge(xs_ready, b * TT + t + 1)
                    for j in range(KT):
                        ins = pe.transpose(ps[:, bank, j * P:(j + 1) * P], x_nat[:, t % 2, j * P:(j + 1) * P], ident[:])
                    ins.then_inc(xt_ready, 1)
                    return
                pe.wait_ge(xl_ready, b * TT + t + 1)
                c = "qkv".index(kind)
                n = 0
                for j in range(KT):
                    for xpart, wpart in ((0, 0), (0, 1), (1, 0)):
                        ins = pe.matmul(ps[:, bank], xn[:, xpart, j, t * P:(t + 1) * P],
                                        wqkv[:, wpart, j, c * D:(c + 1) * D], start=(n == 0), stop=(n == 3 * KT - 1))
                        n += 1
                ins.then_inc(chunk_ready, 1)

            def transposes(b, n):
                pe.wait_ge(part_lo, b * HEADS + 2 * (n // 2) + 2)
                for r in range(2):
                    for t in range(TT):
                        ins = pe.transpose(ps[0:SR, r, t * P:(t + 1) * P],
                                           parts[:, n // 2 % 2, r, n % 2, t].bitcast(F32), ident[:])
                ins.then_inc(t_ready, 1)

            def max_scores(b, g, i):
                h, t = divmod(i, TT)
                n = HG * TT * g + i
                stacked(b, g, h)
                wait(pe, max_ready, b * (HEADS * TT) + n - 1)
                pe.matmul(ps[:, 2 + i % 2], q_st[0:SR, g % 2, h, t * P:(t + 1) * P],
                          k_st[0:SR, g % 2, h], start=True, stop=True).then_inc(m_ready, 1)

            def max_rows(b, g):
                pe.wait_ge(max_ready, b * (HEADS * TT) + HG * TT * (g + 1))
                pe.transpose(ps[0:HG * TT, 0, 0:P], mx[:, g % 2], ident[:]).then_inc(maxt_ready, 1)

            def scores(b, g, kt, pair):
                n = (TT * g + kt) * 2 + pair
                if kt == 0 and pair == 0:
                    pe.wait_ge(nm_in, b * (NG * 32) + 32 * (g + 1))
                wait(pe, exp_ready, b * (NG * TT * 2) + n)
                for i in range(2):
                    h = 2 * pair + i
                    ins = pe.matmul(ps[:, 4 + i], k_st[0:SR + 2, g % 2, h, kt * P:(kt + 1) * P],
                                    q_st[0:SR + 2, g % 2, h], start=True, stop=True)
                ins.then_inc(st_ready, 1)

            def products(b, g, kt, what):
                if what == 0:
                    pe.wait_ge(exp_ready, b * (NG * TT * 2) + (TT * g + kt) * 2 + 2)
                    if kt == 0:
                        pe.wait_ge(norm_ready, b * NG + g + 1)
                        if g % NG == 0:
                            pe.wait_ge(v_moved, b + g // NG + 1)
                for h in range(HG):
                    col = (HG * (g % NG) + h) * DH
                    w = v[:, kt, col:col + DH] if what == 0 else ones[:]
                    ins = pe.matmul(ps[h * DH:(h + 1) * DH, 6 + what], w, p_sb[:, kt % 2, h],
                                    start=(kt == 0), stop=(kt == TT - 1))
                if what == 1:
                    ins.then_inc(pv_ready, 1)

            def step(b, g, s, last):
                stacks = s < 2 and (not last or g + 1 < NG)
                slots = () if last else SLOTS.get((g, s), ())
                maxima = list(range(M_FIRST[s], M_FIRST[s + 1])) if not last or g + 1 < NG else []
                if stacks:
                    if (g, s) == (-1, 0):
                        pe.wait_ge(v_ready, TT)
                    else:
                        banks_left(b, g + (s - 1) // TT, (s - 1) % TT, last)
                    transposes(b, HG * (g + 1) + 2 * s)
                if g >= 0:
                    scores(b, g, s, 0)

                def some_maxima(most):
                    for _ in range(min(most, len(maxima))):
                        max_scores(b, g + 1, maxima.pop(0))

                if s == 1:
                    some_maxima(2)
                if stacks:
                    stacked(b, g + 1, 2 * s)
                    transposes(b, HG * (g + 1) + 2 * s + 1)
                if slots:
                    if s == 1:
                        stacked(b, g + 1, 2 * s + 1)
                    else:
                        banks_left(b, g, s - 1, last)
                    slot(b + 1, *slots[0])
                if s == 2:
                    some_maxima(2)
                if slots:
                    slot(b + 1, *slots[1])
                before = divmod(TT * g + s - 1, TT)
                if before[0] >= 0:
                    products(b, *before, 0)
                    some_maxima(2)
                    products(b, *before, 1)
                some_maxima(2)
                if g >= 0:
                    scores(b, g, s, 1)
                some_maxima(len(maxima))
                if s == 2 and (not last or g + 1 < NG):
                    if slots:
                        slot_left(b + 1, *slots[0])
                    else:
                        banks_left(b, g, s - 1, last)
                    max_rows(b, g + 1)

            for t in range(TT):
                if t >= 2:
                    slot_left(0, "x", t - 2)
                slot(0, "x", t)
            slot_left(0, "x", TT - 1)
            for t in range(TT):
                pe.wait_ge(w_lo, KT)
                for r in range(2):
                    if t >= 1:
                        slot_left(0, "qk"[r], t - 1)
                    slot(0, "qk"[r], t)
            slot_left(0, "k", TT - 1)
            for t in range(TT):
                if t >= 2:
                    slot_left(0, "v", t - 2)
                slot(0, "v", t)
            for g, s in AHEAD:
                step(0, g, s, False)

            def turn(b, last):
                for g, s in TURN:
                    if not last or g < NG:
                        step(b, g, s, last)
                if last:
                    products(b, NG - 1, TT - 1, 0)
                    products(b, NG - 1, TT - 1, 1)

            with pe.Fori(0, B - 1) as b:
                turn(b, False)
            turn(B - 1, True)

        @block.vector
        def _(dve):
            nc.vector.memset(k_st[SR:SR + DH].bitcast(F32), 1.0).then_inc(ones_ready, 1)
            dve.wait_ge(const_in, 16 * 5)
            nc.vector.scalar_tensor_tensor(out=grow[:], in0=gqk[:, 0], scalar=float(DH) ** -0.5,
                                           in1=gqk[:, 1], op0=ALU.mult, op1=ALU.mult).then_inc(grow_ready, 1)
            dve.wait_ge(emb_mm, 1)
            sv = ps[:, 0, 0:2 * KT * B].rearrange("p (m b) -> p m b", b=B)
            bb = bemb[:].rearrange("p (m o) -> p m o", o=1).broadcast_to([P, 2 * KT, B])
            dve.wait_ge(grow_ready, 1)
            nc.vector.tensor_tensor(ab[:].rearrange("p a k b -> p (a k) b"), sv, bb, ALU.add).then_inc(ab_ready, 1)
            dve.wait_ge(ab_ready, 1)
            nc.vector.scalar_tensor_tensor(out=ab[:, 0], in0=ab[:, 0], scalar=1.0,
                                           in1=gn[:].rearrange("p (k o) -> p k o", o=1).broadcast_to([P, KT, B]),
                                           op0=ALU.add, op1=ALU.mult).then_inc(ab_ready, 1)
            dve.sem_inc(norm_ready, 1)

            def tile_norm(b, t):
                i = t % 2
                v_, y_, f_ = sx[:, i, 1:2], sx[:, i, 2:3], sx[:, i, 3:4]
                dve.wait_ge(ssx_ready, b * TT + t + 1)
                nc.vector.tensor_scalar(v_, sx[:, i, 0:1], 1.0 / D, EPS, ALU.mult, ALU.add).then_inc(vx_ready, 1)
                dve.wait_ge(gx_ready, b * (2 * TT) + 2 * t + 2)
                nc.vector.tensor_scalar(f_, y_, y_, v_, ALU.mult, ALU.mult).then_inc(nx_ready, 1)
                dve.wait_ge(nx_ready, b * (2 * TT) + 2 * t + 1)
                nc.vector.tensor_scalar(f_, f_, -0.5, 1.5, ALU.mult, ALU.add).then_inc(nx_ready, 1)
                dve.wait_ge(nx_ready, b * (2 * TT) + 2 * t + 2)
                nc.vector.tensor_scalar(x_nat[:, i], x_nat[:, i], f_, y_, ALU.mult, ALU.mult).then_inc(xs_ready, 1)

            def tile_split(b, t):
                dve.wait_ge(xtmp_ready, b * TT + t + 1)
                cols = slice(t * P, (t + 1) * P)
                nc.vector.tensor_copy(xn[:, 0, :, cols], xtmp[:, t % 2]).then_inc(xh_ready, 1)
                dve.wait_ge(xh_ready, b * TT + t + 1)
                nc.vector.tensor_tensor(xn[:, 1, :, cols], xtmp[:, t % 2], xn[:, 0, :, cols].bitcast(F32),
                                        ALU.subtract).then_inc(xl_ready, 1)

            def head_sums(b, kind, t):
                r = "qk".index(kind)
                n = 2 * t + r
                dve.wait_ge(sq_ready, b * (2 * TT) + n + 1)
                nc.vector.tensor_reduce(sh[:, r, 0], sq[:, r].rearrange("p (h d) -> p h d", d=DH),
                                        AX.X, ALU.add).then_inc(ss_ready, 1)
                dve.wait_ge(ss_ready, b * (2 * TT) + n + 1)
                nc.vector.tensor_scalar(sh[:, r, 1], sh[:, r, 0], 1.0 / DH, EPS, ALU.mult, ALU.add).then_inc(vv_ready, 1)

            def head_norms(b, kind, t):
                r = "qk".index(kind)
                n = 2 * t + r
                v_, y_, f_ = sh[:, r, 1], sh[:, r, 2], sh[:, r, 3]
                dve.wait_ge(gr_ready, b * (4 * TT) + 2 * n + 2)
                nc.vector.tensor_tensor(f_, y_, y_, ALU.mult).then_inc(nr_ready, 1)
                dve.wait_ge(nr_ready, b * (6 * TT) + 3 * n + 1)
                nc.vector.scalar_tensor_tensor(out=f_, in0=f_, scalar=-0.5, in1=v_, op0=ALU.mult,
                                               op1=ALU.mult).then_inc(nr_ready, 1)
                dve.wait_ge(nr_ready, b * (6 * TT) + 3 * n + 2)
                nc.vector.scalar_tensor_tensor(out=f_, in0=f_, scalar=1.5, in1=y_, op0=ALU.add,
                                               op1=ALU.mult).then_inc(nr_ready, 1)
                dve.wait_ge(nr_ready, b * (6 * TT) + 3 * n + 3)
                half = b % 2
                a = qk[:, half, t] if isinstance(half, int) else qk[:, bass.ds(half, 1), t].rearrange("p o n -> p (o n)")
                a = a[:, r * D:(r + 1) * D].rearrange("p (h d) -> p h d", d=DH)
                nc.vector.tensor_tensor(
                    a, ps[:, r].rearrange("p (h d) -> p h d", d=DH),
                    f_.rearrange("p (h o) -> p h o", o=1).broadcast_to([P, HEADS, DH]), ALU.mult).then_inc(qk_ready, 1)
                if r == 0:
                    dve.wait_ge(qk_ready, b * (2 * TT) + n + 1)
                    nc.vector.tensor_tensor(
                        a, a, grow[:].rearrange("p (o d) -> p o d", o=1).broadcast_to([P, HEADS, DH]),
                        ALU.mult).then_inc(qg_ready, 1)

            def part_low(b, n):
                dve.wait_ge(part_hi, b * (2 * HEADS) + 4 * (n + 1))
                for r, c in ((0, 1), (1, 2)):
                    nc.vector.tensor_tensor(part(n, r, c), heads_of(b, n, r), part(n, r, 0).bitcast(F32),
                                            ALU.subtract).then_inc(part_lo, 1)

            def maximum(b, g, i):
                dve.wait_ge(m_ready, b * (HEADS * TT) + HG * TT * g + i + 1)
                nc.vector.tensor_reduce(mx[:, g % 2, i:i + 1], ps[:, 2 + i % 2], AX.X,
                                        ALU.max).then_inc(max_ready, 1)

            def minus_max(b, g):
                dve.wait_ge(maxt_ready, b * NG + g + 1)
                wait(dve, nm_in, b * (NG * 32) + 32 * g)
                rows = ps[0:HG * TT, 0, 0:P]
                nc.vector.tensor_scalar(nm[:, 0], rows, -1.0, None, ALU.mult).then_inc(nmhi_ready, 1)
                dve.wait_ge(nmhi_ready, b * NG + g + 1)
                nc.vector.scalar_tensor_tensor(out=nm[:, 1], in0=rows, scalar=-1.0,
                                               in1=nm[:, 0].bitcast(F32), op0=ALU.mult,
                                               op1=ALU.subtract).then_inc(nm_ready, 1)

            def move_v(b):
                dve.wait_ge(v_ready, b * TT + TT)
                dve.wait_ge(pv_ready, b * (NG * TT) + 2)
                nc.vector.tensor_copy(v[:], v_next[:]).then_inc(v_moved, 1)

            def normalise(b, g):
                y_ = o_t[:, g % 2]
                dve.wait_ge(guess_ready, b * (2 * NG) + 2 * g + 2)
                nc.vector.tensor_tensor(o_n[:], ps[:, 7], y_, ALU.mult).then_inc(newton_ready, 1)
                dve.wait_ge(newton_ready, b * (2 * NG) + 2 * g + 1)
                nc.vector.scalar_tensor_tensor(out=o_n[:], in0=o_n[:], scalar=-2.0, in1=y_, op0=ALU.add,
                                               op1=ALU.mult).then_inc(newton_ready, 1)
                dve.wait_ge(newton_ready, b * (2 * NG) + 2 * g + 2)
                nc.vector.scalar_tensor_tensor(out=y_, in0=ps[:, 6], scalar=-1.0, in1=o_n[:], op0=ALU.mult,
                                               op1=ALU.mult).then_inc(norm_ready, 1)

            def weight_low(n):
                dve.wait_ge(w_hi, n + 1)
                nc.vector.tensor_tensor(wqkv[:, 1, n], w_raw[n % 2].rearrange("p k n -> p (k n)"),
                                        wqkv[:, 0, n].bitcast(F32), ALU.subtract).then_inc(w_lo, 1)

            def step(b, g, s, last):
                slots = () if last else SLOTS.get((g, s), ())
                maxima = list(range(M_FIRST[s], M_FIRST[s + 1])) if not last or g + 1 < NG else []
                if slots and slots[0][0] == "x":
                    for kind, t in slots:
                        tile_norm(b + 1, t)
                elif slots and slots[0][0] == "q":
                    head_sums(b + 1, *slots[0])
                for i in maxima[:2]:
                    maximum(b, g + 1, i)
                if slots and slots[0][0] == "q":
                    head_norms(b + 1, *slots[0])
                    head_sums(b + 1, *slots[1])
                    head_norms(b + 1, *slots[1])
                for n in pairs_ahead(g, s, last):
                    part_low(b, n)
                for i in maxima[2:]:
                    maximum(b, g + 1, i)
                if slots and slots[0][0] == "x":
                    for kind, t in slots:
                        tile_split(b + 1, t)
                if s == 2 and maxima:
                    minus_max(b, g + 1)
                if s == 0 and g >= 1:
                    normalise(b, g - 1)
                if s == 0 and g % NG == 0:
                    move_v(b + g // NG)

            for t in range(TT):
                tile_norm(0, t)
                tile_split(0, t)
                weight_low(t)
            for t in range(TT):
                for kind in "qk":
                    head_sums(0, kind, t)
                    head_norms(0, kind, t)
            for n in range(2):
                part_low(0, n)
            for g, s in AHEAD:
                step(0, g, s, False)

            def turn(b, last):
                for g, s in TURN:
                    if not last or g < NG:
                        step(b, g, s, last)
                if last:
                    normalise(b, NG - 1)

            with dve.Fori(0, B - 1) as b:
                turn(b, False)
            turn(B - 1, True)


E_N = 8
I_W = 352
IC = -(-I_W // P)
I_REST = I_W - (IC - 1) * P
TOP = 2
TOK_TILES = B * S // P
SLOT_TILES = (B * S * TOP + E_N * (P - 1)) // P + 1
TILES = TOK_TILES + SLOT_TILES
SHARED = E_N
HOT = 4
PICK_AT, COUNT_AT, WEIGH_AT, PLACE_AT, SLOT_AT, TABLE_AT = 0, 1, 2, 3, 4, 5
TABLE_TILES = TOP * TOK_TILES // (2 * HOT)
FINISH_AT = TABLE_AT + TABLE_TILES
LOOP_FROM = FINISH_AT + 2
assert (TOK_TILES - 1 - LOOP_FROM) % 2 == 0 and (TILES - 3 - LOOP_FROM) % 2 == 0


def ffn_block(nc, o_parts, w_out, h_rows, gate_t, w_gu, w_down, out):
    assert TILES % 2 == 0
    with ExitStack() as ctx:
        def sb(name, shape, dt=F32):
            return ctx.enter_context(nc.sbuf_tensor(name, shape, dt))

        def sem(name):
            return ctx.enter_context(nc.semaphore(name))

        I32 = mybir.dt.int32
        U32 = mybir.dt.uint32
        ps = ctx.enter_context(nc.psum_tensor("ps2", [P, 8, 512], F32))

        wgu = sb("wgu", [P, E_N + 1, KT, 2 * I_W])
        wdn = sb("wdn", [P, E_N + 1, IC, D])
        gate = sb("gate", [P, KT, E_N])
        o_parts_sb = sb("o_parts_sb", [P, 2, 2, KT, P], F32R)
        wo = sb("wo", [P, 2, KT, D], F32R)
        wo_raw = wgu[:, E_N - 1].rearrange("p k n -> p (k n)")[:, 0:KT * D].rearrange("p (k n) -> p k n", k=KT)
        o_raw = wgu[:, E_N - 2].rearrange("p k n -> p (k n)")[:, 0:2 * D].rearrange("p (i k n) -> p i k n", i=2, k=KT)
        rows = sb("rows", [P, 2, D])
        rows_t = sb("rows_t", [P, 2, KT, P])
        act_g = sb("act_g", [P, 2, I_W])
        hid = sb("hid", [P, 2, I_W])
        hid_t = sb("hid_t", [P, 2, IC, P])
        y = sb("y", [P, 2, D])
        idx_g = sb("idx_g", [P, 2], U32)
        idx_s = sb("idx_s", [P, 2], U32)
        tab_tok = sb("tab_tok", [P, TILES], I32)
        tab_w = sb("tab_w", [P, TILES])
        tab_e = sb("tab_e", [1, TILES], I32)

        ident = sb("ident2", [P, P])
        ones = sb("ones2", [P, P])
        before = sb("before", [P, P])
        lane = sb("lane", [P, P])
        own = sb("own", [P, 1])
        token = sb("token", [P, TOK_TILES])
        logits = sb("logits", [P, TOK_TILES, E_N])
        top = sb("top", [P, TOK_TILES, 8])
        top_i = sb("top_i", [P, TOK_TILES, 8], U32)
        pick = sb("pick", [P, TOP, TOK_TILES])
        hot = sb("hot", [P, TOP, TOK_TILES, E_N])
        both = sb("both", [P, TOK_TILES, E_N])
        wts = sb("wts", [P, TOP, TOK_TILES])
        ex = sb("ex", [P, 2, TOK_TILES])
        tot = sb("tot", [P, E_N, TOK_TILES])
        run = sb("run", [P, E_N, TOK_TILES])
        carry = sb("carry", [P, E_N, TOK_TILES])
        cnt_i = sb("cnt_i", [P, E_N], I32)
        cnt = sb("cnt", [P, E_N])
        ends = sb("ends", [P, E_N])
        base = sb("base", [P, E_N])
        pos = sb("pos", [P, TOK_TILES, E_N])
        slot = sb("slot", [P, TOP * TOK_TILES])
        slot_i = sb("slot_i", [P, 3, TOP * TOK_TILES], I32)
        slot_p = sb("slot_p", [P, TOP * TOK_TILES])
        slot_j = sb("slot_j", [P, TOP * TOK_TILES])
        last_w = wdn[:, E_N - 1].rearrange("p c n -> p (c n)")
        hot_p = last_w[:, 0:HOT * P].rearrange("p (i n) -> p i n", i=HOT)
        hot_j = last_w[:, HOT * P:HOT * (P + 2 * SLOT_TILES)].rearrange("p (i a j) -> p i a j", i=HOT, a=2)
        late = last_w[0:1, HOT * (P + 2 * SLOT_TILES):][:, 0:SLOT_TILES * E_N].rearrange("p (j e) -> p j e", e=E_N)
        sel = last_w[:, IC * D - TOP * TOK_TILES * E_N:].rearrange("p (c t e) -> p c t e", c=TOP, e=E_N)
        tile_e = sb("tile_e", [1, SLOT_TILES])
        empty = sb("empty", [P, SLOT_TILES])
        tok_f = sb("tok_f", [P, SLOT_TILES])

        names = ("gate_in shared_in experts_in pool_ready ident_ready wo_in wo_one wo_hi wo_lo o_in0 o_in1 "
                 "o_hi o_lo h_mm h_ready h_out0 h_out1 "
                 "logit_t logit_evac logit_mm logit_out r exp_done count_mm hot_done tab_mm "
                 "idx_ready rows_in0 rows_in1 rows_t_mm rows_t_out gate_mm up_mm silu_done hid_done "
                 "hid_t_mm hid_t_out down_mm y_ready y_out pool_settled").split()
        s = {n: sem(n + "_f") for n in names}
        rows_in = (s["rows_in0"], s["rows_in1"])
        block = ctx.enter_context(nc.Block())
        C = 2

        def at(n):
            return n + (C + 1)

        @block.sync
        def _(sp):
            sp.dma_start(gate[:], gate_t).then_inc(s["gate_in"], 16)
            sp.dma_start(wo_raw, w_out).then_inc(s["wo_in"], 16)

            def load_o(t):
                if t >= 2:
                    sp.wait_ge(s["o_lo"], t - 1)
                sp.dma_start(o_raw[:, t % 2], o_parts[t // TT].rearrange("g p n -> p g n")[:, :, t % TT * P:(t % TT + 1) * P]
                             ).then_inc(s[f"o_in{t % 2}"], 16)

            def store_h(t):
                sp.wait_ge(s["h_ready"], t + 1)
                sp.dma_start(h_rows[t * P:(t + 1) * P], rows[:, t % 2]).then_inc(s[f"h_out{t % 2}"], 16)

            def load_expert(e, name):
                sp.dma_start(wgu[:, e], w_gu[e]).then_inc(s[name], 16)
                sp.dma_start(wdn[:, e], w_down[e]).then_inc(s[name], 16)

            for t in range(TOK_TILES + 2):
                if t < TOK_TILES:
                    load_o(t)
                if t >= 2:
                    store_h(t - 2)
                if t == 4:
                    load_expert(SHARED, "shared_in")
                if t > 4 and t % 2 == 0 and t // 2 - 3 < E_N - 2:
                    load_expert(t // 2 - 3, "experts_in")
            sp.wait_ge(s["wo_lo"], KT)
            sp.wait_ge(s["o_lo"], TOK_TILES)
            load_expert(E_N - 2, "experts_in")
            sp.wait_ge(s["tab_mm"], TOP * TOK_TILES)
            load_expert(E_N - 1, "experts_in")

        @block.gpsimd
        def _(pool):
            nc.gpsimd.memset(ident[:], 0.0).then_inc(s["pool_ready"], 1)
            nc.gpsimd.memset(ones[:], 1.0).then_inc(s["pool_ready"], 1)
            pool.wait_ge(s["pool_ready"], 2)
            nc.gpsimd.affine_select(out=ident[:], in_=ident[:], compare_op=ALU.not_equal, fill=1.0, base=0,
                                    pattern=[[-1, P]], channel_multiplier=1).then_inc(s["ident_ready"], 1)
            nc.gpsimd.affine_select(out=before[:], in_=ones[:], compare_op=ALU.is_gt, fill=0.0, base=0,
                                    pattern=[[1, P]], channel_multiplier=-1).then_inc(s["pool_ready"], 1)
            nc.gpsimd.iota(lane[:], pattern=[[1, P]], base=0, channel_multiplier=0,
                           allow_small_or_imprecise_dtypes=True).then_inc(s["pool_ready"], 1)
            nc.gpsimd.iota(own[:], pattern=[[1, 1]], base=B * S + 1, channel_multiplier=1,
                           allow_small_or_imprecise_dtypes=True).then_inc(s["pool_ready"], 1)
            nc.gpsimd.iota(token[:], pattern=[[P, TOK_TILES]], base=1, channel_multiplier=1,
                           allow_small_or_imprecise_dtypes=True).then_inc(s["pool_ready"], 1)
            nc.gpsimd.iota(tab_tok[:, 0:TOK_TILES], pattern=[[P, TOK_TILES]], base=0,
                           channel_multiplier=1).then_inc(s["pool_ready"], 1)

            def gather(n, par):
                pool.wait_ge(s["idx_ready"], n + 1)
                pool.sem_inc(s["pool_settled"], 1)
                pool.indirect_dma_start(out=rows[:, par], out_offset=None, in_=h_rows,
                                        in_offset=bass.IndirectOffsetOnAxis(ap=idx_g[:, par:par + 1], axis=0),
                                        ).then_inc(rows_in[par], 16)

            def scatter(n, par):
                pool.wait_ge(s["y_ready"], at(n))
                if not isinstance(n, int) or n > 0:
                    pool.wait_ge(s["y_out"], 16 * n)
                pool.sem_inc(s["pool_settled"], 1)
                pool.indirect_dma_start(out=out, in_=y[:, par], in_offset=None,
                                        out_offset=bass.IndirectOffsetOnAxis(ap=idx_s[:, par:par + 1], axis=0),
                                        compute_op=ALU.add).then_inc(s["y_out"], 16)

            for i in range(2):
                pool.wait_ge(s[f"h_out{i}"], 16 * (TOK_TILES // 2))
            pool.wait_ge(s["logit_t"], TOK_TILES)
            gather(0, 0)
            gather(1, 1)
            gather(2, 0)
            for m in (1, 2):
                gather(m + 2, m % 2)
                scatter(m - 1, 1 - m % 2)
            with pool.Fori(0, (TILES - 6) // 2) as i:
                for u in range(2):
                    m = i * 2 + (3 + u)
                    gather(m + 2, (1 + u) % 2)
                    scatter(m - 1, u % 2)
            gather(TILES - 1, 1)
            for n in range(TILES - 4, TILES):
                scatter(n, n % 2)
            pool.wait_ge(s["y_out"], 16 * TILES)

        @block.scalar
        def _(act):
            for k in range(KT):
                act.wait_ge(s["wo_one"], k + 1)
                nc.scalar.copy(wo[:, 0, k], wo_raw[:, k]).then_inc(s["wo_hi"], 1)
            for t in range(TOK_TILES + 2):
                if t < TOK_TILES:
                    act.wait_ge(s[f"o_in{t % 2}"], 16 * (t // 2 + 1))
                    if t >= 2:
                        act.wait_ge(s["h_mm"], t - 1)
                    nc.scalar.copy(o_parts_sb[:, t % 2, 0], o_raw[:, t % 2]).then_inc(s["o_hi"], 1)
                if t >= 2:
                    act.wait_ge(s["logit_t"], t - 1)
                    if t >= 4:
                        act.wait_ge(s["logit_mm"], t - 3)
                    nc.scalar.copy(rows_t[:, t % 2].rearrange("p k n -> p (k n)"), ps[:, t % 2]).then_inc(s["logit_evac"], 1)
            act.wait_ge(s["logit_mm"], TOK_TILES)
            for c in ("rows_t_out", "silu_done", "hid_t_out"):
                act.sem_inc(s[c], C)

            def rows_out(n, par):
                act.wait_ge(s["rows_t_mm"], n + 1)
                act.wait_ge(s["up_mm"], at(n - 2))
                nc.scalar.copy(rows_t[:, par].rearrange("p k n -> p (k n)"), ps[:, 0]).then_inc(s["rows_t_out"], 1)

            def silu(n, par):
                act.wait_ge(s["gate_mm"], n + 1)
                act.wait_ge(s["hid_done"], at(n - 2))
                nc.scalar.activation(act_g[:, par], ps[:, 2 + 2 * par, 0:I_W], ACT.Silu).then_inc(s["silu_done"], 1)

            def hid_out(n, par):
                act.wait_ge(s["hid_t_mm"], at(n))
                act.wait_ge(s["down_mm"], at(n - 2))
                nc.scalar.copy(hid_t[:, par, 0:IC - 1].rearrange("p k n -> p (k n)"),
                               ps[:, 1, 0:(IC - 1) * P])
                nc.scalar.copy(hid_t[0:I_REST, par, IC - 1], ps[0:I_REST, 1, (IC - 1) * P:IC * P]
                               ).then_inc(s["hid_t_out"], 1)

            rows_out(0, 0)
            silu(0, 0)
            rows_out(1, 1)
            for n in (1, 2):
                silu(n, n % 2)
                hid_out(n - 1, 1 - n % 2)
                rows_out(n + 1, 1 - n % 2)
            act.wait_ge(s["r"], R_DIFF)
            nc.scalar.activation(ex[:, 0], ex[:, 1], ACT.Exp).then_inc(s["exp_done"], 1)
            with act.Fori(0, (TILES - 4) // 2) as i:
                for u in range(2):
                    n = i * 2 + (3 + u)
                    silu(n, (1 + u) % 2)
                    hid_out(n - 1, u % 2)
                    rows_out(n + 1, u % 2)
            silu(TILES - 1, 1)
            hid_out(TILES - 2, 0)
            hid_out(TILES - 1, 1)

        @block.tensor
        def _(pe):
            pe.wait_ge(s["ident_ready"], 1)
            pe.wait_ge(s["gate_in"], 16)

            def logit(t):
                pe.wait_ge(s["logit_evac"], t + 1)
                for k in range(KT):
                    ins = pe.matmul(ps[:, 7, t * E_N:(t + 1) * E_N], rows_t[:, t % 2, k], gate[:, k],
                                    start=(k == 0), stop=(k == KT - 1))
                ins.then_inc(s["logit_mm"], 1)

            pe.wait_ge(s["wo_lo"], KT)
            for t in range(TOK_TILES + 2):
                if t < TOK_TILES:
                    pe.wait_ge(s["o_lo"], t + 1)
                    if t >= 2:
                        pe.wait_ge(s["h_ready"], t - 1)
                    n = 0
                    for k in range(KT):
                        for o_part, w_part in ((0, 0), (0, 1), (1, 0)):
                            ins = pe.matmul(ps[:, 2 + t % 2], o_parts_sb[:, t % 2, o_part, k], wo[:, w_part, k],
                                            start=(n == 0), stop=(n == 3 * KT - 1))
                            n += 1
                    ins.then_inc(s["h_mm"], 1)
                if 1 <= t <= TOK_TILES:
                    u = t - 1
                    pe.wait_ge(s["h_ready"], u + 1)
                    if u >= 2:
                        pe.wait_ge(s["logit_evac"], u - 1)
                    for k in range(KT):
                        ins = pe.transpose(ps[:, u % 2, k * P:(k + 1) * P], rows[:, u % 2, k * P:(k + 1) * P], ident[:])
                    ins.then_inc(s["logit_t"], 1)
                if t >= 2:
                    logit(t - 2)

            def counts():
                pe.wait_ge(s["pool_ready"], 7)
                pe.wait_ge(s["r"], R_HOT)
                flat = both[:].rearrange("p t e -> p (t e)")
                pe.matmul(ps[:, 7, P:2 * P], before[:], flat, start=True, stop=True)
                pe.matmul(ps[:, 7, 2 * P:3 * P], ones[:], flat, start=True, stop=True).then_inc(s["count_mm"], 1)

            def table(half):
                for n in range(half * HOT, (half + 1) * HOT):
                    pe.wait_ge(s["hot_done"], 3 * (n + 1))
                    pe.matmul(ps[:, 7, 3 * P:3 * P + 2 * SLOT_TILES], hot_p[:, n % HOT],
                              hot_j[:, n % HOT].rearrange("p a j -> p (a j)"),
                              start=(n == 0), stop=(n == TOP * TOK_TILES - 1)).then_inc(s["tab_mm"], 1)

            for c in ("up_mm", "hid_t_mm", "down_mm"):
                pe.sem_inc(s[c], C)

            def rows_turn(n, par):
                pe.wait_ge(rows_in[par], (n // 2 + 1) * 16 if isinstance(n, int) else n[1])
                n = n if isinstance(n, int) else n[0]
                pe.wait_ge(s["rows_t_out"], at(n - 1))
                for k in range(KT):
                    ins = pe.transpose(ps[:, 0, k * P:(k + 1) * P], rows[:, par, k * P:(k + 1) * P], ident[:])
                ins.then_inc(s["rows_t_mm"], 1)

            def gate_up(n, par, e, up):
                if up:
                    pe.wait_ge(s["hid_done"], at(n - 2))
                else:
                    pe.wait_ge(s["rows_t_out"], at(n))
                    pe.wait_ge(s["silu_done"], at(n - 2))
                for k in range(KT):
                    w = wgu[:, bass.ds(e, 1), k, up * I_W:(up + 1) * I_W].rearrange("p o n -> p (o n)")
                    ins = pe.matmul(ps[:, 2 + 2 * par + up, 0:I_W], rows_t[:, par, k], w,
                                    start=(k == 0), stop=(k == KT - 1))
                ins.then_inc(s["up_mm" if up else "gate_mm"], 1)

            def hid_turn(n, par):
                pe.wait_ge(s["hid_done"], at(n))
                pe.wait_ge(s["hid_t_out"], at(n - 1))
                for c in range(IC):
                    w = P if c < IC - 1 else I_REST
                    ins = pe.transpose(ps[0:w, 1, c * P:(c + 1) * P], hid[:, par, c * P:c * P + w], ident[:])
                ins.then_inc(s["hid_t_mm"], 1)

            def down(n, par, e):
                pe.wait_ge(s["hid_t_out"], at(n))
                pe.wait_ge(s["y_ready"], at(n - 1))
                for c in range(IC):
                    w = P if c < IC - 1 else I_REST
                    wd = wdn[0:w, bass.ds(e, 1), c].rearrange("p o n -> p (o n)")
                    ins = pe.matmul(ps[:, 6], hid_t[0:w, par, c], wd, start=(c == 0), stop=(c == IC - 1))
                ins.then_inc(s["down_mm"], 1)

            def expert(n):
                return pe.value_load(tab_e[0:1, bass.ds(n, 1)], min_val=0, max_val=E_N)

            pe.wait_ge(s["shared_in"], 32)
            rows_turn(0, 0)
            gate_up(0, 0, SHARED, 0)
            rows_turn(1, 1)
            gate_up(0, 0, SHARED, 1)

            def body(i, first, u, e, e_last):
                n = i * 2 + (first + u)
                par = (first + u) % 2
                gate_up(n, par, e, 0)
                hid_turn(n - 1, 1 - par)
                rows_turn((n + 1, i * 16 + 16 * ((first + u + 1) // 2 + 1)), 1 - par)
                gate_up(n, par, e, 1)
                down(n - 1, 1 - par, e_last)

            for n in range(1, LOOP_FROM):
                gate_up(n, n % 2, SHARED, 0)
                hid_turn(n - 1, 1 - n % 2)
                if TABLE_AT < n <= FINISH_AT:
                    table(2 * (n - 1 - TABLE_AT))
                rows_turn(n + 1, 1 - n % 2)
                gate_up(n, n % 2, SHARED, 1)
                down(n - 1, 1 - n % 2, SHARED)
                if TABLE_AT < n <= FINISH_AT:
                    table(2 * (n - 1 - TABLE_AT) + 1)
                if n == COUNT_AT + 1:
                    counts()
            with pe.Fori(0, (TOK_TILES - 1 - LOOP_FROM) // 2) as i:
                for u in range(2):
                    body(i, LOOP_FROM, u, SHARED, SHARED)
            pe.wait_ge(s["experts_in"], 32 * E_N)
            with pe.Fori(0, SLOT_TILES // 2) as i:
                for u in range(2):
                    n = i * 2 + (TOK_TILES - 1 + u)
                    body(i, TOK_TILES - 1, u, expert(n), expert(n - 1))
            n = TILES - 1
            e = expert(n)
            e_last = expert(n - 1)
            gate_up(n, 1, e, 0)
            hid_turn(n - 1, 0)
            gate_up(n, 1, e, 1)
            down(n - 1, 0, e_last)
            hid_turn(n, 1)
            down(n, 1, e)

        @block.vector
        def _(dve):
            done = [0]

            def step(ins):
                done[0] += 1
                ins.then_inc(s["r"], 1)
                dve.wait_ge(s["r"], done[0])

            V = nc.vector
            for k in range(KT):
                if k == 0:
                    dve.wait_ge(s["wo_in"], 16)
                    dve.wait_ge(s["ident_ready"], 1)
                V.tensor_tensor(wo_raw[:, k, k * P:(k + 1) * P], wo_raw[:, k, k * P:(k + 1) * P], ident[:],
                                ALU.add).then_inc(s["wo_one"], 1)
            for k in range(KT):
                dve.wait_ge(s["wo_hi"], k + 1)
                V.tensor_tensor(wo[:, 1, k], wo_raw[:, k], wo[:, 0, k].bitcast(F32), ALU.subtract).then_inc(s["wo_lo"], 1)
            for t in range(TOK_TILES + 1):
                if t < TOK_TILES:
                    dve.wait_ge(s["o_hi"], t + 1)
                    V.tensor_tensor(o_parts_sb[:, t % 2, 1], o_raw[:, t % 2], o_parts_sb[:, t % 2, 0].bitcast(F32),
                                    ALU.subtract).then_inc(s["o_lo"], 1)
                if t >= 1:
                    u = t - 1
                    dve.wait_ge(s["h_mm"], u + 1)
                    if u >= 2:
                        dve.wait_ge(s[f"h_out{u % 2}"], 16 * (u // 2))
                        dve.wait_ge(s["logit_t"], u - 1)
                    V.tensor_copy(rows[:, u % 2], ps[:, 2 + u % 2]).then_inc(s["h_ready"], 1)

            dve.wait_ge(s["pool_ready"], 7)
            step(V.memset(tab_e[:], SHARED))
            step(V.memset(tab_w[:], 1.0))
            step(V.memset(run[:], 1.0))
            step(V.memset(run[:, :, 0:1], 0.0))

            def pick_experts():
                dve.wait_ge(s["logit_mm"], TOK_TILES)
                step(V.tensor_copy(logits[:].rearrange("p t e -> p (t e)"), ps[:, 7, 0:TOK_TILES * E_N]))
                for t in range(TOK_TILES):
                    ins = V.max(top[:, t], logits[:, t])
                step(ins)
                for t in range(TOK_TILES):
                    ins = V.max_index(top_i[:, t], top[:, t], logits[:, t])
                step(ins)
                step(V.tensor_tensor(ex[:, 1], top[:, :, 1], top[:, :, 0], ALU.subtract))
                assert done[0] == R_DIFF

            def hot_experts():
                for c in range(TOP):
                    step(V.tensor_copy(pick[:, c], top_i[:, :, c]))
                    step(V.tensor_tensor(
                        hot[:, c],
                        pick[:, c].rearrange("p (t o) -> p t o", o=1).broadcast_to([P, TOK_TILES, E_N]),
                        lane[:, 0:E_N].rearrange("p (o e) -> p o e", o=1).broadcast_to([P, TOK_TILES, E_N]),
                        ALU.is_equal))
                step(V.tensor_tensor(both[:], hot[:, 0], hot[:, 1], ALU.add))
                assert done[0] == R_HOT

            def weights():
                dve.wait_ge(s["exp_done"], 1)
                step(V.tensor_scalar(ex[:, 1], ex[:, 0], 1.0, None, ALU.add))
                step(V.reciprocal(wts[:, 0], ex[:, 1]))
                step(V.tensor_tensor(wts[:, 1], ex[:, 0], wts[:, 0], ALU.mult))

            def places():
                dve.wait_ge(s["count_mm"], 1)
                step(V.tensor_copy(tot[:], ps[:, 7, 2 * P:3 * P].rearrange("p (t e) -> p e t", e=E_N)))
                step(V.tensor_tensor_scan(carry[:].rearrange("p e t -> p (e t)"), run[:].rearrange("p e t -> p (e t)"),
                                          tot[:].rearrange("p e t -> p (e t)"), 0.0, ALU.mult, ALU.add))
                step(V.tensor_scalar(cnt_i[:], carry[:, :, TOK_TILES - 1], float(P - 1), None, ALU.add))
                step(V.tensor_scalar(cnt_i[:], cnt_i[:], 7, None, ALU.arith_shift_right))
                step(V.tensor_copy(cnt[:], cnt_i[:]))
                step(V.tensor_tensor_scan(ends[:], ones[:, 0:E_N], cnt[:], 0.0, ALU.mult, ALU.add))
                step(V.tensor_tensor(base[:], ends[:], cnt[:], ALU.subtract))
                step(V.tensor_tensor(carry[:], carry[:], tot[:], ALU.subtract))
                step(V.scalar_tensor_tensor(
                    out=pos[:], in0=base[:].rearrange("p (o e) -> p o e", o=1).broadcast_to([P, TOK_TILES, E_N]),
                    scalar=float(P), in1=carry[:].rearrange("p e t -> p t e"), op0=ALU.mult, op1=ALU.add))
                step(V.tensor_tensor(pos[:].rearrange("p t e -> p (t e)"), pos[:].rearrange("p t e -> p (t e)"),
                                     ps[:, 7, P:2 * P], ALU.add))

            def slots_of_tokens():
                for c in range(TOP):
                    step(V.tensor_tensor(sel[:, c], hot[:, c], pos[:], ALU.mult))
                step(V.tensor_reduce(slot[:], sel.rearrange("p c t e -> p (c t) e"), AX.X, ALU.add))
                step(V.tensor_copy(slot_i[:, 0], slot[:]))
                step(V.tensor_scalar(slot_i[:, 1], slot_i[:, 0], P - 1, None, ALU.bitwise_and))
                step(V.tensor_scalar(slot_i[:, 2], slot_i[:, 0], 7, None, ALU.arith_shift_right))
                step(V.tensor_copy(slot_p[:], slot_i[:, 1]))
                step(V.tensor_copy(slot_j[:], slot_i[:, 2]))
                step(V.tensor_tensor(
                    late, lane[0:1, 0:SLOT_TILES].rearrange("p (j o) -> p j o", o=1).broadcast_to([1, SLOT_TILES, E_N]),
                    ends[0:1].rearrange("p (o e) -> p o e", o=1).broadcast_to([1, SLOT_TILES, E_N]), ALU.is_ge))
                step(V.tensor_reduce(tile_e[:], late, AX.X, ALU.add))
                step(V.tensor_scalar(tab_e[:, TOK_TILES:], tile_e[:], float(E_N - 1), None, ALU.min))

            def hot_rows(half):
                for n in range(half * HOT, (half + 1) * HOT):
                    c, t = divmod(n, TOK_TILES)
                    i = n % HOT
                    if n >= HOT:
                        dve.wait_ge(s["tab_mm"], n - HOT + 1)
                    V.tensor_scalar(hot_p[:, i], lane[:], slot_p[:, n:n + 1], None,
                                    ALU.is_equal).then_inc(s["hot_done"], 1)
                    V.tensor_scalar(hot_j[:, i, 0], lane[:, 0:SLOT_TILES], slot_j[:, n:n + 1],
                                    token[:, t:t + 1], ALU.is_equal, ALU.mult).then_inc(s["hot_done"], 1)
                    V.tensor_scalar(hot_j[:, i, 1], lane[:, 0:SLOT_TILES], slot_j[:, n:n + 1],
                                    wts[:, c, t:t + 1], ALU.is_equal, ALU.mult).then_inc(s["hot_done"], 1)

            def tables():
                dve.wait_ge(s["tab_mm"], TOP * TOK_TILES)
                step(V.tensor_copy(tok_f[:], ps[:, 7, 3 * P:3 * P + SLOT_TILES]))
                step(V.tensor_copy(tab_w[:, TOK_TILES:], ps[:, 7, 3 * P + SLOT_TILES:3 * P + 2 * SLOT_TILES]))
                step(V.tensor_scalar(empty[:], tok_f[:], 0.0, None, ALU.is_equal))
                step(V.scalar_tensor_tensor(out=tok_f[:], in0=empty[:], scalar=own[:], in1=tok_f[:],
                                            op0=ALU.mult, op1=ALU.add))
                step(V.tensor_scalar(tab_tok[:, TOK_TILES:], tok_f[:], -1.0, None, ALU.add))

            for c in ("hid_done", "y_ready"):
                dve.sem_inc(s[c], C)

            def index(n, par):
                V.tensor_copy(idx_g[:, par:par + 1], tab_tok[:, bass.ds(n, 1)]).then_inc(s["idx_ready"], 1)

            def multiply(n, par):
                dve.wait_ge(s["up_mm"], at(n))
                dve.wait_ge(s["silu_done"], at(n))
                dve.wait_ge(s["hid_t_mm"], at(n - 2))
                V.tensor_tensor(hid[:, par], act_g[:, par], ps[:, 3 + 2 * par, 0:I_W], ALU.mult).then_inc(s["hid_done"], 1)

            def weigh(n, par):
                dve.wait_ge(s["down_mm"], at(n))
                if not isinstance(n, int) or n > 1:
                    dve.wait_ge(s["y_out"], 16 * (n - 1))
                V.tensor_copy(idx_s[:, par:par + 1], tab_tok[:, bass.ds(n, 1)])
                V.tensor_scalar(y[:, par], ps[:, 6], tab_w[:, bass.ds(n, 1)], None, ALU.mult).then_inc(s["y_ready"], 1)

            stages = {PICK_AT: pick_experts, COUNT_AT: hot_experts, WEIGH_AT: weights, PLACE_AT: places,
                      SLOT_AT: slots_of_tokens, FINISH_AT: tables}
            index(0, 0)
            index(1, 1)
            for n in range(LOOP_FROM):
                multiply(n, n % 2)
                if TABLE_AT <= n < FINISH_AT:
                    hot_rows(2 * (n - TABLE_AT))
                index(n + 2, n % 2)
                if n >= 1:
                    weigh(n - 1, 1 - n % 2)
                if n in stages:
                    stages[n]()
                elif TABLE_AT <= n < FINISH_AT:
                    hot_rows(2 * (n - TABLE_AT) + 1)
            with dve.Fori(0, (TILES - 3 - LOOP_FROM) // 2) as i:
                for u in range(2):
                    n = i * 2 + (LOOP_FROM + u)
                    multiply(n, (LOOP_FROM + u) % 2)
                    index(n + 2, (LOOP_FROM + u) % 2)
                    weigh(n - 1, (LOOP_FROM + u + 1) % 2)
            multiply(TILES - 3, 1)
            index(TILES - 1, 1)
            weigh(TILES - 4, 0)
            multiply(TILES - 2, 0)
            weigh(TILES - 3, 1)
            multiply(TILES - 1, 1)
            weigh(TILES - 2, 0)
            weigh(TILES - 1, 1)


R_DIFF = 8
R_HOT = 13


def kernel(**inputs):
    import numpy as np
    import concourse.bacc as bacc
    from concourse.bass_utils import run_bass_kernel_spmd as run

    nc = bacc.Bacc("TRN2", target_bir_lowering=False, num_devices=1)
    i = {k: np.asarray(a) for k, a in inputs.items()}

    def tiles(a):
        return np.ascontiguousarray(a.reshape(-1, P, a.shape[-1]).transpose(1, 0, 2))

    def all_experts(name):
        return np.concatenate([i[f"L0_ffn_expert_{name}_w"], i[f"L0_ffn_shared_{name}_w"][None]])

    gu = np.concatenate([all_experts("gate"), all_experts("up")], axis=1)
    gu = gu.reshape(E_N + 1, 2 * I_W, KT, P).transpose(0, 3, 2, 1)
    dn = np.pad(all_experts("down"), ((0, 0), (0, 0), (0, IC * P - I_W)))
    dn = dn.reshape(E_N + 1, D, IC, P).transpose(0, 3, 2, 1)
    arrays = {
        "x": np.ascontiguousarray(i["x"].reshape(B * S, D)),
        "cond_t": tiles(np.ascontiguousarray(i["cond_2048"].T)),
        "w_emb": tiles(i["L0_cond_W_emb"]),
        "b_emb": np.ascontiguousarray(i["L0_cond_b_emb"].reshape(2 * KT, P).T),
        "g_norm": np.ascontiguousarray(i["L0_cond_g_norm"].reshape(KT, P).T),
        "w_qkv": np.ascontiguousarray(tiles(i["L0_cond_W_qkv"]).reshape(P, KT, 3, D)),
        "g_q": i["L0_cond_g_q"].reshape(1, DH),
        "g_k": i["L0_cond_g_k"].reshape(1, DH),
        "w_out": tiles(i["L0_cond_W_out"]),
        "gate_t": tiles(np.ascontiguousarray(i["L0_ffn_gate_weight"].T)),
        "w_gu": np.ascontiguousarray(gu),
        "w_down": np.ascontiguousarray(dn),
    }
    ap = {k: nc.dram_tensor(k, a.shape, F32, kind="ExternalInput").ap() for k, a in arrays.items()}
    h_rows = nc.dram_tensor("h_rows", (B * S + P, D), F32, kind="Internal").ap()
    out = nc.dram_tensor("out", (B * S + P, D), F32, kind="ExternalOutput").ap()
    o_parts = nc.dram_tensor("o_parts", (B, NG, P, S), F32, kind="Internal").ap()
    attention_block(nc, *(ap[k] for k in ("x", "cond_t", "w_emb", "b_emb", "g_norm", "w_qkv", "g_q", "g_k")),
                    h_rows, o_parts, out)
    ffn_block(nc, o_parts, ap["w_out"], h_rows, ap["gate_t"], ap["w_gu"], ap["w_down"], out)
    got = run(nc, [arrays], core_ids=[0]).results[0]["out"]
    return np.ascontiguousarray(got[0:B * S]).reshape(B, S, D)
```

```python
from contextlib import ExitStack

import concourse.bass as bass
from concourse import mybir

ALU = mybir.AluOpType
ACT = mybir.ActivationFunctionType
AX = mybir.AxisListType
F32 = mybir.dt.float32
F32R = mybir.dt.float32r

P = 128
B = 4
S = 512
D = 512
HEADS = 16
DH = D // HEADS
KT = D // P
TT = S // P
HG = P // DH
NG = HEADS // HG
SR = 3 * DH
EPS = 1e-6
LN_EXP = 6
CREDIT = 16
M_FIRST = (0, 4, 9, 16, 16)
SLOTS = {
    (0, 2): (("x", 0), ("x", 1)), (0, 3): (("x", 2), ("x", 3)),
    (1, 1): (("q", 0), ("k", 0)), (1, 2): (("q", 1), ("k", 1)),
    (1, 3): (("q", 2), ("k", 2)), (2, 1): (("q", 3), ("k", 3)),
    (2, 2): (("v", 0), ("v", 1)), (3, 2): (("v", 2), ("v", 3)),
}
X_NORM = (0, 1)
QK_NORM = {(1, 2): 0, (1, 3): 1, (2, 0): 2, (2, 2): 3}


def attention_block(nc, x, cond_t, w_emb, b_emb, g_norm, w_qkv, g_q, g_k, h_rows, o_parts, out):
    with ExitStack() as ctx:
        def sb(name, shape, dt=F32):
            return ctx.enter_context(nc.sbuf_tensor(name, shape, dt))

        def sem(name):
            return ctx.enter_context(nc.semaphore(name))

        ps = ctx.enter_context(nc.psum_tensor("ps", [P, 8, S], F32))

        wqkv = sb("wqkv", [P, 2, KT, 3 * D], F32R)
        xn = sb("xn", [P, 2, KT, S], F32R)
        x_nat = sb("x_nat", [P, TT, D])
        xtmp = sb("xtmp", [P, 2, KT, P])
        sq = sb("sq", [P, 2, D])
        qk = sb("qk", [P, 2, TT, 2 * D])
        v = sb("v", [P, TT, D])
        v_next = sb("v_next", [P, TT, D])
        parts = sb("parts", [P, 2, 2, 2, TT, SR], F32R)
        q_st = sb("q_st", [P, 2, HG, S], F32R)
        k_st = sb("k_st", [P, 2, HG, S], F32R)
        p_sb = sb("p_sb", [P, 2, HG, S])
        o_t = sb("o_t", [P, 2, S])
        o_n = sb("o_n", [P, S])
        ident = sb("ident", [P, P])
        ones = sb("ones", [P, DH])
        ab = sb("ab", [P, 2, KT, B])
        condt = sb("condt", [P, KT, B])
        bemb = sb("bemb", [P, 2 * KT])
        gn = sb("gn", [P, KT])
        gqk = sb("gqk", [P, 2, DH])
        grow = sb("grow", [P, DH])
        sx = sb("sx", [P, 4, TT])
        sh = sb("sh", [P, 4, 2 * HEADS])
        mx = sb("mx", [P, 2, HG * TT])
        nm = sb("nm", [HG * TT, 2, P], F32R)
        w_raw = [p_sb[:, 0, 0:3, :], p_sb[:, 1, 0:3, :]]
        w_emb_sb = qk[:, 1]

        rows_out = sem("rows_out")
        const_in = sem("const_in")
        wemb_in = sem("wemb_in")
        wraw_in = [sem("wraw_in0"), sem("wraw_in1")]
        ident0 = sem("ident0")
        pool_const = sem("pool_const")
        pool_settled = sem("pool_settled")
        act_settled = sem("act_settled")
        w_hi = sem("w_hi")
        w_lo = sem("w_lo")
        emb_mm = sem("emb_mm")
        ab_ready = sem("ab_ready")
        ones_ready = sem("ones_ready")
        grow_ready = sem("grow_ready")
        x_in = [sem(f"x_in{t}") for t in range(TT)]
        ssx_ready = sem("ssx_ready")
        vx_ready = sem("vx_ready")
        gx_ready = sem("gx_ready")
        nx_ready = sem("nx_ready")
        xs_ready = sem("xs_ready")
        xt_ready = sem("xt_ready")
        xtmp_ready = sem("xtmp_ready")
        xh_ready = sem("xh_ready")
        xl_ready = sem("xl_ready")
        chunk_ready = sem("chunk_ready")
        sq_ready = sem("sq_ready")
        ss_ready = sem("ss_ready")
        vv_ready = sem("vv_ready")
        gr_ready = sem("gr_ready")
        nr_ready = sem("nr_ready")
        raw_ready = sem("raw_ready")
        qk_ready = sem("qk_ready")
        qg_ready = sem("qg_ready")
        v_ready = sem("v_ready")
        v_moved = sem("v_moved")
        part_hi = sem("part_hi")
        part_lo = sem("part_lo")
        t_ready = sem("t_ready")
        stack_ready = sem("stack_ready")
        m_ready = sem("m_ready")
        max_ready = sem("max_ready")
        maxt_ready = sem("maxt_ready")
        nmhi_ready = sem("nmhi_ready")
        nm_ready = sem("nm_ready")
        nm_in = sem("nm_in")
        st_ready = sem("st_ready")
        exp_ready = sem("exp_ready")
        pv_ready = sem("pv_ready")
        guess_ready = sem("guess_ready")
        newton_ready = sem("newton_ready")
        norm_ready = sem("norm_ready")
        o_out = [sem("o_out0"), sem("o_out1")]

        PAIRS = HEADS // 2

        def pairs_ahead(g, s, last):
            n = 2 * (g + 2) + s - 2
            return [n] if s >= 2 and (n < PAIRS or not last) else []

        x_tiles = x.rearrange("(b t p) h -> b t p h", b=B, p=P)
        block = ctx.enter_context(nc.Block())

        def wait(eng, s, value):
            if not isinstance(value, int) or value > 0:
                eng.wait_ge(s, value)

        def part(n, r, c):
            return parts[:, n % 2, r, :, :, c * DH:(c + 1) * DH].rearrange("p h t d -> p t h d")

        def heads_of(b, n, r):
            half = (b + n // (HEADS // 2)) % 2
            n = n % (HEADS // 2)
            cols = slice(r * D + 2 * n * DH, r * D + 2 * (n + 1) * DH)
            if isinstance(half, int):
                a = qk[:, half, :, cols]
            else:
                a = qk[:, bass.ds(half, 1), :, cols].rearrange("p o t n -> p (o t) n")
            return a.rearrange("p t (h d) -> p t h d", d=DH)


        TURN = [(g, s) for g in range(NG) for s in range(TT)][1:] + [(NG, 0)]
        AHEAD = [(-1, s) for s in range(TT)] + [(0, 0)]

        @block.sync
        def _(sp):
            sp.dma_start(condt[:], cond_t).then_inc(const_in, 16)
            sp.dma_start(bemb[:], b_emb).then_inc(const_in, 16)
            sp.dma_start(gn[:], g_norm).then_inc(const_in, 16)
            sp.dma_start(gqk[:, 0], g_q.broadcast_to([P, DH])).then_inc(const_in, 16)
            sp.dma_start(gqk[:, 1], g_k.broadcast_to([P, DH])).then_inc(const_in, 16)
            for t in range(TT):
                sp.dma_start(x_nat[:, t], x_tiles[0, t]).then_inc(x_in[t], 16)
            sp.dma_start(w_emb_sb, w_emb).then_inc(wemb_in, 16)
            sp.dma_start(w_raw[0], w_qkv[:, 0]).then_inc(wraw_in[0], 16)
            sp.dma_start(w_raw[1], w_qkv[:, 1]).then_inc(wraw_in[1], 16)
            for credit in o_out:
                sp.sem_inc(credit, CREDIT)

            def load_x(b, t):
                wait(sp, xt_ready, (b - 1) * TT + t + 1)
                sp.dma_start(x_nat[:, t], x_tiles[b, t]).then_inc(x_in[t], 16)

            def max_rows(b, g):
                sp.wait_ge(nm_ready, b * NG + g + 1)
                for which in range(2):
                    row = SR + which
                    sp.dma_start(
                        q_st[row:row + 1, g % 2].rearrange("o h (t q) -> o (h t) q", q=P).bitcast(F32),
                        nm[:, which, :].bitcast(F32)).then_inc(nm_in, 16)

            def store_o(b, g):
                sp.wait_ge(norm_ready, b * NG + g + 2)
                sp.dma_start(o_parts[b, g], o_t[:, g % 2]).then_inc(o_out[g % 2], 16)

            for t in range(2, TT):
                sp.wait_ge(w_lo, t - 1)
                sp.dma_start(w_raw[t % 2], w_qkv[:, t]).then_inc(wraw_in[t % 2], 16)
            sp.dma_start(out[0:B * S], x).then_inc(rows_out, 16)
            sp.dma_start(out[B * S:B * S + P], x[0:P]).then_inc(rows_out, 16)
            sp.dma_start(h_rows[B * S:B * S + P], x[0:P]).then_inc(rows_out, 16)
            max_rows(0, 0)

            def turn(b, last):
                if not last:
                    for t in range(TT):
                        load_x(b + 1, t)
                for g in range(NG):
                    if g + 1 < NG or not last:
                        max_rows(b, g + 1)
                    store_o(b, g)

            with sp.Fori(0, B - 1) as b:
                turn(b, False)
            turn(B - 1, True)
            for slot in range(2):
                sp.wait_ge(o_out[slot], CREDIT + 16 * B * NG // 2)
            sp.wait_ge(rows_out, 48)

        @block.gpsimd
        def _(pool):
            nc.gpsimd.memset(ident[:], 0.0).then_inc(ident0, 1)
            pool.wait_ge(ident0, 1)
            nc.gpsimd.affine_select(out=ident[:], in_=ident[:], compare_op=ALU.not_equal, fill=1.0, base=0,
                                    pattern=[[-1, P]], channel_multiplier=1).then_inc(pool_const, 1)
            nc.gpsimd.memset(ones[:], 1.0).then_inc(pool_const, 1)

            def part_high(b, n):
                if n % PAIRS == 0:
                    pool.wait_ge(qg_ready, b * TT + TT * (1 + n // PAIRS))
                    pool.wait_ge(qk_ready, b * TT + TT * (1 + n // PAIRS))
                wait(pool, t_ready, b * HEADS + 2 * (n - 1))
                pool.sem_inc(pool_settled, 1)
                for r, c in ((0, 0), (1, 0), (0, 2), (1, 1)):
                    nc.gpsimd.tensor_copy(part(n, r, c), heads_of(b, n, r)).then_inc(part_hi, 1)

            for n in range(2):
                part_high(0, n)
            for g, s in AHEAD:
                for n in pairs_ahead(g, s, False):
                    part_high(0, n)

            def turn(b, last):
                for g, s in TURN:
                    for n in pairs_ahead(g, s, last):
                        part_high(b, n)

            with pool.Fori(0, B - 1) as b:
                turn(b, False)
            turn(B - 1, True)

        @block.scalar
        def _(act):
            def column(a, b):
                return a[:, b:b + 1] if isinstance(b, int) else a[:, bass.ds(b, 1)]

            def x_sums(b):
                for t in range(TT):
                    act.wait_ge(x_in[t], b * 16 + 16)
                    if t == 0:
                        wait(act, ss_ready, b * (2 * TT))
                        wait(act, xs_ready, b * TT)
                    if t >= 2:
                        act.wait_ge(ssx_ready, b * TT + t - 1)
                    nc.scalar.activation(sq[:, t % 2], x_nat[:, t], ACT.Square,
                                         accum_out=sx[:, 0, t:t + 1]).then_inc(ssx_ready, 1)

            def x_guess(b):
                act.wait_ge(vx_ready, b + 1)
                nc.scalar.activation(sx[:, 2], sx[:, 1], ACT.Ln).then_inc(gx_ready, 1)
                act.wait_ge(gx_ready, b * 2 + 1)
                nc.scalar.activation(sx[:, 2], sx[:, 2], ACT.Exp, scale=-0.5).then_inc(gx_ready, 1)

            def tile_out(b, t):
                act.wait_ge(xt_ready, b * TT + t + 1)
                wait(act, xl_ready, b * TT + t - 1)
                act.sem_inc(act_settled, 1)
                for j in range(KT):
                    ins = nc.scalar.activation(xtmp[:, t % 2, j], ps[:, t % 2, j * P:(j + 1) * P], ACT.Identity,
                                               bias=column(ab[:, 1, j], b), scale=column(ab[:, 0, j], b))
                ins.then_inc(xtmp_ready, 1)

            def chunk_out(b, kind, t):
                if kind == "v":
                    act.wait_ge(chunk_ready, b * (3 * TT) + 2 * TT + t + 1)
                    wait(act, v_moved, b)
                    nc.scalar.copy(v_next[:, t], ps[:, t % 2]).then_inc(v_ready, 1)
                    return
                r = "qk".index(kind)
                n = 2 * t + r
                act.wait_ge(chunk_ready, b * (3 * TT) + n + 1)
                if n < 2:
                    act.wait_ge(ssx_ready, b * TT + TT)
                else:
                    act.wait_ge(ss_ready, b * (2 * TT) + n - 1)
                nc.scalar.activation(sq[:, r], ps[:, r], ACT.Square).then_inc(sq_ready, 1)
                wait(act, part_lo, b * HEADS - (HEADS - 4) if not isinstance(b, int) or b > 0 else 0)
                act.sem_inc(act_settled, 1)
                half = b % 2
                a = qk[:, half, t] if isinstance(half, int) else qk[:, bass.ds(half, 1), t].rearrange("p o n -> p (o n)")
                nc.scalar.copy(a[:, r * D:(r + 1) * D], ps[:, r]).then_inc(raw_ready, 1)

            def qk_guess(b, t):
                act.wait_ge(vv_ready, b * TT + t + 1)
                wait(act, qk_ready, b * TT + t)
                nc.scalar.activation(sh[:, 2], sh[:, 1], ACT.Ln).then_inc(gr_ready, 1)
                act.wait_ge(gr_ready, b * (2 * TT) + 2 * t + 1)
                nc.scalar.activation(sh[:, 2], sh[:, 2], ACT.Exp, scale=-0.5).then_inc(gr_ready, 1)

            def stack(b, n):
                act.wait_ge(t_ready, b * HEADS + n + 1)
                for r in range(2):
                    nc.scalar.copy((q_st, k_st)[r][0:SR, n // HG % 2, n % HG],
                                   ps[0:SR, 2 * (n % 2) + r]).then_inc(stack_ready, 1)

            def exps(b, g, kt, pair):
                act.wait_ge(st_ready, b * (NG * TT * 2) + (TT * g + kt) * 2 + pair + 1)
                act.wait_ge(pv_ready, b * (NG * TT) + TT * g + kt + 1)
                nc.scalar.activation(p_sb[:, kt % 2, 2 * pair:2 * pair + 2], ps[:, 4:6],
                                     ACT.Exp).then_inc(exp_ready, 1)

            def sums_guess(b, g):
                act.wait_ge(pv_ready, b * (NG * TT) + TT * (g + 1) + 2)
                act.wait_ge(o_out[g % 2], b * (8 * NG) + 16 * (g // 2) + CREDIT)
                nc.scalar.activation(o_t[:, g % 2], ps[:, 7], ACT.Ln).then_inc(guess_ready, 1)
                act.wait_ge(guess_ready, b * (2 * NG) + 2 * g + 1)
                nc.scalar.activation(o_t[:, g % 2], o_t[:, g % 2], ACT.Exp, scale=-1.0).then_inc(guess_ready, 1)

            def weight_high(n):
                act.wait_ge(wraw_in[n % 2], 16 * (n // 2 + 1))
                nc.scalar.copy(wqkv[:, 0, n], w_raw[n % 2].rearrange("p k n -> p (k n)")).then_inc(w_hi, 1)

            def step(b, g, s, last):
                slots = () if last else SLOTS.get((g, s), ())
                if g >= 0:
                    exps(b, g, s, 0)
                if s < 2 and (not last or g + 1 < NG):
                    stack(b, HG * (g + 1) + 2 * s)
                    stack(b, HG * (g + 1) + 2 * s + 1)
                if not last and (g, s) in QK_NORM:
                    qk_guess(b + 1, QK_NORM[g, s])
                if s < 2 and g >= 0 and (not last or g + 1 < NG):
                    exps(b, g, s, 1)
                for kind, t in slots:
                    if kind == "x":
                        tile_out(b + 1, t)
                    else:
                        chunk_out(b + 1, kind, t)
                if g >= 0 and not (s < 2 and (not last or g + 1 < NG)):
                    exps(b, g, s, 1)
                if not last and (g, s) == X_NORM:
                    x_sums(b + 1)
                    x_guess(b + 1)
                if s == 0 and g >= 1:
                    sums_guess(b, g - 1)

            nc.scalar.add_instruction(mybir.InstLoadActFuncSet(
                name=nc.get_next_instruction_name(), act_func_set_id=LN_EXP, engine=mybir.EngineType.Activation))
            x_sums(0)
            x_guess(0)
            for n in range(KT):
                weight_high(n)
            act.wait_ge(ab_ready, 2)
            for t in range(TT):
                tile_out(0, t)
            for t in range(TT):
                chunk_out(0, "q", t)
                chunk_out(0, "k", t)
                qk_guess(0, t)
            for t in range(TT):
                chunk_out(0, "v", t)
            for g, s in AHEAD:
                step(0, g, s, False)

            def turn(b, last):
                for g, s in TURN:
                    if not last or g < NG:
                        step(b, g, s, last)
                if last:
                    sums_guess(b, NG - 1)

            with act.Fori(0, B - 1) as b:
                turn(b, False)
            turn(B - 1, True)

        @block.tensor
        def _(pe):
            def slot_left(b, kind, t):
                if kind == "x":
                    pe.wait_ge(xtmp_ready, b * TT + t + 1)
                elif kind == "v":
                    pe.wait_ge(v_ready, b * TT + t + 1)
                else:
                    pe.wait_ge(raw_ready, b * (2 * TT) + 2 * t + "qk".index(kind) + 1)

            def stacked(b, g, i):
                pe.wait_ge(stack_ready, b * (2 * HEADS) + 2 * (HG * g + i) + 2)

            def banks_left(b, g, s, last):
                slots = () if last else SLOTS.get((g, s), ())
                for kind, t in slots:
                    slot_left(b + 1, kind, t)
                if s < 2 and not slots:
                    stacked(b, g + 1, 2 * s)
                if s == 3 and not slots:
                    banks_left(b, g, 2, last)
                if s == 2 and not slots:
                    banks_left(b, g, 1, last)

            def slot(b, kind, t):
                bank = t % 2 if kind in "xv" else "qk".index(kind)
                if kind == "x":
                    pe.wait_ge(xs_ready, b * TT + t + 1)
                    for j in range(KT):
                        ins = pe.transpose(ps[:, bank, j * P:(j + 1) * P], x_nat[:, t, j * P:(j + 1) * P], ident[:])
                    ins.then_inc(xt_ready, 1)
                    return
                pe.wait_ge(xl_ready, b * TT + t + 1)
                c = "qkv".index(kind)
                n = 0
                for j in range(KT):
                    for xpart, wpart in ((0, 0), (0, 1), (1, 0)):
                        ins = pe.matmul(ps[:, bank], xn[:, xpart, j, t * P:(t + 1) * P],
                                        wqkv[:, wpart, j, c * D:(c + 1) * D], start=(n == 0), stop=(n == 3 * KT - 1))
                        n += 1
                ins.then_inc(chunk_ready, 1)

            def transposes(b, n):
                pe.wait_ge(part_lo, b * HEADS + 2 * (n // 2) + 2)
                for r in range(2):
                    for t in range(TT):
                        ins = pe.transpose(ps[0:SR, 2 * (n % 2) + r, t * P:(t + 1) * P],
                                           parts[:, n // 2 % 2, r, n % 2, t].bitcast(F32), ident[:])
                ins.then_inc(t_ready, 1)

            def max_scores(b, g, i):
                h, t = divmod(i, TT)
                n = HG * TT * g + i
                stacked(b, g, h)
                wait(pe, max_ready, b * (HEADS * TT) + n - 1)
                pe.matmul(ps[:, 2 + i % 2], q_st[0:SR, g % 2, h, t * P:(t + 1) * P],
                          k_st[0:SR, g % 2, h], start=True, stop=True).then_inc(m_ready, 1)

            def max_rows(b, g):
                pe.wait_ge(max_ready, b * (HEADS * TT) + HG * TT * (g + 1))
                pe.transpose(ps[0:HG * TT, 3, 0:P], mx[:, g % 2], ident[:]).then_inc(maxt_ready, 1)

            def scores(b, g, kt, pair):
                n = (TT * g + kt) * 2 + pair
                if kt == 0 and pair == 0:
                    pe.wait_ge(nm_in, b * (NG * 32) + 32 * (g + 1))
                wait(pe, exp_ready, b * (NG * TT * 2) + n)
                for i in range(2):
                    h = 2 * pair + i
                    ins = pe.matmul(ps[:, 4 + i], k_st[0:SR + 2, g % 2, h, kt * P:(kt + 1) * P],
                                    q_st[0:SR + 2, g % 2, h], start=True, stop=True)
                ins.then_inc(st_ready, 1)

            def products(b, g, kt, what):
                if what == 0:
                    pe.wait_ge(exp_ready, b * (NG * TT * 2) + (TT * g + kt) * 2 + 2)
                    if kt == 0:
                        pe.wait_ge(norm_ready, b * NG + g + 1)
                        if g % NG == 0:
                            pe.wait_ge(v_moved, b + g // NG + 1)
                for h in range(HG):
                    col = (HG * (g % NG) + h) * DH
                    w = v[:, kt, col:col + DH] if what == 0 else ones[:]
                    ins = pe.matmul(ps[h * DH:(h + 1) * DH, 6 + what], w, p_sb[:, kt % 2, h],
                                    start=(kt == 0), stop=(kt == TT - 1))
                if what == 1:
                    ins.then_inc(pv_ready, 1)

            def step(b, g, s, last):
                stacks = s < 2 and (not last or g + 1 < NG)
                slots = () if last else SLOTS.get((g, s), ())
                maxima = list(range(M_FIRST[s], M_FIRST[s + 1])) if not last or g + 1 < NG else []
                def some_maxima(most):
                    for _ in range(min(most, len(maxima))):
                        max_scores(b, g + 1, maxima.pop(0))

                if g >= 0:
                    scores(b, g, s, 0)
                if stacks:
                    if (g, s) == (-1, 0):
                        pe.wait_ge(v_ready, TT)
                    else:
                        banks_left(b, g + (s - 1) // TT, (s - 1) % TT, last)
                    transposes(b, HG * (g + 1) + 2 * s)
                    wait(pe, nm_ready, b * NG + g + 1)
                    wait(pe, max_ready, b * (HEADS * TT) + HG * TT * (g + 1) + M_FIRST[s])
                    transposes(b, HG * (g + 1) + 2 * s + 1)
                if s == 3 and (not last or g + 1 < NG):
                    max_rows(b, g + 1)
                if slots and not stacks:
                    banks_left(b, g, s - 1, last)
                    slot(b + 1, *slots[0])
                    some_maxima(2)
                    slot(b + 1, *slots[1])
                    some_maxima(2)
                elif not stacks:
                    some_maxima(2)
                before = divmod(TT * g + s - 1, TT)
                if before[0] >= 0:
                    products(b, *before, 0)
                if g >= 0:
                    scores(b, g, s, 1)
                if stacks:
                    stacked(b, g + 1, 2 * s + 1)
                some_maxima(2)
                if before[0] >= 0:
                    products(b, *before, 1)
                some_maxima(len(maxima))
                if stacks and slots:
                    for kind_t in slots:
                        slot(b + 1, *kind_t)

            pe.wait_ge(pool_const, 2)
            for t in range(2):
                slot(0, "x", t)
            pe.wait_ge(const_in, 16 * 5)
            pe.wait_ge(wemb_in, 16)
            for m in range(2 * KT):
                for k in range(KT):
                    ins = pe.matmul(ps[:, 2, m * B:(m + 1) * B], w_emb_sb[:, k, m * P:(m + 1) * P],
                                    condt[:, k], start=(k == 0), stop=(k == KT - 1))
            ins.then_inc(emb_mm, 1)
            pe.wait_ge(ab_ready, 2)
            pe.wait_ge(ones_ready, 1)
            pe.sem_inc(pv_ready, 2)

            for t in range(2, TT):
                slot_left(0, "x", t - 2)
                slot(0, "x", t)
            slot_left(0, "x", TT - 1)
            for t in range(TT):
                pe.wait_ge(w_lo, KT)
                for r in range(2):
                    if t >= 1:
                        slot_left(0, "qk"[r], t - 1)
                    slot(0, "qk"[r], t)
            slot_left(0, "k", TT - 1)
            for t in range(TT):
                if t >= 2:
                    slot_left(0, "v", t - 2)
                slot(0, "v", t)
            for g, s in AHEAD:
                step(0, g, s, False)

            def turn(b, last):
                for g, s in TURN:
                    if not last or g < NG:
                        step(b, g, s, last)
                if last:
                    products(b, NG - 1, TT - 1, 0)
                    products(b, NG - 1, TT - 1, 1)

            with pe.Fori(0, B - 1) as b:
                turn(b, False)
            turn(B - 1, True)

        @block.vector
        def _(dve):
            nc.vector.memset(k_st[SR:SR + DH].bitcast(F32), 1.0).then_inc(ones_ready, 1)

            def x_norm(b):
                v_, y_, f_ = sx[:, 1], sx[:, 2], sx[:, 3]
                dve.wait_ge(ssx_ready, b * TT + TT)
                nc.vector.tensor_scalar(v_, sx[:, 0], 1.0 / D, EPS, ALU.mult, ALU.add).then_inc(vx_ready, 1)
                dve.wait_ge(gx_ready, b * 2 + 2)
                nc.vector.tensor_tensor(f_, y_, y_, ALU.mult).then_inc(nx_ready, 1)
                dve.wait_ge(nx_ready, b * 3 + 1)
                nc.vector.scalar_tensor_tensor(out=f_, in0=f_, scalar=-0.5, in1=v_, op0=ALU.mult,
                                               op1=ALU.mult).then_inc(nx_ready, 1)
                dve.wait_ge(nx_ready, b * 3 + 2)
                nc.vector.scalar_tensor_tensor(out=f_, in0=f_, scalar=1.5, in1=y_, op0=ALU.add,
                                               op1=ALU.mult).then_inc(nx_ready, 1)
                dve.wait_ge(nx_ready, b * 3 + 3)
                for t in range(TT):
                    nc.vector.tensor_scalar(x_nat[:, t], x_nat[:, t], sx[:, 3, t:t + 1], None,
                                            ALU.mult).then_inc(xs_ready, 1)

            def tile_split(b, t):
                dve.wait_ge(xtmp_ready, b * TT + t + 1)
                cols = slice(t * P, (t + 1) * P)
                nc.vector.tensor_copy(xn[:, 0, :, cols], xtmp[:, t % 2]).then_inc(xh_ready, 1)
                dve.wait_ge(xh_ready, b * TT + t + 1)
                nc.vector.tensor_tensor(xn[:, 1, :, cols], xtmp[:, t % 2], xn[:, 0, :, cols].bitcast(F32),
                                        ALU.subtract).then_inc(xl_ready, 1)

            def qk_sums(b, t):
                for r in range(2):
                    dve.wait_ge(sq_ready, b * (2 * TT) + 2 * t + r + 1)
                    nc.vector.tensor_reduce(sh[:, 0, r * HEADS:(r + 1) * HEADS],
                                            sq[:, r].rearrange("p (h d) -> p h d", d=DH),
                                            AX.X, ALU.add).then_inc(ss_ready, 1)
                dve.wait_ge(ss_ready, b * (2 * TT) + 2 * t + 2)
                nc.vector.tensor_scalar(sh[:, 1], sh[:, 0], 1.0 / DH, EPS, ALU.mult, ALU.add).then_inc(vv_ready, 1)

            def qk_norm(b, t):
                v_, y_, f_ = sh[:, 1], sh[:, 2], sh[:, 3]
                dve.wait_ge(gr_ready, b * (2 * TT) + 2 * t + 2)
                nc.vector.tensor_tensor(f_, y_, y_, ALU.mult).then_inc(nr_ready, 1)
                dve.wait_ge(nr_ready, b * (3 * TT) + 3 * t + 1)
                nc.vector.scalar_tensor_tensor(out=f_, in0=f_, scalar=-0.5, in1=v_, op0=ALU.mult,
                                               op1=ALU.mult).then_inc(nr_ready, 1)
                dve.wait_ge(nr_ready, b * (3 * TT) + 3 * t + 2)
                nc.vector.scalar_tensor_tensor(out=f_, in0=f_, scalar=1.5, in1=y_, op0=ALU.add,
                                               op1=ALU.mult).then_inc(nr_ready, 1)
                dve.wait_ge(nr_ready, b * (3 * TT) + 3 * t + 3)
                dve.wait_ge(raw_ready, b * (2 * TT) + 2 * t + 2)
                half = b % 2
                a = qk[:, half, t] if isinstance(half, int) else qk[:, bass.ds(half, 1), t].rearrange("p o n -> p (o n)")
                a = a.rearrange("p (h d) -> p h d", d=DH)
                nc.vector.tensor_tensor(
                    a, a, f_.rearrange("p (h o) -> p h o", o=1).broadcast_to([P, 2 * HEADS, DH]),
                    ALU.mult).then_inc(qk_ready, 1)
                dve.wait_ge(qk_ready, b * TT + t + 1)
                nc.vector.tensor_tensor(
                    a[:, 0:HEADS], a[:, 0:HEADS], grow[:].rearrange("p (o d) -> p o d", o=1).broadcast_to([P, HEADS, DH]),
                    ALU.mult).then_inc(qg_ready, 1)

            def part_low(b, n):
                dve.wait_ge(part_hi, b * (2 * HEADS) + 4 * (n + 1))
                for r, c in ((0, 1), (1, 2)):
                    nc.vector.tensor_tensor(part(n, r, c), heads_of(b, n, r), part(n, r, 0).bitcast(F32),
                                            ALU.subtract).then_inc(part_lo, 1)

            def maximum(b, g, i):
                dve.wait_ge(m_ready, b * (HEADS * TT) + HG * TT * g + i + 1)
                nc.vector.tensor_reduce(mx[:, g % 2, i:i + 1], ps[:, 2 + i % 2], AX.X,
                                        ALU.max).then_inc(max_ready, 1)

            def minus_max(b, g):
                dve.wait_ge(maxt_ready, b * NG + g + 1)
                wait(dve, nm_in, b * (NG * 32) + 32 * g)
                rows = ps[0:HG * TT, 3, 0:P]
                nc.vector.tensor_scalar(nm[:, 0], rows, -1.0, None, ALU.mult).then_inc(nmhi_ready, 1)
                dve.wait_ge(nmhi_ready, b * NG + g + 1)
                nc.vector.scalar_tensor_tensor(out=nm[:, 1], in0=rows, scalar=-1.0,
                                               in1=nm[:, 0].bitcast(F32), op0=ALU.mult,
                                               op1=ALU.subtract).then_inc(nm_ready, 1)

            def move_v(b):
                dve.wait_ge(v_ready, b * TT + TT)
                dve.wait_ge(pv_ready, b * (NG * TT) + 2)
                nc.vector.tensor_copy(v[:], v_next[:]).then_inc(v_moved, 1)

            def normalise(b, g):
                y_ = o_t[:, g % 2]
                dve.wait_ge(guess_ready, b * (2 * NG) + 2 * g + 2)
                nc.vector.tensor_tensor(o_n[:], ps[:, 7], y_, ALU.mult).then_inc(newton_ready, 1)
                dve.wait_ge(newton_ready, b * (2 * NG) + 2 * g + 1)
                nc.vector.scalar_tensor_tensor(out=o_n[:], in0=o_n[:], scalar=-2.0, in1=y_, op0=ALU.add,
                                               op1=ALU.mult).then_inc(newton_ready, 1)
                dve.wait_ge(newton_ready, b * (2 * NG) + 2 * g + 2)
                nc.vector.scalar_tensor_tensor(out=y_, in0=ps[:, 6], scalar=-1.0, in1=o_n[:], op0=ALU.mult,
                                               op1=ALU.mult).then_inc(norm_ready, 1)

            def weight_low(n):
                dve.wait_ge(w_hi, n + 1)
                nc.vector.tensor_tensor(wqkv[:, 1, n], w_raw[n % 2].rearrange("p k n -> p (k n)"),
                                        wqkv[:, 0, n].bitcast(F32), ALU.subtract).then_inc(w_lo, 1)

            def step(b, g, s, last):
                slots = () if last else SLOTS.get((g, s), ())
                maxima = list(range(M_FIRST[s], M_FIRST[s + 1])) if not last or g + 1 < NG else []
                if not last and (g, s) in QK_NORM:
                    qk_norm(b + 1, QK_NORM[g, s])
                if s == 3 and (not last or g + 1 < NG):
                    minus_max(b, g + 1)
                first = 2 if s >= 2 else len(maxima)
                for i in maxima[:first]:
                    maximum(b, g + 1, i)
                if slots and slots[0][0] == "q":
                    qk_sums(b + 1, slots[0][1])
                elif slots and slots[0][0] == "x":
                    for kind, t in slots:
                        tile_split(b + 1, t)
                for i in maxima[first:]:
                    maximum(b, g + 1, i)
                for n in pairs_ahead(g, s, last):
                    part_low(b, n)
                if not last and (g, s) == X_NORM:
                    x_norm(b + 1)
                if s == 0 and g >= 1:
                    normalise(b, g - 1)
                if s == 0 and g % NG == 0:
                    move_v(b + g // NG)

            x_norm(0)
            for n in range(KT - 1):
                weight_low(n)
            dve.wait_ge(const_in, 16 * 5)
            nc.vector.scalar_tensor_tensor(out=grow[:], in0=gqk[:, 0], scalar=float(DH) ** -0.5,
                                           in1=gqk[:, 1], op0=ALU.mult, op1=ALU.mult).then_inc(grow_ready, 1)
            dve.wait_ge(emb_mm, 1)
            sv = ps[:, 2, 0:2 * KT * B].rearrange("p (m b) -> p m b", b=B)
            bb = bemb[:].rearrange("p (m o) -> p m o", o=1).broadcast_to([P, 2 * KT, B])
            dve.wait_ge(grow_ready, 1)
            nc.vector.tensor_tensor(ab[:].rearrange("p a k b -> p (a k) b"), sv, bb, ALU.add).then_inc(ab_ready, 1)
            dve.wait_ge(ab_ready, 1)
            nc.vector.scalar_tensor_tensor(out=ab[:, 0], in0=ab[:, 0], scalar=1.0,
                                           in1=gn[:].rearrange("p (k o) -> p k o", o=1).broadcast_to([P, KT, B]),
                                           op0=ALU.add, op1=ALU.mult).then_inc(ab_ready, 1)
            dve.sem_inc(norm_ready, 1)
            weight_low(KT - 1)
            for t in range(TT):
                tile_split(0, t)
            for t in range(TT):
                qk_sums(0, t)
                qk_norm(0, t)
            for n in range(2):
                part_low(0, n)
            for g, s in AHEAD:
                step(0, g, s, False)

            def turn(b, last):
                for g, s in TURN:
                    if not last or g < NG:
                        step(b, g, s, last)
                if last:
                    normalise(b, NG - 1)

            with dve.Fori(0, B - 1) as b:
                turn(b, False)
            turn(B - 1, True)


E_N = 8
I_W = 352
IC = -(-I_W // P)
I_REST = I_W - (IC - 1) * P
TOP = 2
TOK_TILES = B * S // P
SLOT_TILES = (B * S * TOP + E_N * (P - 1)) // P
TILES = TOK_TILES + SLOT_TILES
SHARED = E_N
GU_COLS = KT * 2 * I_W
W_COLS = GU_COLS + IC * D
STAGE = 2
HOT = 8
MAX_AT, INDEX_AT, COUNT_AT, PLACE_AT, SLOT_AT, TABLE_AT = 0, 1, 2, 3, 4, 5
TABLE_TILES = TOP * TOK_TILES // HOT
FINISH_AT = TABLE_AT + TABLE_TILES
LOOP_FROM = FINISH_AT + 2
SLOT_LOOP = TOK_TILES + 2
assert (TOK_TILES - 1 - LOOP_FROM) % 2 == 0 and SLOT_LOOP % 2 == 0 and TILES % 2 == 1


def ffn_block(nc, o_parts, w_out, h_rows, gate_t, w_gu, w_down, out):
    with ExitStack() as ctx:
        def sb(name, shape, dt=F32):
            return ctx.enter_context(nc.sbuf_tensor(name, shape, dt))

        def sem(name):
            return ctx.enter_context(nc.semaphore(name))

        I32 = mybir.dt.int32
        U32 = mybir.dt.uint32
        ps = ctx.enter_context(nc.psum_tensor("ps2", [P, 8, 512], F32))

        wgu = sb("wgu", [P, E_N, KT, 2 * I_W])
        wdn = sb("wdn", [P, E_N, IC, D])
        parts = sb("parts2", [P, 2 * W_COLS], F32R)
        sh = parts[:].rearrange("p (a n) -> p a n", a=2)
        sh_gu = sh[:, :, 0:GU_COLS].rearrange("p a (k n) -> p a k n", k=KT)
        sh_dn = sh[:, :, GU_COLS:].rearrange("p a (c n) -> p a c n", c=IC)
        wo = parts[:, 0:2 * KT * D].rearrange("p (a k n) -> p a k n", a=2, k=KT)
        o_parts_sb = parts[:, 2 * KT * D:2 * KT * D + 4 * D].rearrange("p (i a k n) -> p i a k n", i=2, a=2, k=KT)
        gate = sb("gate", [P, KT, E_N])

        def in_weights(e):
            return wgu[:, e].rearrange("p k n -> p (k n)")[:, 0:KT * D].rearrange("p (k n) -> p k n", k=KT)

        wo_raw = in_weights(E_N - 1)
        o_raw = [in_weights(E_N - 2 - b) for b in range(B)]
        rows = sb("rows", [P, 2, D])
        rows_t = sb("rows_t", [P, 2, KT, P])
        rows_p = sb("rows_p", [P, 2, 2, KT, P], F32R)
        hid_p = sb("hid_p", [P, 2, IC, P], F32R)
        act_g = sb("act_g", [P, I_W])
        hid = sb("hid", [P, I_W])
        hid_t = sb("hid_t", [P, 2, IC, P])
        y = sb("y", [P, 2, D])
        idx_g = sb("idx_g", [P, 2], U32)
        idx_s = sb("idx_s", [P, 2], U32)
        tab_tok = sb("tab_tok", [P, TILES], I32)
        tab_w = sb("tab_w", [P, TILES])
        tab_e = sb("tab_e", [1, TILES], I32)

        ident = sb("ident2", [P, P])
        ones = sb("ones2", [P, P])
        before = sb("before", [P, P])
        lane = sb("lane", [P, P])
        own = sb("own", [P, 1])
        token = sb("token", [P, TOK_TILES])
        logits = sb("logits", [P, TOK_TILES, E_N])
        top = sb("top", [P, TOK_TILES, 8])
        top_i = sb("top_i", [P, TOK_TILES, 8], U32)
        pick = sb("pick", [P, TOP, TOK_TILES])
        hot = sb("hot", [P, TOP, TOK_TILES, E_N])
        both = sb("both", [P, TOK_TILES, E_N])
        wts = sb("wts", [P, TOP, TOK_TILES])
        ex = sb("ex", [P, 2, TOK_TILES])
        run = sb("run", [P, E_N, TOK_TILES])
        cnt_i = sb("cnt_i", [P, E_N], I32)
        cnt = sb("cnt", [P, E_N])
        ends = sb("ends", [P, E_N])
        base = sb("base", [P, E_N])
        slot = sb("slot", [P, TOP * TOK_TILES])
        slot_i = sb("slot_i", [P, 3, TOP * TOK_TILES], I32)
        slot_p = sb("slot_p", [P, TOP * TOK_TILES])
        slot_j = sb("slot_j", [P, TOP * TOK_TILES])
        last_w = wgu[:, E_N - 1].rearrange("p k n -> p (k n)")
        hot_p = last_w[:, 0:HOT * P].rearrange("p (i n) -> p i n", i=HOT)
        hot_j = last_w[:, HOT * P:HOT * (P + 2 * SLOT_TILES)].rearrange("p (i a j) -> p i a j", i=HOT, a=2)
        late = last_w[0:1, HOT * (P + 2 * SLOT_TILES):][:, 0:SLOT_TILES * E_N].rearrange("p (j e) -> p j e", e=E_N)
        sel = last_w[:, KT * 2 * I_W - TOP * TOK_TILES * E_N:].rearrange("p (c t e) -> p c t e", c=TOP, e=E_N)
        small = last_w[:, HOT * (P + 2 * SLOT_TILES) + SLOT_TILES * E_N:][:, 0:3 * TOK_TILES * E_N]
        tot, carry = (small[:, n * P:(n + 1) * P].rearrange("p (e t) -> p e t", e=E_N) for n in range(2))
        pos = small[:, 2 * P:3 * P].rearrange("p (t e) -> p t e", e=E_N)
        tile_e = sb("tile_e", [1, SLOT_TILES])
        empty = sb("empty", [P, SLOT_TILES])
        tok_f = sb("tok_f", [P, SLOT_TILES])

        names = ("gate_in shared_in experts_in pool_ready ident_ready wo_one wo_hi wo_lo "
                 "o_hi o_lo h_mm h_ready h_out0 h_out1 "
                 "logit_t logit_evac logit_mm r exp_done count_mm hot_done tab_mm "
                 "idx_ready rows_in0 rows_in1 rows_t_mm rows_t_out gate_mm up_mm silu_done hid_done "
                 "hid_t_mm hid_t_out down_mm y_ready y_out pool_settled").split()
        s = {n: sem(n + "_f") for n in names}
        wo_in = [sem(f"wo_in{k}") for k in range(KT)]
        o_in = [sem(f"o_in{n}") for n in range(TT + B - 1)]
        sh_hi = sem("sh_hi")
        sh_lo = sem("sh_lo")
        rows_lo = sem("rows_lo")
        hid_lo = sem("hid_lo")
        rows_in = (s["rows_in0"], s["rows_in1"])
        block = ctx.enter_context(nc.Block())
        C = 2

        def o_tile(t):
            return o_raw[t // TT][:, :, t % TT * P:(t % TT + 1) * P]

        def shared_pieces(part):
            pieces = [(wgu[:, STAGE, k], sh_gu[:, part, k]) for k in range(KT)]
            return pieces + [(wdn[:, STAGE], sh_dn[:, part])]

        def hid_rows(c):
            return P if c < IC - 1 else I_REST

        def at(n):
            return n + (C + 1)

        @block.sync
        def _(sp):
            sp.dma_start(gate[:], gate_t).then_inc(s["gate_in"], 16)
            for k in range(KT):
                sp.dma_start(wo_raw[:, k], w_out[:, k]).then_inc(wo_in[k], 16)
            for t in range(TT):
                sp.dma_start(o_tile(t), o_parts[0].rearrange("g p n -> p g n")[:, :, t * P:(t + 1) * P]
                             ).then_inc(o_in[t], 16)
            for b in range(1, B):
                sp.dma_start(o_raw[b], o_parts[b].rearrange("g p n -> p g n")).then_inc(o_in[TT - 1 + b], 16)

            def store_h(t):
                sp.wait_ge(s["h_ready"], t + 1)
                sp.dma_start(h_rows[t * P:(t + 1) * P], rows[:, t % 2]).then_inc(s[f"h_out{t % 2}"], 16)

            def load_piece(n):
                e = n // 2
                if e == E_N - 1:
                    sp.wait_ge(s["tab_mm"], TOP * TOK_TILES)
                sp.dma_start((wgu, wdn)[n % 2][:, e], (w_gu, w_down)[n % 2][e]).then_inc(s["experts_in"], 16)

            sp.dma_start(wgu[:, STAGE], w_gu[SHARED]).then_inc(s["shared_in"], 16)
            sp.dma_start(wdn[:, STAGE], w_down[SHARED]).then_inc(s["shared_in"], 16)
            early = 4
            assert early <= 2 * STAGE and STAGE < E_N - 1 - B
            for t in range(TOK_TILES):
                store_h(t)
                if t % 2 == 1 and t // 2 < early:
                    load_piece(t // 2)
            for n in range(early, 2 * E_N):
                sp.wait_ge(s["rows_t_mm"], n - early + 2)
                if n // 2 == STAGE:
                    sp.wait_ge(sh_lo, KT + 1)
                load_piece(n)

        @block.gpsimd
        def _(pool):
            nc.gpsimd.memset(ident[:], 0.0).then_inc(s["pool_ready"], 1)
            nc.gpsimd.memset(ones[:], 1.0).then_inc(s["pool_ready"], 1)
            pool.wait_ge(s["pool_ready"], 2)
            nc.gpsimd.affine_select(out=ident[:], in_=ident[:], compare_op=ALU.not_equal, fill=1.0, base=0,
                                    pattern=[[-1, P]], channel_multiplier=1).then_inc(s["ident_ready"], 1)
            nc.gpsimd.affine_select(out=before[:], in_=ones[:], compare_op=ALU.is_gt, fill=0.0, base=0,
                                    pattern=[[1, P]], channel_multiplier=-1).then_inc(s["pool_ready"], 1)
            nc.gpsimd.iota(lane[:], pattern=[[1, P]], base=0, channel_multiplier=0,
                           allow_small_or_imprecise_dtypes=True).then_inc(s["pool_ready"], 1)
            nc.gpsimd.iota(own[:], pattern=[[1, 1]], base=B * S + 1, channel_multiplier=1,
                           allow_small_or_imprecise_dtypes=True).then_inc(s["pool_ready"], 1)
            nc.gpsimd.iota(token[:], pattern=[[P, TOK_TILES]], base=1, channel_multiplier=1,
                           allow_small_or_imprecise_dtypes=True).then_inc(s["pool_ready"], 1)
            nc.gpsimd.iota(tab_tok[:, 0:TOK_TILES], pattern=[[P, TOK_TILES]], base=0,
                           channel_multiplier=1).then_inc(s["pool_ready"], 1)

            def gather(n, par):
                pool.wait_ge(s["idx_ready"], n + 1)
                pool.sem_inc(s["pool_settled"], 1)
                pool.indirect_dma_start(out=rows[:, par], out_offset=None, in_=h_rows,
                                        in_offset=bass.IndirectOffsetOnAxis(ap=idx_g[:, par:par + 1], axis=0),
                                        ).then_inc(rows_in[par], 16)

            def scatter(n, par):
                pool.wait_ge(s["y_ready"], at(n))
                if not isinstance(n, int) or n > 0:
                    pool.wait_ge(s["y_out"], 16 * n)
                pool.sem_inc(s["pool_settled"], 1)
                pool.indirect_dma_start(out=out, in_=y[:, par], in_offset=None,
                                        out_offset=bass.IndirectOffsetOnAxis(ap=idx_s[:, par:par + 1], axis=0),
                                        compute_op=ALU.add).then_inc(s["y_out"], 16)

            for i in range(2):
                pool.wait_ge(s[f"h_out{i}"], 16 * (TOK_TILES // 2))
            pool.wait_ge(s["logit_t"], TOK_TILES)
            gather(0, 0)
            gather(1, 1)
            gather(2, 0)
            for m in (1, 2, 3):
                gather(m + 2, m % 2)
                scatter(m - 1, 1 - m % 2)
            with pool.Fori(0, (TILES - 7) // 2) as i:
                for u in range(2):
                    m = i * 2 + (4 + u)
                    gather(m + 2, u)
                    scatter(m - 1, 1 - u)
            gather(TILES - 1, (TILES - 1) % 2)
            for n in range(TILES - 4, TILES):
                scatter(n, n % 2)
            pool.wait_ge(s["y_out"], 16 * TILES)

        @block.scalar
        def _(act):
            for k in range(KT):
                act.wait_ge(s["wo_one"], k + 1)
                nc.scalar.copy(wo[:, 0, k], wo_raw[:, k]).then_inc(s["wo_hi"], 1)
            for t in range(TOK_TILES + 2):
                if t < TOK_TILES:
                    act.wait_ge(o_in[t if t < TT else TT - 1 + t // TT], 16)
                    if t >= 2:
                        act.wait_ge(s["h_mm"], t - 1)
                    nc.scalar.copy(o_parts_sb[:, t % 2, 0], o_tile(t)).then_inc(s["o_hi"], 1)
                if t >= 2:
                    act.wait_ge(s["logit_t"], t - 1)
                    if t >= 4:
                        act.wait_ge(s["logit_mm"], t - 3)
                    nc.scalar.copy(rows_t[:, t % 2].rearrange("p k n -> p (k n)"), ps[:, t % 2]).then_inc(s["logit_evac"], 1)
            act.wait_ge(s["shared_in"], 32)
            act.wait_ge(s["h_mm"], TOK_TILES)
            for raw, high in shared_pieces(0):
                nc.scalar.copy(high, raw).then_inc(sh_hi, 1)
            for c in ("rows_t_out", "silu_done", "hid_t_out"):
                act.sem_inc(s[c], C)

            def rows_out(n, par):
                act.wait_ge(s["rows_t_mm"], n + 1)
                act.wait_ge(s["up_mm"], at(n - 2))
                nc.scalar.copy(rows_t[:, par].rearrange("p k n -> p (k n)"), ps[:, 0]).then_inc(s["rows_t_out"], 1)

            def rows_high(n, par):
                act.wait_ge(s["rows_t_mm"], n + 1)
                act.wait_ge(s["up_mm"], at(n - 2))
                nc.scalar.copy(rows_p[:, par, 0].rearrange("p k n -> p (k n)"), ps[:, 0]).then_inc(s["rows_t_out"], 1)

            def silu(n, par):
                act.wait_ge(s["gate_mm"], n + 1)
                act.wait_ge(s["hid_done"], at(n - 1))
                nc.scalar.activation(act_g[:], ps[:, 2 + 2 * par, 0:I_W], ACT.Silu).then_inc(s["silu_done"], 1)

            def hid_out(n, par):
                act.wait_ge(s["hid_t_mm"], at(n))
                act.wait_ge(s["down_mm"], at(n - 2))
                nc.scalar.copy(hid_t[:, par, 0:IC - 1].rearrange("p k n -> p (k n)"),
                               ps[:, 1, 0:(IC - 1) * P])
                nc.scalar.copy(hid_t[0:I_REST, par, IC - 1], ps[0:I_REST, 1, (IC - 1) * P:IC * P]
                               ).then_inc(s["hid_t_out"], 1)

            def hid_high(n):
                act.wait_ge(s["hid_t_mm"], at(n))
                act.wait_ge(s["down_mm"], at(n - 1))
                nc.scalar.copy(hid_p[:, 0, 0:IC - 1].rearrange("p k n -> p (k n)"),
                               ps[:, 1, 0:(IC - 1) * P])
                nc.scalar.copy(hid_p[0:I_REST, 0, IC - 1], ps[0:I_REST, 1, (IC - 1) * P:IC * P]
                               ).then_inc(s["hid_t_out"], 1)

            rows_high(0, 0)
            silu(0, 0)
            rows_high(1, 1)
            for n in range(1, LOOP_FROM):
                if n == 2:
                    act.wait_ge(s["r"], R_DIFF)
                    nc.scalar.activation(ex[:, 0], ex[:, 1], ACT.Exp).then_inc(s["exp_done"], 1)
                silu(n, n % 2)
                hid_high(n - 1)
                rows_high(n + 1, 1 - n % 2)
            with act.Fori(0, (TOK_TILES - 1 - LOOP_FROM) // 2) as i:
                for u in range(2):
                    n = i * 2 + (LOOP_FROM + u)
                    silu(n, (LOOP_FROM + u) % 2)
                    hid_high(n - 1)
                    rows_high(n + 1, (LOOP_FROM + u + 1) % 2)
            act.wait_ge(s["logit_mm"], TOK_TILES)
            for n in (TOK_TILES - 1, TOK_TILES):
                silu(n, n % 2)
                hid_high(n - 1)
                rows_out(n + 1, 1 - n % 2)
            n = TOK_TILES + 1
            silu(n, n % 2)
            hid_out(n - 1, 1 - n % 2)
            rows_out(n + 1, 1 - n % 2)
            with act.Fori(0, (TILES - 1 - SLOT_LOOP) // 2) as i:
                for u in range(2):
                    n = i * 2 + (SLOT_LOOP + u)
                    silu(n, u)
                    hid_out(n - 1, 1 - u)
                    rows_out(n + 1, 1 - u)
            silu(TILES - 1, 0)
            hid_out(TILES - 2, 1)
            hid_out(TILES - 1, 0)

        @block.tensor
        def _(pe):
            pe.wait_ge(s["ident_ready"], 1)
            pe.wait_ge(s["gate_in"], 16)

            def logit(t):
                pe.wait_ge(s["logit_evac"], t + 1)
                for k in range(KT):
                    ins = pe.matmul(ps[:, 7, t * E_N:(t + 1) * E_N], rows_t[:, t % 2, k], gate[:, k],
                                    start=(k == 0), stop=(k == KT - 1))
                ins.then_inc(s["logit_mm"], 1)

            for t in range(TOK_TILES + 2):
                if t < TOK_TILES:
                    pe.wait_ge(s["o_lo"], t + 1)
                    if t >= 2:
                        pe.wait_ge(s["h_ready"], t - 1)
                    n = 0
                    for k in range(KT):
                        pe.wait_ge(s["wo_lo"], k + 1)
                        for o_part, w_part in ((0, 0), (0, 1), (1, 0)):
                            ins = pe.matmul(ps[:, 2 + t % 2], o_parts_sb[:, t % 2, o_part, k], wo[:, w_part, k],
                                            start=(n == 0), stop=(n == 3 * KT - 1))
                            n += 1
                    ins.then_inc(s["h_mm"], 1)
                if 1 <= t <= TOK_TILES:
                    u = t - 1
                    pe.wait_ge(s["h_ready"], u + 1)
                    if u >= 2:
                        pe.wait_ge(s["logit_evac"], u - 1)
                    for k in range(KT):
                        ins = pe.transpose(ps[:, u % 2, k * P:(k + 1) * P], rows[:, u % 2, k * P:(k + 1) * P], ident[:])
                    ins.then_inc(s["logit_t"], 1)
                if t >= 2:
                    logit(t - 2)

            def counts():
                pe.wait_ge(s["pool_ready"], 7)
                pe.wait_ge(s["r"], R_HOT)
                flat = both[:].rearrange("p t e -> p (t e)")
                pe.matmul(ps[:, 7, P:2 * P], before[:], flat, start=True, stop=True)
                pe.matmul(ps[:, 7, 2 * P:3 * P], ones[:], flat, start=True, stop=True).then_inc(s["count_mm"], 1)

            def table(group):
                pe.wait_ge(s["hot_done"], 4 * (group + 1))
                for n in range(group * HOT, (group + 1) * HOT):
                    pe.matmul(ps[:, 7, 3 * P:3 * P + 2 * SLOT_TILES], hot_p[:, n % HOT],
                              hot_j[:, n % HOT].rearrange("p a j -> p (a j)"),
                              start=(n == 0), stop=(n == TOP * TOK_TILES - 1)).then_inc(s["tab_mm"], 1)

            for c in ("up_mm", "hid_t_mm", "down_mm"):
                pe.sem_inc(s[c], C)

            def rows_turn(n, par, shared=True):
                pe.wait_ge(rows_in[par], (n // 2 + 1) * 16 if isinstance(n, int) else n[1])
                n = n if isinstance(n, int) else n[0]
                if not shared:
                    pe.wait_ge(s["rows_t_out"], at(n - 1))
                elif not isinstance(n, int) or n > 0:
                    pe.wait_ge(rows_lo, n)
                for k in range(KT):
                    ins = pe.transpose(ps[:, 0, k * P:(k + 1) * P], rows[:, par, k * P:(k + 1) * P], ident[:])
                ins.then_inc(s["rows_t_mm"], 1)

            def gate_up(n, par, e, up):
                if up:
                    pe.wait_ge(s["hid_done"], at(n - 2))
                else:
                    pe.wait_ge(s["rows_t_out"], at(n))
                    pe.wait_ge(s["silu_done"], at(n - 2))
                for k in range(KT):
                    w = wgu[:, bass.ds(e, 1), k, up * I_W:(up + 1) * I_W].rearrange("p o n -> p (o n)")
                    ins = pe.matmul(ps[:, 2 + 2 * par + up, 0:I_W], rows_t[:, par, k], w,
                                    start=(k == 0), stop=(k == KT - 1))
                ins.then_inc(s["up_mm" if up else "gate_mm"], 1)

            def gate_up_shared(n, par, up):
                if up:
                    pe.wait_ge(s["hid_done"], at(n - 2))
                else:
                    pe.wait_ge(rows_lo, n + 1)
                    pe.wait_ge(sh_lo, KT)
                    pe.wait_ge(s["silu_done"], at(n - 2))
                i = 0
                for k in range(KT):
                    for r_part, w_part in ((0, 0), (0, 1), (1, 0)):
                        ins = pe.matmul(ps[:, 2 + 2 * par + up, 0:I_W], rows_p[:, par, r_part, k],
                                        sh_gu[:, w_part, k, up * I_W:(up + 1) * I_W],
                                        start=(i == 0), stop=(i == 3 * KT - 1))
                        i += 1
                ins.then_inc(s["up_mm" if up else "gate_mm"], 1)

            def down_shared(n):
                pe.wait_ge(hid_lo, n + 1)
                pe.wait_ge(sh_lo, KT + 1)
                pe.wait_ge(s["y_ready"], at(n - 1))
                i = 0
                for c in range(IC):
                    w = hid_rows(c)
                    for h_part, w_part in ((0, 0), (0, 1), (1, 0)):
                        ins = pe.matmul(ps[:, 6], hid_p[0:w, h_part, c], sh_dn[0:w, w_part, c],
                                        start=(i == 0), stop=(i == 3 * IC - 1))
                        i += 1
                ins.then_inc(s["down_mm"], 1)

            def hid_turn(n, shared=True):
                pe.wait_ge(s["hid_done"], at(n))
                if not shared:
                    pe.wait_ge(s["hid_t_out"], at(n - 1))
                elif not isinstance(n, int) or n > 0:
                    pe.wait_ge(hid_lo, n)
                for c in range(IC):
                    w = P if c < IC - 1 else I_REST
                    ins = pe.transpose(ps[0:w, 1, c * P:(c + 1) * P], hid[:, c * P:c * P + w], ident[:])
                ins.then_inc(s["hid_t_mm"], 1)

            def down(n, par, e):
                pe.wait_ge(s["hid_t_out"], at(n))
                pe.wait_ge(s["y_ready"], at(n - 1))
                for c in range(IC):
                    w = P if c < IC - 1 else I_REST
                    wd = wdn[0:w, bass.ds(e, 1), c].rearrange("p o n -> p (o n)")
                    ins = pe.matmul(ps[:, 6], hid_t[0:w, par, c], wd, start=(c == 0), stop=(c == IC - 1))
                ins.then_inc(s["down_mm"], 1)

            def expert(n):
                return pe.value_load(tab_e[0:1, bass.ds(n, 1)], min_val=0, max_val=E_N - 1)

            rows_turn(0, 0)
            gate_up_shared(0, 0, 0)
            rows_turn(1, 1)
            gate_up_shared(0, 0, 1)

            def body_shared(n, par, rows_count=None):
                gate_up_shared(n, par, 0)
                hid_turn(n - 1)
                rows_turn(n + 1 if rows_count is None else (n + 1, rows_count), 1 - par)
                gate_up_shared(n, par, 1)
                down_shared(n - 1)

            for n in range(1, LOOP_FROM):
                body_shared(n, n % 2)
                if TABLE_AT < n <= FINISH_AT:
                    table(n - 1 - TABLE_AT)
                if n == COUNT_AT + 1:
                    counts()
            with pe.Fori(0, (TOK_TILES - 1 - LOOP_FROM) // 2) as i:
                for u in range(2):
                    first = LOOP_FROM + u
                    body_shared(i * 2 + first, first % 2, i * 16 + 16 * ((first + 1) // 2 + 1))
            n = TOK_TILES - 1
            body_shared(n, n % 2)
            pe.wait_ge(s["experts_in"], 32 * E_N)
            n = TOK_TILES
            e = expert(n)
            gate_up(n, 0, e, 0)
            hid_turn(n - 1)
            rows_turn(n + 1, 1, False)
            gate_up(n, 0, e, 1)
            down_shared(n - 1)

            def body(n, par, e, e_last, rows_count=None, shared_before=False):
                gate_up(n, par, e, 0)
                hid_turn(n - 1, shared_before)
                rows_turn(n + 1 if rows_count is None else (n + 1, rows_count), 1 - par, False)
                gate_up(n, par, e, 1)
                down(n - 1, 1 - par, e_last)

            n = TOK_TILES + 1
            body(n, n % 2, expert(n), expert(n - 1), shared_before=True)
            with pe.Fori(0, (TILES - 1 - SLOT_LOOP) // 2) as i:
                for u in range(2):
                    n = i * 2 + (SLOT_LOOP + u)
                    body(n, u, expert(n), expert(n - 1), i * 16 + 16 * ((SLOT_LOOP + u + 1) // 2 + 1))
            n = TILES - 1
            e = expert(n)
            e_last = expert(n - 1)
            gate_up(n, 0, e, 0)
            hid_turn(n - 1, False)
            gate_up(n, 0, e, 1)
            down(n - 1, 1, e_last)
            hid_turn(n, False)
            down(n, 0, e)

        @block.vector
        def _(dve):
            done = [0]

            def step(ins):
                done[0] += 1
                ins.then_inc(s["r"], 1)
                dve.wait_ge(s["r"], done[0])

            V = nc.vector
            for k in range(KT):
                dve.wait_ge(wo_in[k], 16)
                if k == 0:
                    dve.wait_ge(s["ident_ready"], 1)
                V.tensor_tensor(wo_raw[:, k, k * P:(k + 1) * P], wo_raw[:, k, k * P:(k + 1) * P], ident[:],
                                ALU.add).then_inc(s["wo_one"], 1)
            for k in range(KT):
                dve.wait_ge(s["wo_hi"], k + 1)
                V.tensor_tensor(wo[:, 1, k], wo_raw[:, k], wo[:, 0, k].bitcast(F32), ALU.subtract).then_inc(s["wo_lo"], 1)
            for t in range(TOK_TILES + 1):
                if t < TOK_TILES:
                    dve.wait_ge(s["o_hi"], t + 1)
                    V.tensor_tensor(o_parts_sb[:, t % 2, 1], o_tile(t), o_parts_sb[:, t % 2, 0].bitcast(F32),
                                    ALU.subtract).then_inc(s["o_lo"], 1)
                if t >= 1:
                    u = t - 1
                    dve.wait_ge(s["h_mm"], u + 1)
                    if u >= 2:
                        dve.wait_ge(s[f"h_out{u % 2}"], 16 * (u // 2))
                        dve.wait_ge(s["logit_t"], u - 1)
                    V.tensor_copy(rows[:, u % 2], ps[:, 2 + u % 2]).then_inc(s["h_ready"], 1)

            def index(n, par):
                V.tensor_copy(idx_g[:, par:par + 1], tab_tok[:, bass.ds(n, 1)]).then_inc(s["idx_ready"], 1)

            dve.wait_ge(s["pool_ready"], 7)
            index(0, 0)
            index(1, 1)
            for n, ((raw, high), (_, low)) in enumerate(zip(shared_pieces(0), shared_pieces(1))):
                dve.wait_ge(sh_hi, n + 1)
                V.tensor_tensor(low, raw, high.bitcast(F32), ALU.subtract).then_inc(sh_lo, 1)

            step(V.memset(tab_w[:], 1.0))
            step(V.memset(run[:], 1.0))
            step(V.memset(run[:, :, 0:1], 0.0))

            def pick_maxima():
                dve.wait_ge(s["logit_mm"], TOK_TILES)
                step(V.tensor_copy(logits[:].rearrange("p t e -> p (t e)"), ps[:, 7, 0:TOK_TILES * E_N]))
                for t in range(TOK_TILES):
                    ins = V.max(top[:, t], logits[:, t])
                step(ins)

            def pick_indices():
                for t in range(TOK_TILES):
                    ins = V.max_index(top_i[:, t], top[:, t], logits[:, t])
                step(ins)
                step(V.tensor_tensor(ex[:, 1], top[:, :, 1], top[:, :, 0], ALU.subtract))
                assert done[0] == R_DIFF

            def hot_experts():
                for c in range(TOP):
                    step(V.tensor_copy(pick[:, c], top_i[:, :, c]))
                    step(V.tensor_tensor(
                        hot[:, c],
                        pick[:, c].rearrange("p (t o) -> p t o", o=1).broadcast_to([P, TOK_TILES, E_N]),
                        lane[:, 0:E_N].rearrange("p (o e) -> p o e", o=1).broadcast_to([P, TOK_TILES, E_N]),
                        ALU.is_equal))
                step(V.tensor_tensor(both[:], hot[:, 0], hot[:, 1], ALU.add))
                assert done[0] == R_HOT

            def places():
                dve.wait_ge(s["exp_done"], 1)
                step(V.tensor_scalar(ex[:, 1], ex[:, 0], 1.0, None, ALU.add))
                step(V.reciprocal(wts[:, 0], ex[:, 1]))
                step(V.tensor_tensor(wts[:, 1], ex[:, 0], wts[:, 0], ALU.mult))

                dve.wait_ge(s["count_mm"], 1)
                step(V.tensor_copy(tot, ps[:, 7, 2 * P:3 * P].rearrange("p (t e) -> p e t", e=E_N)))
                step(V.tensor_tensor_scan(carry.rearrange("p e t -> p (e t)"), run[:].rearrange("p e t -> p (e t)"),
                                          tot.rearrange("p e t -> p (e t)"), 0.0, ALU.mult, ALU.add))
                step(V.tensor_scalar(cnt_i[:], carry[:, :, TOK_TILES - 1], float(P - 1), None, ALU.add))
                step(V.tensor_scalar(cnt_i[:], cnt_i[:], 7, None, ALU.arith_shift_right))
                step(V.tensor_copy(cnt[:], cnt_i[:]))
                step(V.tensor_tensor_scan(ends[:], ones[:, 0:E_N], cnt[:], 0.0, ALU.mult, ALU.add))
                step(V.tensor_tensor(base[:], ends[:], cnt[:], ALU.subtract))
                step(V.tensor_tensor(carry, carry, tot, ALU.subtract))
                step(V.scalar_tensor_tensor(
                    out=pos, in0=base[:].rearrange("p (o e) -> p o e", o=1).broadcast_to([P, TOK_TILES, E_N]),
                    scalar=float(P), in1=carry.rearrange("p e t -> p t e"), op0=ALU.mult, op1=ALU.add))
                step(V.tensor_tensor(pos.rearrange("p t e -> p (t e)"), pos.rearrange("p t e -> p (t e)"),
                                     ps[:, 7, P:2 * P], ALU.add))

            def slots_of_tokens():
                for c in range(TOP):
                    step(V.tensor_tensor(sel[:, c], hot[:, c], pos, ALU.mult))
                step(V.tensor_reduce(slot[:], sel.rearrange("p c t e -> p (c t) e"), AX.X, ALU.add))
                step(V.tensor_copy(slot_i[:, 0], slot[:]))
                step(V.tensor_scalar(slot_i[:, 1], slot_i[:, 0], P - 1, None, ALU.bitwise_and))
                step(V.tensor_scalar(slot_i[:, 2], slot_i[:, 0], 7, None, ALU.arith_shift_right))
                step(V.tensor_copy(slot_p[:], slot_i[:, 1]))
                step(V.tensor_copy(slot_j[:], slot_i[:, 2]))
                step(V.tensor_tensor(
                    late, lane[0:1, 0:SLOT_TILES].rearrange("p (j o) -> p j o", o=1).broadcast_to([1, SLOT_TILES, E_N]),
                    ends[0:1].rearrange("p (o e) -> p o e", o=1).broadcast_to([1, SLOT_TILES, E_N]), ALU.is_ge))
                step(V.tensor_reduce(tile_e[:], late, AX.X, ALU.add))
                step(V.tensor_scalar(tab_e[:, TOK_TILES:], tile_e[:], float(E_N - 1), None, ALU.min))

            def hot_rows(group):
                if group:
                    dve.wait_ge(s["tab_mm"], group * HOT)
                cols = slice(group * HOT, (group + 1) * HOT)
                c, t = divmod(group * HOT, TOK_TILES)

                def spread(a, n):
                    return a.rearrange("p (i o) -> p i o", o=1).broadcast_to([P, HOT, n])

                def lanes(n):
                    return lane[:, 0:n].rearrange("p (o n) -> p o n", o=1).broadcast_to([P, HOT, n])

                V.tensor_tensor(hot_p, lanes(P), spread(slot_p[:, cols], P), ALU.is_equal).then_inc(s["hot_done"], 1)
                V.tensor_tensor(hot_j[:, :, 0], lanes(SLOT_TILES), spread(slot_j[:, cols], SLOT_TILES),
                                ALU.is_equal).then_inc(s["hot_done"], 1)
                dve.wait_ge(s["hot_done"], 4 * group + 2)
                V.tensor_tensor(hot_j[:, :, 1], hot_j[:, :, 0], spread(wts[:, c, t:t + HOT], SLOT_TILES),
                                ALU.mult).then_inc(s["hot_done"], 1)
                V.tensor_tensor(hot_j[:, :, 0], hot_j[:, :, 0], spread(token[:, t:t + HOT], SLOT_TILES),
                                ALU.mult).then_inc(s["hot_done"], 1)

            def tables():
                dve.wait_ge(s["tab_mm"], TOP * TOK_TILES)
                step(V.tensor_copy(tok_f[:], ps[:, 7, 3 * P:3 * P + SLOT_TILES]))
                step(V.tensor_copy(tab_w[:, TOK_TILES:], ps[:, 7, 3 * P + SLOT_TILES:3 * P + 2 * SLOT_TILES]))
                step(V.tensor_scalar(empty[:], tok_f[:], 0.0, None, ALU.is_equal))
                step(V.scalar_tensor_tensor(out=tok_f[:], in0=empty[:], scalar=own[:], in1=tok_f[:],
                                            op0=ALU.mult, op1=ALU.add))
                step(V.tensor_scalar(tab_tok[:, TOK_TILES:], tok_f[:], -1.0, None, ALU.add))

            for c in ("hid_done", "y_ready"):
                dve.sem_inc(s[c], C)

            def multiply(n, par):
                dve.wait_ge(s["up_mm"], at(n))
                dve.wait_ge(s["silu_done"], at(n))
                dve.wait_ge(s["hid_t_mm"], at(n - 1))
                V.tensor_tensor(hid[:], act_g[:], ps[:, 3 + 2 * par, 0:I_W], ALU.mult).then_inc(s["hid_done"], 1)

            def rows_low(n, par):
                dve.wait_ge(s["rows_t_out"], at(n))
                V.tensor_tensor(rows_p[:, par, 1].rearrange("p k n -> p (k n)"), ps[:, 0],
                                rows_p[:, par, 0].rearrange("p k n -> p (k n)").bitcast(F32),
                                ALU.subtract).then_inc(rows_lo, 1)

            def hid_low(n):
                dve.wait_ge(s["hid_t_out"], at(n))
                V.tensor_tensor(hid_p[:, 1, 0:IC - 1].rearrange("p k n -> p (k n)"), ps[:, 1, 0:(IC - 1) * P],
                                hid_p[:, 0, 0:IC - 1].rearrange("p k n -> p (k n)").bitcast(F32), ALU.subtract)
                V.tensor_tensor(hid_p[0:I_REST, 1, IC - 1], ps[0:I_REST, 1, (IC - 1) * P:IC * P],
                                hid_p[0:I_REST, 0, IC - 1].bitcast(F32), ALU.subtract).then_inc(hid_lo, 1)

            def weigh(n, par):
                dve.wait_ge(s["down_mm"], at(n))
                if not isinstance(n, int) or n > 1:
                    dve.wait_ge(s["y_out"], 16 * (n - 1))
                V.tensor_copy(idx_s[:, par:par + 1], tab_tok[:, bass.ds(n, 1)])
                V.tensor_scalar(y[:, par], ps[:, 6], tab_w[:, bass.ds(n, 1)], None, ALU.mult).then_inc(s["y_ready"], 1)

            stages = {MAX_AT: pick_maxima, INDEX_AT: pick_indices, COUNT_AT: hot_experts, PLACE_AT: places,
                      SLOT_AT: slots_of_tokens, FINISH_AT: tables}
            rows_low(0, 0)
            for n in range(LOOP_FROM):
                if n >= 1:
                    hid_low(n - 1)
                rows_low(n + 1, 1 - n % 2)
                multiply(n, n % 2)
                index(n + 2, n % 2)
                if n >= 1:
                    weigh(n - 1, 1 - n % 2)
                if n in stages:
                    stages[n]()
                elif TABLE_AT <= n < FINISH_AT:
                    hot_rows(n - TABLE_AT)
            with dve.Fori(0, (TOK_TILES - 1 - LOOP_FROM) // 2) as i:
                for u in range(2):
                    n = i * 2 + (LOOP_FROM + u)
                    par = (LOOP_FROM + u) % 2
                    hid_low(n - 1)
                    rows_low(n + 1, 1 - par)
                    multiply(n, par)
                    index(n + 2, par)
                    weigh(n - 1, 1 - par)
            for n in (TOK_TILES - 1, TOK_TILES):
                hid_low(n - 1)
                multiply(n, n % 2)
                index(n + 2, n % 2)
                weigh(n - 1, 1 - n % 2)
            n = TOK_TILES + 1
            multiply(n, n % 2)
            index(n + 2, n % 2)
            weigh(n - 1, 1 - n % 2)
            with dve.Fori(0, (TILES - 3 - SLOT_LOOP) // 2) as i:
                for u in range(2):
                    n = i * 2 + (SLOT_LOOP + u)
                    multiply(n, u)
                    index(n + 2, u)
                    weigh(n - 1, 1 - u)
            multiply(TILES - 3, 0)
            index(TILES - 1, 0)
            weigh(TILES - 4, 1)
            multiply(TILES - 2, 1)
            weigh(TILES - 3, 0)
            multiply(TILES - 1, 0)
            weigh(TILES - 2, 1)
            weigh(TILES - 1, 0)


R_DIFF = 7
R_HOT = 12


def kernel(**inputs):
    import numpy as np
    import concourse.bacc as bacc
    from concourse.bass_utils import run_bass_kernel_spmd as run

    nc = bacc.Bacc("TRN2", target_bir_lowering=False, num_devices=1)
    i = {k: np.asarray(a) for k, a in inputs.items()}

    def tiles(a):
        return np.ascontiguousarray(a.reshape(-1, P, a.shape[-1]).transpose(1, 0, 2))

    def all_experts(name):
        return np.concatenate([i[f"L0_ffn_expert_{name}_w"], i[f"L0_ffn_shared_{name}_w"][None]])

    gu = np.concatenate([all_experts("gate"), all_experts("up")], axis=1)
    gu = gu.reshape(E_N + 1, 2 * I_W, KT, P).transpose(0, 3, 2, 1)
    dn = np.pad(all_experts("down"), ((0, 0), (0, 0), (0, IC * P - I_W)))
    dn = dn.reshape(E_N + 1, D, IC, P).transpose(0, 3, 2, 1)
    arrays = {
        "x": np.ascontiguousarray(i["x"].reshape(B * S, D)),
        "cond_t": tiles(np.ascontiguousarray(i["cond_2048"].T)),
        "w_emb": tiles(i["L0_cond_W_emb"]),
        "b_emb": np.ascontiguousarray(i["L0_cond_b_emb"].reshape(2 * KT, P).T),
        "g_norm": np.ascontiguousarray(i["L0_cond_g_norm"].reshape(KT, P).T),
        "w_qkv": np.ascontiguousarray(tiles(i["L0_cond_W_qkv"]).reshape(P, KT, 3, D)),
        "g_q": i["L0_cond_g_q"].reshape(1, DH),
        "g_k": i["L0_cond_g_k"].reshape(1, DH),
        "w_out": tiles(i["L0_cond_W_out"]),
        "gate_t": tiles(np.ascontiguousarray(i["L0_ffn_gate_weight"].T)),
        "w_gu": np.ascontiguousarray(gu),
        "w_down": np.ascontiguousarray(dn),
    }
    ap = {k: nc.dram_tensor(k, a.shape, F32, kind="ExternalInput").ap() for k, a in arrays.items()}
    h_rows = nc.dram_tensor("h_rows", (B * S + P, D), F32, kind="Internal").ap()
    out = nc.dram_tensor("out", (B * S + P, D), F32, kind="ExternalOutput").ap()
    o_parts = nc.dram_tensor("o_parts", (B, NG, P, S), F32, kind="Internal").ap()
    attention_block(nc, *(ap[k] for k in ("x", "cond_t", "w_emb", "b_emb", "g_norm", "w_qkv", "g_q", "g_k")),
                    h_rows, o_parts, out)
    ffn_block(nc, o_parts, ap["w_out"], h_rows, ap["gate_t"], ap["w_gu"], ap["w_down"], out)
    got = run(nc, [arrays], core_ids=[0]).results[0]["out"]
    return np.ascontiguousarray(got[0:B * S]).reshape(B, S, D)
```
